# Optimizing a Trainium2 kernel written in Bass

```python
import numpy as np
import jax
import jax.numpy as jnp

def _softmax(x, axis=-1):
    return jax.nn.softmax(x, axis=axis)

def _gelu(x):
    return jax.nn.gelu(x, approximate=True)

def _silu(x):
    return jax.nn.silu(x)

def _sigmoid(x):
    return jax.nn.sigmoid(x)

def _layernorm(x, axis=-1, eps=1e-05):
    m = jnp.mean(x, axis=axis, keepdims=True)
    v = jnp.var(x, axis=axis, keepdims=True)
    return (x - m) / jnp.sqrt(v + eps)

def _scatter_add(tgt, idx, src, axis=0):
    return tgt.at[idx].add(src)

def _segment_sum(src, seg, n):
    return jax.ops.segment_sum(src, seg, n)
kernel_name = 'mk_decoder_preln_d1_seqx_r4_64a831'

def setup_inputs(seed: int=0):
    np.random.seed(seed)
    _w = jnp.asarray

    def _rec_inputs():
        import jax
        import jax.numpy as jnp
        _rk = jax.random.key(seed)
        x = -0.0002928 + 1 * jax.random.normal(jax.random.fold_in(_rk, 1), (32, 256, 256), jnp.float32)
        _lenS = 256 - jax.random.randint(jax.random.fold_in(_rk, 7), (32,), 0, max(1, 256 // 4) + 1, jnp.int32)
        _lenS2 = 256 - jax.random.randint(jax.random.fold_in(_rk, 8), (32,), 0, max(1, 256 // 4) + 1, jnp.int32)
        _ctx_1024P = jax.random.normal(jax.random.fold_in(_rk, 11), (32, 16, 256), jnp.float32)
        _ctx_1024c = jax.random.dirichlet(jax.random.fold_in(_rk, 511), 0.3 * jnp.ones((16,), jnp.float32), (32, 256))
        _ctx_1024t = jnp.einsum('bsk,bkd->bsd', _ctx_1024c, _ctx_1024P)
        _ctx_1024t = _ctx_1024t * jax.lax.rsqrt(jnp.mean(jnp.square(_ctx_1024t)) + 1e-12) * 0.953939
        ctx_1024 = -1.39393e-06 + 0.999914 * (_ctx_1024t + 0.3 * jax.random.normal(jax.random.fold_in(_rk, 611), (32, 256, 256), jnp.float32))
        return (x, ctx_1024)
    x, ctx_1024 = _rec_inputs()

    def _L0_attn_setup():
        import jax, jax.numpy as jnp
        import numpy as np
        EPS = 1e-08

        def unit_projection(x):
            f = jnp.fft.fft(x)
            f = f / (jnp.abs(f) + EPS)
            return jnp.fft.ifft(f).real

        def bind(a, b):
            return jnp.fft.ifft(jnp.fft.fft(a) * jnp.fft.fft(b)).real

        def unbind(s, a):
            return jnp.fft.ifft(jnp.fft.fft(s) * jnp.conj(jnp.fft.fft(a))).real
        key = jax.random.key(seed)
        B, S, D = (4, 1024, 256)
        ks = jax.random.split(key, 7)
        scale = 1.0 / np.sqrt(D)
        x = jax.random.normal(ks[0], (B, S, D), dtype=jnp.float32)
        Wq = jax.random.uniform(ks[1], (D, D), jnp.float32, -scale, scale)
        bq = jax.random.uniform(ks[2], (D,), jnp.float32, -scale, scale)
        Wk = jax.random.uniform(ks[3], (D, D), jnp.float32, -scale, scale)
        bk = jax.random.uniform(ks[4], (D,), jnp.float32, -scale, scale)
        Wv = jax.random.uniform(ks[5], (D, D), jnp.float32, -scale, scale)
        bv = jax.random.uniform(ks[6], (D,), jnp.float32, -scale, scale)
        return {'x': x, 'Wq': Wq, 'bq': bq, 'Wk': Wk, 'bk': bk, 'Wv': Wv, 'bv': bv}
    _L0_attn_all = _L0_attn_setup()
    _L0_attn_in = {k: v for k, v in _L0_attn_all.items() if k in ('Wq', 'bq', 'Wk', 'bk', 'Wv', 'bv')}
    del _L0_attn_all

    def _L0_xattn_setup():
        import jax, jax.numpy as jnp
        import numpy as np
        import math
        EPS = 1e-05

        def _layernorm(x, gamma, beta):
            mu = jnp.mean(x, axis=-1, keepdims=True)
            var = jnp.mean(jnp.square(x - mu), axis=-1, keepdims=True)
            return (x - mu) * jax.lax.rsqrt(var + EPS) * gamma + beta
        key = jax.random.key(seed)
        ks = jax.random.split(key, 8)
        B, Sq, Sk, D = (2, 512, 512, 256)
        s = 1.0 / math.sqrt(D)
        return {'Q': jax.random.normal(ks[0], (B, Sq, D), jnp.float32), 'K': jax.random.normal(ks[1], (B, Sk, D), jnp.float32), 'Wq': jax.random.normal(ks[2], (D, D), jnp.float32) * s, 'bq': jnp.zeros((D,), jnp.float32), 'Wk': jax.random.normal(ks[3], (D, D), jnp.float32) * s, 'bk': jnp.zeros((D,), jnp.float32), 'Wv': jax.random.normal(ks[4], (D, D), jnp.float32) * s, 'bv': jnp.zeros((D,), jnp.float32), 'Wo': jax.random.normal(ks[5], (D, D), jnp.float32) * s, 'bo': jnp.zeros((D,), jnp.float32), 'g0': jnp.ones((D,), jnp.float32), 'b0': jnp.zeros((D,), jnp.float32), 'g1': jnp.ones((D,), jnp.float32), 'b1': jnp.zeros((D,), jnp.float32)}
    _L0_xattn_all = _L0_xattn_setup()
    _L0_xattn_in = {k: v for k, v in _L0_xattn_all.items() if k in ('Wq', 'bq', 'Wk', 'bk', 'Wv', 'bv', 'Wo', 'bo', 'g0', 'b0', 'g1', 'b1')}
    del _L0_xattn_all

    def _L0_ffn_setup():
        import jax, jax.numpy as jnp
        import numpy as np
        DIM = 256

        def _reference_tuple_inner(x, W_r, W_k, W_v, mu_r, mu_k):
            B, T, C = x.shape
            x_prev = jnp.concatenate([jnp.zeros((B, 1, C), x.dtype), x[:, :-1, :]], axis=1)
            xr = mu_r * x + (1.0 - mu_r) * x_prev
            xk = mu_k * x + (1.0 - mu_k) * x_prev
            r = jax.nn.sigmoid(jnp.einsum('btc,dc->btd', xr, W_r))
            k = jnp.einsum('btc,dc->btd', xk, W_k)
            k_act = jnp.square(jax.nn.relu(k))
            out = r * jnp.einsum('btc,dc->btd', k_act, W_v)
            new_state = x[:, -1, :]
            return (out, new_state)
        key = jax.random.key(seed)
        ks = jax.random.split(key, 6)
        B, T, C = (8, 512, DIM)
        x = jax.random.normal(ks[0], (B, T, C), dtype=jnp.float32)
        s = 1.0 / np.sqrt(C)
        W_r = jax.random.uniform(ks[1], (C, C), jnp.float32, -s, s)
        W_k = jax.random.uniform(ks[2], (C, C), jnp.float32, -s, s)
        W_v = jax.random.uniform(ks[3], (C, C), jnp.float32, -s, s)
        mu_r = jax.random.uniform(ks[4], (C,), jnp.float32)
        mu_k = jax.random.uniform(ks[5], (C,), jnp.float32)
        return {'x': x, 'W_r': W_r, 'W_k': W_k, 'W_v': W_v, 'mu_r': mu_r, 'mu_k': mu_k}
    _L0_ffn_all = _L0_ffn_setup()
    _L0_ffn_in = {k: v for k, v in _L0_ffn_all.items() if k in ('W_r', 'W_k', 'W_v', 'mu_r', 'mu_k')}
    del _L0_ffn_all
    return {'x': x, 'ctx_1024': ctx_1024, 'L0_attn_Wq': _L0_attn_in['Wq'], 'L0_attn_bq': _L0_attn_in['bq'], 'L0_attn_Wk': _L0_attn_in['Wk'], 'L0_attn_bk': _L0_attn_in['bk'], 'L0_attn_Wv': _L0_attn_in['Wv'], 'L0_attn_bv': _L0_attn_in['bv'], 'L0_xattn_Wq': _L0_xattn_in['Wq'], 'L0_xattn_bq': _L0_xattn_in['bq'], 'L0_xattn_Wk': _L0_xattn_in['Wk'], 'L0_xattn_bk': _L0_xattn_in['bk'], 'L0_xattn_Wv': _L0_xattn_in['Wv'], 'L0_xattn_bv': _L0_xattn_in['bv'], 'L0_xattn_Wo': _L0_xattn_in['Wo'], 'L0_xattn_bo': _L0_xattn_in['bo'], 'L0_xattn_g0': _L0_xattn_in['g0'], 'L0_xattn_b0': _L0_xattn_in['b0'], 'L0_xattn_g1': _L0_xattn_in['g1'], 'L0_xattn_b1': _L0_xattn_in['b1'], 'L0_ffn_W_r': _L0_ffn_in['W_r'], 'L0_ffn_W_k': _L0_ffn_in['W_k'], 'L0_ffn_W_v': _L0_ffn_in['W_v'], 'L0_ffn_mu_r': _L0_ffn_in['mu_r'], 'L0_ffn_mu_k': _L0_ffn_in['mu_k']}

def reference(x, ctx_1024, L0_attn_Wq, L0_attn_bq, L0_attn_Wk, L0_attn_bk, L0_attn_Wv, L0_attn_bv, L0_xattn_Wq, L0_xattn_bq, L0_xattn_Wk, L0_xattn_bk, L0_xattn_Wv, L0_xattn_bv, L0_xattn_Wo, L0_xattn_bo, L0_xattn_g0, L0_xattn_b0, L0_xattn_g1, L0_xattn_b1, L0_ffn_W_r, L0_ffn_W_k, L0_ffn_W_v, L0_ffn_mu_r, L0_ffn_mu_k):
    import jax
    import jax.numpy as jnp

    def _L0_attn_ref(x, Wq, bq, Wk, bk, Wv, bv):
        import jax, jax.numpy as jnp
        import numpy as np
        EPS = 1e-08

        def unit_projection(x):
            f = jnp.fft.fft(x)
            f = f / (jnp.abs(f) + EPS)
            return jnp.fft.ifft(f).real

        def bind(a, b):
            return jnp.fft.ifft(jnp.fft.fft(a) * jnp.fft.fft(b)).real

        def unbind(s, a):
            return jnp.fft.ifft(jnp.fft.fft(s) * jnp.conj(jnp.fft.fft(a))).real
        query = unit_projection(jnp.einsum('bsd,ed->bse', x, Wq) + bq)
        keys = unit_projection(jnp.einsum('bsd,ed->bse', x, Wk) + bk)
        values = unit_projection(jnp.einsum('bsd,ed->bse', x, Wv) + bv)
        x_k = bind(keys, values)
        s = jnp.cumsum(x_k, axis=1)
        out = unbind(s, query)
        return out

    def _L0_xattn_ref(Q, K, Wq, bq, Wk, bk, Wv, bv, Wo, bo, g0, b0, g1, b1):
        import jax, jax.numpy as jnp
        import numpy as np
        import math
        EPS = 1e-05

        def _layernorm(x, gamma, beta):
            mu = jnp.mean(x, axis=-1, keepdims=True)
            var = jnp.mean(jnp.square(x - mu), axis=-1, keepdims=True)
            return (x - mu) * jax.lax.rsqrt(var + EPS) * gamma + beta
        H = 16
        B, Sq, D = Q.shape
        dh = D // H
        Qp = Q @ Wq + bq
        Kp = K @ Wk + bk
        Vp = Kp @ Wv + bv
        Qh = Qp.reshape(B, Sq, H, dh).transpose(0, 2, 1, 3)
        Kh = Kp.reshape(B, -1, H, dh).transpose(0, 2, 1, 3)
        Vh = Vp.reshape(B, -1, H, dh).transpose(0, 2, 1, 3)
        scores = jnp.einsum('bhqd,bhkd->bhqk', Qh, Kh) / math.sqrt(dh)
        attn = jax.nn.softmax(scores, axis=-1)
        Oh = Qh + jnp.einsum('bhqk,bhkd->bhqd', attn, Vh)
        O = Oh.transpose(0, 2, 1, 3).reshape(B, Sq, D)
        O = _layernorm(O, g0, b0)
        O = O + jax.nn.gelu(O @ Wo + bo, approximate=False)
        O = _layernorm(O, g1, b1)
        return O

    def _L0_ffn_ref(x, W_r, W_k, W_v, mu_r, mu_k):
        import jax, jax.numpy as jnp
        import numpy as np
        DIM = 256

        def _reference_tuple_inner(x, W_r, W_k, W_v, mu_r, mu_k):
            B, T, C = x.shape
            x_prev = jnp.concatenate([jnp.zeros((B, 1, C), x.dtype), x[:, :-1, :]], axis=1)
            xr = mu_r * x + (1.0 - mu_r) * x_prev
            xk = mu_k * x + (1.0 - mu_k) * x_prev
            r = jax.nn.sigmoid(jnp.einsum('btc,dc->btd', xr, W_r))
            k = jnp.einsum('btc,dc->btd', xk, W_k)
            k_act = jnp.square(jax.nn.relu(k))
            out = r * jnp.einsum('btc,dc->btd', k_act, W_v)
            new_state = x[:, -1, :]
            return (out, new_state)
        return _reference_tuple_inner(x, W_r, W_k, W_v, mu_r, mu_k)[0]
    x = x + _L0_attn_ref(_layernorm(x, axis=-1), L0_attn_Wq, L0_attn_bq, L0_attn_Wk, L0_attn_bk, L0_attn_Wv, L0_attn_bv)
    x = x + _L0_xattn_ref(_layernorm(x, axis=-1), ctx_1024, L0_xattn_Wq, L0_xattn_bq, L0_xattn_Wk, L0_xattn_bk, L0_xattn_Wv, L0_xattn_bv, L0_xattn_Wo, L0_xattn_bo, L0_xattn_g0, L0_xattn_b0, L0_xattn_g1, L0_xattn_b1)
    x = x + _L0_ffn_ref(_layernorm(x, axis=-1), L0_ffn_W_r, L0_ffn_W_k, L0_ffn_W_v, L0_ffn_mu_r, L0_ffn_mu_k)
    return x

_drawn_inputs = setup_inputs


def setup_inputs(seed=0):
    import zlib

    import numpy as np

    out = dict(_drawn_inputs(seed))
    spreads = {'L0_xattn_bq': (0.0, 0.1),
     'L0_xattn_bk': (0.0, 0.1),
     'L0_xattn_bv': (0.0, 0.1),
     'L0_xattn_bo': (0.0, 0.1),
     'L0_xattn_g0': (1.0, 0.2),
     'L0_xattn_b0': (0.0, 0.1),
     'L0_xattn_g1': (1.0, 0.2),
     'L0_xattn_b1': (0.0, 0.1)}
    factors = {'L0_ffn_W_r': 4.403, 'L0_ffn_mu_r': 8.0}
    for name, (base, spread) in spreads.items():
        noise = np.random.default_rng([zlib.crc32(name.encode()), seed]).standard_normal(out[name].shape)
        drawn = base * np.exp(spread * noise) if base else spread * noise
        out[name] = jnp.asarray(drawn.astype(out[name].dtype))
    for name, factor in factors.items():
        out[name] = (out[name] * factor).astype(out[name].dtype)
    return out
```

```python
from contextlib import ExitStack

import numpy as np

import concourse.bass as bass
from concourse import mybir

ALU = mybir.AluOpType
ACT = mybir.ActivationFunctionType
AX = mybir.AxisListType
F32 = mybir.dt.float32
BF16 = mybir.dt.bfloat16

P = 128
B = 32
S = 256
D = 256
H = 16
DH = D // H
ST = S // P
DC = D // P
HP = P // DH
SPLITS = 6
KROWS = SPLITS * DH
R = 3
EPS_UNIT = 1e-8
EPS_LN = 1e-5
LN_FLOOR = float(2.0 ** -64)
SOFTMAX_SCALE = float(DH) ** -0.5
NBINS = D // 2 + 1

Q_LO, Q_HI, Q_MID = 0, 1, 2
K_MID, K_HI, K_LO = 0, 1, 2
Q_RUNS = [(0, Q_HI, 2), (2, Q_LO, 2), (4, Q_HI, 2)]
K_RUNS = [(0, K_MID, 2), (2, K_HI, 2), (4, K_HI, 1), (5, K_MID, 1)]

NB = 7
BK_F, BV_F, BQ_F, B_Q, B_K, B_V, B_O = range(NB)

HEAD_SEMS = 8

SLOTS = 16
LAST_OFF = 5
FIRST_STEP = -1
LOOP_FIRST = 7
LOOP_STEPS = 24
END_STEP = B + LAST_OFF


class Shared:
    pass


class Step:

    def __init__(self, t, i=None, batches=B):
        self.t, self.i, self.batches = t, i, batches

    def live(self, off):
        return self.i is not None or 0 <= self.t - off < self.batches

    def batch(self, off):
        return self.t - off if self.i is None else R * self.i + (self.t - off)

    def slot(self, off):
        return (self.t - off) % R

    def after(self, off, lag=0):
        n = self.t - off - lag + 1
        return min(n, self.batches) if self.i is None else R * self.i + n

    def after_head(self, off, h, lag=0):
        n = self.t - off - lag
        if self.i is None:
            return 2 * self.batches if n >= self.batches else 2 * n + h // HEAD_SEMS + 1
        return 2 * R * self.i + 2 * n + h // HEAD_SEMS + 1

    def dma_after(self, off, dmas=1, lag=0):
        n = 16 * dmas * ((self.t - off) // R + 1 - lag)
        return n if self.i is None else 16 * dmas * self.i + n


def wait(eng, sem, value):
    if not (isinstance(value, int) and value <= 0):
        eng.wait_ge(sem, value)


def wait_all(eng, *pairs):
    for _, value in pairs:
        if not isinstance(value, int):
            eng.to_reg(value)
    for sem, value in pairs:
        wait(eng, sem, value)


def run_steps(eng, step, first, loop_first, loop_steps, end, batches=B):
    for t in range(first, loop_first):
        step(Step(t, batches=batches))
    with eng.Fori(0, loop_steps // R) as i:
        for j in range(R):
            step(Step(loop_first + j, i, batches))
    for t in range(loop_first + loop_steps, end):
        step(Step(t, batches=batches))


def decoder_kernel(nc, x, ctx, attn_w, attn_b, wq, wk, wv, wo, rows, g0c, wr_t, wk_t, wv_t, dft, idft, tri,
                   ident, masks, out):
    q_dram = nc.dram_tensor("q_scratch", (R, 3, P, DC * S), BF16)
    k_dram = nc.dram_tensor("k_scratch", (R, 3, P, DC * S), BF16)
    m_dram = nc.dram_tensor("m_scratch", (R, 3, H * S), BF16)
    x1_dram = nc.dram_tensor("x1_rows", (B, S, D), F32)
    o_dram = nc.dram_tensor("o_rows", (B, S, D), F32)

    with ExitStack() as stack:
        def sb(name, shape, dt=F32):
            return stack.enter_context(nc.sbuf_tensor(name, list(shape), dt))

        def sem(name):
            return stack.enter_context(nc.semaphore(name))

        wf = sb("wf", [P, 3, DC, D])
        wq_sb = sb("wq_sb", [P, DC, D])
        wk_sb = sb("wk_sb", [P, DC, D])
        wv_sb = sb("wv_sb", [P, DC, D])
        wo_sb = sb("wo_sb", [P, DC, D])
        wr_sb = sb("wr_sb", [P, DC, D])
        wkf_sb = sb("wkf_sb", [P, DC, D])
        wvf_sb = sb("wvf_sb", [P, DC, D])
        idft_sb = sb("idft_sb", [P, DC, D])
        tri_sb = sb("tri_sb", [P, 2, P])
        id_sb = sb("id_sb", [P, P])
        idb_sb = sb("idb_sb", [P, P], BF16)
        bias_rows = sb("bias_rows", [P, NB, 2, D], BF16)
        ones_bf = sb("ones_bf", [P, S], BF16)
        vec = sb("vec", [P, 3, D])
        g0_row = sb("g0_row", [P, D])
        cols = sb("cols", [P, 4, DC])
        mask_sb = sb("mask_sb", [P, 4])
        eps_sb = sb("eps_sb", [P, ST])
        half_neg = sb("half_neg", [P, ST])

        psum = [stack.enter_context(nc.psum_tensor(f"bank{i}", [P, 512], F32)) for i in range(8)]

        setup_done = sem("setup_done")
        w_in = sem("w_in")
        setup_mm = sem("setup_mm")
        setup_pe = sem("setup_pe")
        setup_v = sem("setup_v")
        setup_g = sem("setup_g")

        with ExitStack() as tmp:
            def tb(name, shape, dt=F32):
                return tmp.enter_context(nc.sbuf_tensor(name, list(shape), dt))

            aw = tb("aw", [P, 3, DC, D])
            ab = tb("ab", [P, 3, DC])
            dft_sb = tb("dft_sb", [P, DC, D])
            rw = tb("rw", [P, 4, D])
            abw = tb("abw", [P, 3, DC, P])
            b0w = tb("b0w", [P, DC, P])
            row = tb("row", [P, D])
            hi = tb("hi", [P, D], BF16)
            rest = tb("rest", [P, D])
            mid = tb("mid", [P, D], BF16)
            rest2 = tb("rest2", [P, D])
            acc1 = tb("acc1", [P, D])
            acc2 = tb("acc2", [P, D])
            wo_raw = tb("wo_raw", [P, DC, D])
            wv_raw = tb("wv_raw", [P, DC, D])
            N_LOADS = 19

            with nc.Block() as block:
                @block.sync
                def _(sp):
                    def load(dst, src):
                        sp.dma_start(dst, src).then_inc(w_in, 16)

                    for i in range(3):
                        load(aw[:, i], attn_w[i].rearrange("(c p) n -> p c n", p=P))
                    load(ab[:], attn_b)
                    load(dft_sb[:], dft.rearrange("(c p) n -> p c n", p=P))
                    load(idft_sb[:], idft.rearrange("(c p) n -> p c n", p=P))
                    for dst, src in ((wq_sb, wq), (wk_sb, wk), (wv_sb, wv), (wo_raw, wo), (wr_sb, wr_t),
                                     (wkf_sb, wk_t), (wv_raw, wv_t)):
                        load(dst[:], src.rearrange("(c p) n -> p c n", p=P))
                    load(tri_sb[:], tri)
                    load(id_sb[:], ident)
                    load(rw[:], rows[0:4].partition_broadcast(P))
                    load(vec[:], rows[4:7].partition_broadcast(P))
                    load(cols[:], g0c)
                    load(mask_sb[:], masks)
                    sp.wait_ge(w_in, 16 * N_LOADS)
                    sp.wait_ge(setup_v, SETUP_V)

                @block.gpsimd
                def _(pool):
                    pool.memset(ones_bf[:], 1.0).then_inc(setup_g, 1)
                    pool.memset(eps_sb[:], EPS_LN).then_inc(setup_g, 1)
                    pool.memset(half_neg[:], -0.5).then_inc(setup_g, 1)
                    pool.wait_ge(setup_g, 3)

                @block.tensor
                def _(pe):
                    pe.wait_ge(w_in, 16 * N_LOADS)
                    for i in range(3):
                        for c in range(DC):
                            for e in range(DC):
                                last = pe.matmul(psum[i][:, c * D:(c + 1) * D], aw[:, i, e, c * P:(c + 1) * P],
                                                 dft_sb[:, e, :], start=(e == 0), stop=(e == DC - 1))
                        last.then_inc(setup_mm, 1)
                    pe.wait_ge(setup_pe, 1)
                    for i in range(3):
                        for e in range(DC):
                            last = pe.matmul(psum[3 + i][:, 0:D], abw[:, i, e, :], dft_sb[:, e, :],
                                             start=(e == 0), stop=(e == DC - 1))
                        last.then_inc(setup_mm, 1)
                    for e in range(DC):
                        last = pe.matmul(psum[6][:, 0:D], b0w[:, e, :], wo_raw[:, e, :],
                                         start=(e == 0), stop=(e == DC - 1))
                    last.then_inc(setup_mm, 1)

                n_v = [0]

                @block.vector
                def _(v):
                    def chain(ins):
                        n_v[0] += 1
                        ins.then_inc(setup_v, 1)
                        v.wait_ge(setup_v, n_v[0])

                    v.wait_ge(w_in, 16 * N_LOADS)
                    v.wait_ge(setup_g, 3)
                    for i in range(3):
                        for c in range(DC):
                            chain(v.tensor_scalar(abw[:, i, c, :], tri_sb[:, 1, :], ab[:, i, c:c + 1], None, ALU.mult))
                    for c in range(DC):
                        chain(v.tensor_scalar(b0w[:, c, :], tri_sb[:, 1, :], cols[:, 1, c:c + 1], None, ALU.mult))
                    v.tensor_copy(idb_sb[:], id_sb[:]).then_inc(setup_pe, 1)
                    v.wait_ge(setup_pe, 1)
                    for c in range(DC):
                        chain(v.tensor_scalar(wo_sb[:, c, :], wo_raw[:, c, :], cols[:, 0, c:c + 1], None, ALU.mult))
                    chain(v.tensor_scalar(wvf_sb[:], wv_raw[:], 0.5, None, ALU.mult))
                    chain(v.tensor_copy(g0_row[:], rw[:, 3, :]))
                    for i in range(3):
                        v.wait_ge(setup_mm, i + 1)
                        chain(v.tensor_copy(wf[:, i], psum[i][:, :].rearrange("p (c n) -> p c n", c=DC)))

                    def split_rows(n):
                        chain(v.tensor_copy(hi[:], row[:]))
                        chain(v.tensor_tensor(rest[:], row[:], hi[:], ALU.subtract))
                        chain(v.tensor_copy(mid[:], rest[:]))
                        chain(v.tensor_tensor(rest2[:], rest[:], mid[:], ALU.subtract))
                        chain(v.tensor_scalar(acc1[:], hi[:], mask_sb[:, 0:1], None, ALU.mult))
                        chain(v.scalar_tensor_tensor(acc2[:], mid[:], mask_sb[:, 1:2], acc1[:], ALU.mult, ALU.add))
                        for d in range(2):
                            chain(v.scalar_tensor_tensor(bias_rows[:, n, d, :], rest2[:], mask_sb[:, 2:3], acc2[:],
                                                         ALU.mult, ALU.add))

                    for i in range(3):
                        v.wait_ge(setup_mm, 4 + i)
                        chain(v.tensor_copy(row[:], psum[3 + i][:, 0:D]))
                        split_rows(BK_F + i)
                    for i in range(3):
                        chain(v.tensor_copy(row[:], rw[:, i, :]))
                        split_rows(B_Q + i)
                    v.wait_ge(setup_mm, 7)
                    chain(v.tensor_tensor(row[:], psum[6][:, 0:D], g0_row[:], ALU.add))
                    split_rows(B_O)
                    v.wait_ge(setup_v, n_v[0])
                    assert n_v[0] == SETUP_V, n_v[0]

            with nc.Block() as block:
                @block.sync
                def _(sp):
                    sp.dma_start(g0_row[:], rows[7].partition_broadcast(P)).then_inc(setup_done, 16)
                    sp.wait_ge(setup_done, 16)

        w = Shared()
        w.wf = wf
        w.wq = wq_sb
        w.wk = wk_sb
        w.wv = wv_sb
        w.wo = wo_sb
        w.wr = wr_sb
        w.wkf = wkf_sb
        w.wvf = wvf_sb
        w.idft = idft_sb
        w.tri = tri_sb
        w.ident = id_sb
        w.ident_bf = idb_sb
        w.bias = bias_rows
        w.ones = ones_bf
        w.g0 = g0_row[:]
        w.b0 = vec[:, 0]
        w.g1 = vec[:, 1]
        w.b1 = vec[:, 2]
        w.mu_r = cols[:, 2]
        w.mu_k = cols[:, 3]
        w.eps_unit = mask_sb[:, 3:4]
        w.eps = eps_sb
        w.half_neg = half_neg
        w.ready = setup_done
        attention(nc, w, psum, x, ctx, q_dram, k_dram, m_dram, x1_dram, o_dram)
        feed_forward(nc, w, psum, x1_dram, o_dram, out)


SETUP_V = 6 + 2 + 2 + 1 + 1 + 3 + 3 * (1 + 8) * 2 + (1 + 8)


PIECES = [(0, "spec_k"), (5, "turn_o1"), (0, "spec_v"), (1, "turn_g"), (0, "spec_q"), (2, "turn_q"), (1, "inverse"),
          (0, None), (2, "proj_v"), (3, "turn_m"), (1, "proj_k"), (1, "turn_h2"), (0, "cumsum"), (-1, "turn_h"),
          (1, "proj_q"), (4, "turn_o0")]
N_FIRST = 7
T_FIRST = 14
PV_SLOT = {3: (0, 4), 7: (1, 4), 11: (2, 4), 15: (3, 4)}
O_OFF = (4, 5)
N_OFF = 2
T_OFF = 3


def n_head(slot):
    return (slot - N_FIRST, N_OFF) if slot >= N_FIRST else (slot - N_FIRST + SLOTS, N_OFF + 1)


def t_head(slot):
    return (slot - T_FIRST, T_OFF) if slot >= T_FIRST else (slot - T_FIRST + SLOTS, T_OFF + 1)


def attention(nc, w, psum, x, ctx, q_dram, k_dram, m_dram, x1_dram, o_dram):
    with ExitStack() as stack:
        def sb(name, shape, dt=F32):
            return stack.enter_context(nc.sbuf_tensor(name, list(shape), dt))

        sems = []

        def sem(name):
            sems.append(nc.alloc_semaphore(name))
            return sems[-1]

        x_sb = sb("x_sb", [P, R, ST, D])
        h_sb = sb("h_sb", [P, ST, D])
        hT = sb("hT", [P, DC, S])
        spec = sb("spec", [P, 3, ST, D])
        sq = sb("sq", [P, 3, ST, D])
        mag = sb("mag", [P, 3, ST, NBINS])
        mag2 = sb("mag2", [P, 3, ST, NBINS])
        inv = sb("inv", [P, 2, ST, NBINS])
        kv_direct = sb("kv_direct", [P, ST, D])
        kv_cross = sb("kv_cross", [P, ST, D])
        kv = sb("kv", [P, ST, D])
        bound = sb("bound", [P, ST, D])
        unit_q = sb("unit_q", [P, ST, D])
        sums = sb("sums", [P, ST, D])
        g_direct = sb("g_direct", [P, ST, D])
        g_cross = sb("g_cross", [P, ST, D])
        g_sb = sb("g_sb", [P, ST, D])
        gT = sb("gT", [P, DC, S])
        x1 = sb("x1", [P, ST, D])
        h2 = sb("h2", [P, ST, D])
        h2T = sb("h2T", [P, DC, S])
        cT = sb("cT", [P, DC, S])
        kT = sb("kT", [P, DC * S])
        qT = sb("qT", [P, DC * S])
        q_parts = sb("q_parts", [P, 3, DC * S], BF16)
        k_parts = sb("k_parts", [P, 3, DC * S], BF16)
        q_rest = sb("q_rest", [P, DC * S])
        k_rest = sb("k_rest", [P, DC * S])
        q_stack = sb("q_stack", [P, R, H, S], BF16)
        k_stack = sb("k_stack", [P, R, H, S], BF16)
        v_sb = sb("v_sb", [P, R, ST, H, 2 * DH])
        neg_max = sb("neg_max", [P, R, ST, H])
        max_rest = sb("max_rest", [P, ST, H])
        max_parts = sb("max_parts", [P, ST, P], BF16)
        mT = sb("mT", [3 * H, ST, P], BF16)
        probs = sb("probs", [P, 8, ST, S])
        oT = sb("oT", [P, 2, 2, S])
        den = sb("den", [P, 2, ST, 8])
        heads = sb("heads", [P, 2, ST, 8, DH])
        q_rows = sb("q_rows", [P, R, ST, D])
        o_sb = sb("o_sb", [P, ST, D])
        stats = sb("stats", [P, 2, ST, 6])
        moments = sb("moments", [P, 2, ST, 2])
        guard = sb("guard", [P, 2])
        var_eps = sb("var_eps", [P, 2, ST])
        rstd = sb("rstd", [P, 2, ST])
        zeros = sb("zeros", [P, ST, H])

        n_bank = psum[0:2]
        t_bank = psum[2:4]
        pv_bank = psum[4:6]
        work = psum[6:8]

        x_in = [sem(f"x_in{r}") for r in range(R)]
        c_in = [sem(f"c_in{r}") for r in range(R)]
        q_out = [sem(f"q_out{r}") for r in range(R)]
        k_out = [sem(f"k_out{r}") for r in range(R)]
        q_in = [sem(f"q_in{r}") for r in range(R)]
        k_in = [sem(f"k_in{r}") for r in range(R)]
        m_out = [sem(f"m_out{r}") for r in range(R)]
        m_in = [sem(f"m_in{r}") for r in range(R)]
        x1_out = [sem(f"x1_out{r}") for r in range(R)]
        o_out = [sem(f"o_out{r}") for r in range(R)]
        buffers_set = sem("buffers_set")
        stats_done = [sem("stats_done0"), sem("stats_done1")]
        moments_done = [sem("moments_done0"), sem("moments_done1")]
        guard_set = [sem("guard_set0"), sem("guard_set1")]
        var_done = [sem("var_done0"), sem("var_done1")]
        rstd_done = [sem("rstd_done0"), sem("rstd_done1")]
        h_done, h2_done = sem("h_done"), sem("h2_done")
        pe_done = {name: sem("pe_" + name) for _, name in PIECES if name}
        hT_done, h2T_done, gT_done = sem("hT_done"), sem("h2T_done"), sem("gT_done")
        spec_done = [sem(f"spec_done{i}") for i in range(3)]
        sq_done = [sem(f"sq_done{i}") for i in range(3)]
        mag_done, log_done, abs_done, log2_done = sem("mag_done"), sem("log_done"), sem("abs_done"), sem("log2_done")
        log_kv_done, inv_done = sem("log_kv_done"), sem("inv_done")
        kv_products, kv_done, bound_done, unit_q_done = (sem("kv_products"), sem("kv_done"), sem("bound_done"),
                                                         sem("unit_q_done"))
        sums_done, g_products, g_done = sem("sums_done"), sem("g_products"), sem("g_done")
        x1_done = sem("x1_done")
        qT_done, kT_done = sem("qT_done"), sem("kT_done")
        q_hi, q_left, q_mid, q_lo = sem("q_hi"), sem("q_left"), sem("q_mid"), sem("q_lo")
        k_hi, k_left, k_mid, k_lo = sem("k_hi"), sem("k_left"), sem("k_mid"), sem("k_lo")
        v_done = sem("v_done")
        n_scores = [sem(f"n_scores{h}") for h in range(HEAD_SEMS)]
        max_done = [sem(f"max_done{h}") for h in range(HEAD_SEMS)]
        m_hi, m_left, m_mid, m_left2, m_lo, mT_done = (sem("m_hi"), sem("m_left"), sem("m_mid"), sem("m_left2"),
                                                       sem("m_lo"), sem("mT_done"))
        t_scores = [sem(f"t_scores{h}") for h in range(HEAD_SEMS)]
        exp_done = [sem(f"exp_done{h}") for h in range(HEAD_SEMS)]
        pv_done = [sem(f"pv_done{g}") for g in range(4)]
        oT_done = [sem("oT_done0"), sem("oT_done1")]
        o_set = sem("o_set")
        den_done = [sem("den_done0"), sem("den_done1")]
        heads_done = [sem("heads_done0"), sem("heads_done1")]
        o_added = [sem("o_added0"), sem("o_added1")]

        emptied = {"turn_h": hT_done, "turn_q": o_set, "turn_g": gT_done, "spec_k": spec_done[0],
                   "spec_v": spec_done[1], "turn_m": mT_done, "spec_q": spec_done[2], "inverse": x1_done,
                   "turn_o0": heads_done[0], "turn_h2": h2T_done, "proj_k": kT_done,
                   "proj_q": qT_done, "cumsum": sums_done, "turn_o1": heads_done[1], "proj_v": v_done}

        def ends(a):
            return a[:, :, 0:2 * P:P]

        def bins(a, half):
            return a[:, :, half * P + 1:(half + 1) * P]

        block = stack.enter_context(nc.Block())

        @block.sync
        def _(sp):
            def step(st):
                if st.live(2):
                    r = st.slot(2)
                    for parts_done, parts, dram, out_sem, in_sem, to, runs in (
                            (k_lo, k_parts, k_dram, k_out, k_in, k_stack, K_RUNS),
                            (q_lo, q_parts, q_dram, q_out, q_in, q_stack, Q_RUNS)):
                        wait_all(sp, (pv_done[-1], st.after(2, R)), (parts_done, st.after(2)),
                                 (in_sem[r], st.dma_after(2, dmas=len(runs), lag=1)))
                        sp.dma_start(dram[r].rearrange("s p n -> p s n"), parts[:]).then_inc(out_sem[r], 16)
                        wait_all(sp, (out_sem[r], st.dma_after(2)))
                        for group, part, n in runs:
                            sp.dma_start(to[DH * group:DH * (group + n), r].rearrange("p h n -> p (h n)"),
                                         dram[r, part:part + n].rearrange("s (d h) n -> (s d) (h n)", h=HP)) \
                                .then_inc(in_sem[r], 16)
                if st.live(-1):
                    wait_all(sp, (x1_done, st.after(-1, R)))
                    r = st.slot(-1)
                    sp.dma_start(x_sb[:, r], rows_of(x, st.batch(-1))).then_inc(x_in[r], 16)
                if st.live(5):
                    wait_all(sp, (o_added[0], st.after(5)), (o_added[1], st.after(5)))
                    sp.dma_start(rows_of(o_dram, st.batch(5)), o_sb[:]).then_inc(o_out[st.slot(5)], 16)
                if st.live(1):
                    wait_all(sp, (x1_done, st.after(1)))
                    sp.dma_start(rows_of(x1_dram, st.batch(1)), x1[:]).then_inc(x1_out[st.slot(1)], 16)
                if st.live(3):
                    r = st.slot(3)
                    wait_all(sp, (mT_done, st.after(3)), (m_in[r], st.dma_after(3, lag=1)))
                    sp.dma_start(m_dram[r].rearrange("s (h n) -> (s h) n", n=S), mT[:].rearrange("p a b -> p (a b)")) \
                        .then_inc(m_out[r], 16)
                    wait_all(sp, (m_out[r], st.dma_after(3)), (pv_done[-1], st.after(3, R)))
                    sp.dma_start(q_stack[KROWS:KROWS + 3, r].rearrange("p h n -> p (h n)"), m_dram[r]) \
                        .then_inc(m_in[r], 16)
                if st.live(0):
                    wait_all(sp, (pe_done["proj_k"], st.after(0, 1)))
                    sp.dma_start(cT[:], one_of(ctx, st.batch(0))).then_inc(c_in[st.slot(0)], 16)

            run_steps(sp, step, FIRST_STEP, LOOP_FIRST, LOOP_STEPS, END_STEP)
            for r in range(R):
                n = 16 * len(range(r, B, R))
                sp.wait_ge(x1_out[r], n)
                sp.wait_ge(o_out[r], n)
                sp.wait_ge(m_out[r], n)
                sp.wait_ge(k_out[r], n)
                sp.wait_ge(q_out[r], n)

        @block.tensor
        def _(pe):
            def bank_free(st, slot):
                for back in range(2, SLOTS + 1, 2):
                    before = Step(st.t - (slot < back), st.i)
                    off, name = PIECES[(slot - back) % SLOTS]
                    if name and before.live(off):
                        wait(pe, emptied[name], before.after(off))
                        return

            def turn(bank, source, name):
                for s in range(ST):
                    for c in range(DC):
                        last = pe.transpose(bank[:, c * S + s * P:c * S + (s + 1) * P],
                                            source[:, s, c * P:(c + 1) * P], w.ident[:])
                last.then_inc(pe_done[name], 1)

            def rows_times(bank, left, right, name, bias=None):
                if bias is not None:
                    pe.matmul(bank[:], w.ones[:, 0:P], w.bias[:, bias].rearrange("p a n -> p (a n)"), start=True,
                              stop=False, skip_group_check=True)
                for s in range(ST):
                    for c in range(DC):
                        last = pe.matmul(bank[:, s * D:(s + 1) * D], left[:, c, s * P:(s + 1) * P], right[:, c],
                                         start=(bias is None and s == 0 and c == 0), stop=(c == DC - 1),
                                         skip_group_check=True)
                last.then_inc(pe_done[name], 1)

            def turned_times(bank, right, weight, name, bias):
                for m in range(DC):
                    pe.matmul(bank[:, m * S:(m + 1) * S], w.bias[:, bias, 0, m * P:(m + 1) * P], w.ones[:],
                              start=(m == 0), stop=False, skip_group_check=True)
                    for c in range(DC):
                        last = pe.matmul(bank[:, m * S:(m + 1) * S], weight[:, c, m * P:(m + 1) * P], right[:, c],
                                         start=False, stop=(c == DC - 1), skip_group_check=True)
                last.then_inc(pe_done[name], 1)

            def piece(st, slot):
                off, name = PIECES[slot]
                if name is None or not st.live(off):
                    return
                bank = work[slot % 2]
                bank_free(st, slot)
                if name == "turn_h":
                    wait(pe, h_done, st.after(-1))
                    turn(bank, h_sb, name)
                elif name == "turn_q":
                    wait(pe, qT_done, st.after(2))
                    for s in range(ST):
                        for c in range(DC):
                            last = pe.transpose(bank[:, s * D + c * P:s * D + (c + 1) * P],
                                                qT[:, c * S + s * P:c * S + (s + 1) * P], w.ident[:])
                    last.then_inc(pe_done[name], 1)
                elif name == "turn_g":
                    wait(pe, g_done, st.after(1))
                    turn(bank, g_sb, name)
                elif name in ("spec_k", "spec_v", "spec_q"):
                    i = ("spec_k", "spec_v", "spec_q").index(name)
                    wait(pe, hT_done, st.after(0))
                    rows_times(bank, hT, w.wf[:, i], name, BK_F + i)
                elif name == "turn_m":
                    wait(pe, m_lo, st.after(3))
                    to = bank[:].bitcast(BF16)
                    for s in range(ST):
                        last = pe.transpose(to[:, s * P:(s + 1) * P], max_parts[:, s], w.ident_bf[:])
                    last.then_inc(pe_done[name], 1)
                elif name == "inverse":
                    wait(pe, gT_done, st.after(1))
                    rows_times(bank, gT, w.idft, name)
                elif name in ("turn_o0", "turn_o1"):
                    half = int(name[-1])
                    wait(pe, oT_done[half], st.after(off))
                    for s in range(ST):
                        for g in range(2):
                            last = pe.transpose(bank[:, s * 2 * P + g * P:s * 2 * P + (g + 1) * P],
                                                oT[:, half, g, s * P:(s + 1) * P], w.ident[:])
                    last.then_inc(pe_done[name], 1)
                elif name == "turn_h2":
                    wait(pe, h2_done, st.after(1))
                    turn(bank, h2, name)
                elif name == "proj_k":
                    pe.wait_ge(c_in[st.slot(1)], st.dma_after(1))
                    turned_times(bank, cT, w.wk, name, B_K)
                elif name == "proj_q":
                    wait(pe, h2T_done, st.after(1))
                    turned_times(bank, h2T, w.wq, name, B_Q)
                elif name == "proj_v":
                    wait(pe, kT_done, st.after(2))
                    rows_times(bank, kT[:].rearrange("p (c n) -> p c n", c=DC), w.wv, name, B_V)
                elif name == "cumsum":
                    wait(pe, bound_done, st.after(0))
                    pe.matmul(bank[:, 0:D], w.tri[:, 0], bound[:, 0], start=True, stop=True, skip_group_check=True)
                    pe.matmul(bank[:, D:2 * D], w.tri[:, 1], bound[:, 0], start=False, stop=False,
                              skip_group_check=True)
                    pe.matmul(bank[:, D:2 * D], w.tri[:, 0], bound[:, 1], start=False, stop=True,
                              skip_group_check=True).then_inc(pe_done[name], 1)

            def max_scores(st, slot):
                h, off = n_head(slot)
                if not st.live(off):
                    return
                r = st.slot(off)
                if h == 0:
                    pe.wait_ge(q_in[r], st.dma_after(off, dmas=len(Q_RUNS)))
                    pe.wait_ge(k_in[r], st.dma_after(off, dmas=len(K_RUNS)))
                wait(pe, max_done[(h - 2) % HEAD_SEMS], st.after_head(off, (h - 2) % H, 0 if h >= 2 else 1))
                for s in range(ST):
                    last = pe.matmul(n_bank[h % 2][:, s * S:(s + 1) * S], q_stack[0:KROWS, r, h, s * P:(s + 1) * P],
                                     k_stack[0:KROWS, r, h], start=True, stop=True, skip_group_check=True)
                last.then_inc(n_scores[h % HEAD_SEMS], 1)

            def exp_scores(st, slot):
                h, off = t_head(slot)
                if not st.live(off):
                    return
                r = st.slot(off)
                if h == 0:
                    pe.wait_ge(m_in[r], st.dma_after(off))
                wait(pe, exp_done[(h - 2) % HEAD_SEMS], st.after_head(off, (h - 2) % H, 0 if h >= 2 else 1))
                for s in range(ST):
                    last = pe.matmul(t_bank[h % 2][:, s * S:(s + 1) * S], k_stack[0:KROWS + 3, r, h, s * P:(s + 1) * P],
                                     q_stack[0:KROWS + 3, r, h], start=True, stop=True, skip_group_check=True)
                last.then_inc(t_scores[h % HEAD_SEMS], 1)

            def attend(st, slot):
                if slot not in PV_SLOT:
                    return
                g, off = PV_SLOT[slot]
                if not st.live(off):
                    return
                if g == 0:
                    wait(pe, v_done, st.after(off))
                if g % 2 == 0:
                    wait(pe, oT_done[g // 2], st.after(off, 1))
                wait(pe, exp_done[(4 * g + 3) % HEAD_SEMS], st.after_head(off, 4 * g + 3))
                for s in range(ST):
                    for j in range(4):
                        h = 4 * g + j
                        last = pe.matmul(pv_bank[g // 2][32 * j:32 * j + 32, (g % 2) * S:(g % 2 + 1) * S],
                                         v_sb[:, st.slot(off), s, h], probs[:, h % 8, s], start=(s == 0),
                                         stop=(s == ST - 1), skip_group_check=True)
                last.then_inc(pv_done[g], 1)

            def step(st):
                for slot in range(SLOTS):
                    max_scores(st, slot)
                    exp_scores(st, slot)
                    attend(st, slot)
                    piece(st, slot)

            pe.wait_ge(buffers_set, 4)
            run_steps(pe, step, FIRST_STEP, LOOP_FIRST, LOOP_STEPS, END_STEP)

        @block.scalar
        def _(act):
            def copy(to, bank, name, off, st, done, free=()):
                for s, v in free:
                    wait(act, s, v)
                wait(act, pe_done[name], st.after(off))
                act.activation(to, bank, ACT.Copy).then_inc(done, 1)

            def exps(st, slot):
                h, off = t_head(slot)
                if not st.live(off):
                    return
                wait(act, pv_done[(h - 8) % H // 4], st.after(off, 0 if h >= 8 else 1))
                wait(act, t_scores[h % HEAD_SEMS], st.after_head(off, h))
                act.activation(probs[:, h % 8].rearrange("p s n -> p (s n)"), t_bank[h % 2][:], ACT.Exp,
                               scale=SOFTMAX_SCALE).then_inc(exp_done[h % HEAD_SEMS], 1)

            def flat(a):
                return a.rearrange("p a n -> p (a n)")

            def step(st):
                for slot in range(SLOTS):
                    bank = work[slot % 2][:]
                    exps(st, slot)
                    off, name = PIECES[slot]
                    if slot in (0, 8):
                        half = 0 if slot == 8 else 1
                        at = O_OFF[half]
                        if st.live(at):
                            wait(act, pe_done[f"turn_o{half}"], st.after(at, 1))
                            wait(act, pv_done[2 * half + 1], st.after(at))
                            act.activation(flat(oT[:, half]), pv_bank[half][:], ACT.Copy).then_inc(oT_done[half], 1)
                    if slot == 8 and st.live(0):
                        wait(act, inv_done, st.after(0, 1))
                        wait(act, mag_done, st.after(0))
                        act.activation(mag2[:], mag[:], ACT.Ln).then_inc(log_done, 1)
                    if slot == 9 and st.live(0):
                        wait(act, log_done, st.after(0))
                        act.activation(mag[:], mag2[:], ACT.Exp, scale=0.5).then_inc(abs_done, 1)
                        wait(act, abs_done, st.after(0))
                        act.activation(mag2[:], mag[:], ACT.Ln, bias=w.eps_unit).then_inc(log2_done, 1)
                    if slot == 10 and st.live(0):
                        wait(act, bound_done, st.after(0, 1))
                        wait(act, unit_q_done, st.after(0, 1))
                        wait(act, log_kv_done, st.after(0))
                        act.activation(inv[:], mag2[:, 1:3], ACT.Exp, scale=-1.0).then_inc(inv_done, 1)
                    if name is None or not st.live(off):
                        continue
                    if name == "turn_h":
                        copy(flat(hT[:]), bank, name, -1, st, hT_done, [(pe_done["spec_q"], st.after(-1, 1))])
                    elif name == "turn_q":
                        r = st.slot(2)
                        wait(act, o_added[1], st.after(2, R))
                        wait(act, pe_done[name], st.after(2))
                        for s in range(ST):
                            to = q_rows[:, r, s].rearrange("p (h c d) -> p c d h", c=DC, d=DH)
                            last = act.activation(to, work[slot % 2][:, s * D:(s + 1) * D]
                                                  .rearrange("p (c d h) -> p c d h", c=DC, d=DH), ACT.Copy)
                        last.then_inc(o_set, 1)
                    elif name == "turn_g":
                        copy(flat(gT[:]), bank, name, 1, st, gT_done, [(pe_done["inverse"], st.after(1, 1))])
                    elif name in ("spec_k", "spec_v", "spec_q"):
                        i = ("spec_k", "spec_v", "spec_q").index(name)
                        free = [(sq_done[i], st.after(0, 1)),
                                ((unit_q_done if i == 2 else kv_products), st.after(0, 1))]
                        copy(flat(spec[:, i]), bank, name, 0, st, spec_done[i], free)
                    elif name == "turn_m":
                        if st.live(4):
                            wait(act, m_out[st.slot(4)], st.dma_after(4))
                        wait(act, pe_done[name], st.after(3))
                        act.activation(flat(mT[:]), work[slot % 2][0:3 * H].bitcast(BF16)[:, 0:2 * P], ACT.Copy) \
                            .then_inc(mT_done, 1)
                    elif name == "turn_h2":
                        copy(flat(h2T[:]), bank, name, 1, st, h2T_done, [(pe_done["proj_q"], st.after(1, 1))])
                    elif name == "proj_k":
                        free = [(k_left, st.after(1, 1)), (pe_done["proj_v"], st.after(1, 1))]
                        copy(kT[:], bank, name, 1, st, kT_done, free)
                    elif name == "proj_q":
                        free = [(q_left, st.after(1, 1)), (pe_done["turn_q"], st.after(1, 1))]
                        copy(qT[:], bank, name, 1, st, qT_done, free)
                    elif name == "cumsum":
                        copy(flat(sums[:]), bank, name, 0, st, sums_done, [(g_products, st.after(0, 1))])
                    elif name == "proj_v":
                        r = st.slot(2)
                        wait(act, pv_done[3], st.after(2, R))
                        wait(act, pe_done[name], st.after(2))
                        act.activation(v_sb[:, r, :, :, 0:DH].rearrange("p s h d -> p (s h) d"),
                                       bank.rearrange("p (a d) -> p a d", d=DH), ACT.Copy).then_inc(v_done, 1)

            nc.scalar.preload_act_table_set("natural_log_exp_and_others")
            act.wait_ge(buffers_set, 4)
            run_steps(act, step, FIRST_STEP, LOOP_FIRST, LOOP_STEPS, END_STEP)

        @block.vector
        def _(v):
            def row_moments(st, off, n, tile, ready, reader_done):
                wait(v, *ready)
                for s in range(ST):
                    last = v.bn_stats(stats[:, n, s], tile[:, s])
                last.then_inc(stats_done[n], 1)
                wait(v, reader_done[0], reader_done[1])
                wait(v, stats_done[n], st.after(off))
                wait(v, guard_set[n], st.after(off, 1))
                v.memset(guard[:, n:n + 1], 0.0).then_inc(guard_set[n], 1)
                for s in range(ST):
                    last = v.bn_aggr(moments[:, n, s], stats[:, n, s])
                last.then_inc(moments_done[n], 1)

            def normalise(st, off, n, tile, to, done, free):
                wait(v, *free)
                wait(v, rstd_done[n], st.after(off))
                for s in range(ST):
                    last = v.tensor_scalar(to[:, s], tile[:, s], moments[:, n, s, 0:1], rstd[:, n, s:s + 1],
                                           ALU.subtract, ALU.mult)
                last.then_inc(done, 1)

            def maxima(st, slot):
                h, off = n_head(slot)
                if not st.live(off):
                    return
                if h == 0:
                    wait(v, m_left, st.after(off, R))
                wait(v, n_scores[h % HEAD_SEMS], st.after_head(off, h))
                v.tensor_reduce(neg_max[:, st.slot(off), :, h:h + 1], n_bank[h % 2][:].rearrange("p (s n) -> p s n", s=ST), AX.X,
                                ALU.max, negate=True).then_inc(max_done[h % HEAD_SEMS], 1)

            def hi_part(st, off, full, parts, at, done, out_sem, ready):
                if st.live(off + 1):
                    wait(v, out_sem[st.slot(off + 1)], st.dma_after(off + 1))
                wait(v, ready, st.after(off))
                v.tensor_copy(parts[:, at], full[:]).then_inc(done, 1)

            def take_heads(st, half):
                bank = work[1]
                view = bank[:].rearrange("p (s h e) -> p s h e", s=ST, e=2 * DH)
                wait(v, heads_done[half], st.after(5, 1))
                wait(v, pe_done[f"turn_o{half}"], st.after(5))
                v.reciprocal(den[:, half], view[:, :, :, DH]).then_inc(den_done[half], 1)
                wait(v, o_added[half], st.after(5, 1))
                wait(v, den_done[half], st.after(5))
                v.tensor_tensor(heads[:, half], view[:, :, :, 0:DH],
                                den[:, half].unsqueeze(3).to_broadcast([P, ST, 8, DH]), ALU.mult) \
                    .then_inc(heads_done[half], 1)

            def step(st):
                for slot in range(SLOTS):
                    maxima(st, slot)
                    if slot == 0 and st.live(5):
                        take_heads(st, 0)
                    if slot == 0 and st.live(2):
                        hi_part(st, 2, qT, q_parts, Q_HI, q_hi, q_out, qT_done)
                        wait(v, q_lo, st.after(2, 1))
                        wait(v, q_hi, st.after(2))
                        v.tensor_tensor(q_rest[:], qT[:], q_parts[:, Q_HI], ALU.subtract).then_inc(q_left, 1)
                    if slot == 1 and st.live(2):
                        wait(v, q_left, st.after(2))
                        v.tensor_copy(q_parts[:, Q_MID], q_rest[:]).then_inc(q_mid, 1)
                        wait(v, q_mid, st.after(2))
                        v.tensor_tensor(q_parts[:, Q_LO], q_rest[:], q_parts[:, Q_MID], ALU.subtract) \
                            .then_inc(q_lo, 1)
                    if slot == 2 and st.live(5):
                        take_heads(st, 1)
                    if slot == 4 and st.live(0):
                        wait(v, kv_done, st.after(0, 1))
                        wait(v, spec_done[0], st.after(0))
                        wait(v, spec_done[1], st.after(0))
                        v.tensor_tensor(kv_direct[:], spec[:, 0], spec[:, 1], ALU.mult)
                        v.tensor_tensor(kv_cross[:, :, 0:P], spec[:, 0, :, 0:P], spec[:, 1, :, P:2 * P], ALU.mult)
                        v.tensor_tensor(kv_cross[:, :, P:2 * P], spec[:, 0, :, P:2 * P], spec[:, 1, :, 0:P],
                                        ALU.mult).then_inc(kv_products, 1)
                    if slot == 5 and st.live(0):
                        wait(v, bound_done, st.after(0, 1))
                        wait(v, kv_products, st.after(0))
                        v.tensor_tensor(bins(kv, 0), bins(kv_direct, 0), bins(kv_direct, 1), ALU.subtract)
                        v.tensor_tensor(bins(kv, 1), bins(kv_cross, 0), bins(kv_cross, 1), ALU.add)
                        v.tensor_copy(ends(kv), ends(kv_direct)).then_inc(kv_done, 1)
                    if slot == 7 and st.live(0):
                        for i in range(3):
                            wait(v, sq_done[i], st.after(0))
                        wait(v, log2_done, st.after(0, 1))
                        sq6 = sq[:].rearrange("p i s n -> p (i s) n")
                        mag6 = mag[:].rearrange("p i s n -> p (i s) n")
                        v.scalar_tensor_tensor(mag6[:, :, 1:P], sq6[:, :, 1:P], LN_FLOOR, sq6[:, :, P + 1:2 * P],
                                               ALU.max, ALU.add)
                        v.tensor_scalar(mag6[:, :, 0:P + 1:P], sq6[:, :, 0:P + 1:P], LN_FLOOR, None, ALU.max) \
                            .then_inc(mag_done, 1)
                    if slot == 7 and st.live(1):
                        if st.live(2):
                            wait(v, x1_out[st.slot(2)], st.dma_after(2))
                        wait(v, pe_done["inverse"], st.after(1))
                        v.tensor_tensor(x1[:], x_sb[:, st.slot(1)], work[0][:].rearrange("p (s n) -> p s n", s=ST),
                                        ALU.add).then_inc(x1_done, 1)
                        row_moments(st, 1, 1, x1[:], (x1_done, st.after(1)), (h2_done, st.after(1, 1)))
                    if slot == 8 and st.live(-1):
                        r = st.slot(-1)
                        row_moments(st, -1, 0, x_sb[:, r], (x_in[r], st.dma_after(-1)), (h_done, st.after(-1, 1)))
                    if slot == 9 and st.live(1):
                        normalise(st, 1, 1, x1, h2, h2_done, (pe_done["turn_h2"], st.after(1, 1)))
                    if slot == 11 and st.live(-1):
                        normalise(st, -1, 0, x_sb[:, st.slot(-1)], h_sb, h_done,
                                  (pe_done["turn_h"], st.after(-1, 1)))
                    if slot == 12 and st.live(1):
                        hi_part(st, 1, kT, k_parts, K_HI, k_hi, k_out, kT_done)
                    if slot == 14 and st.live(0):
                        if st.live(1):
                            wait(v, g_done, st.after(0, 1))
                        wait(v, unit_q_done, st.after(0))
                        wait(v, sums_done, st.after(0))
                        v.tensor_tensor(g_direct[:], sums[:], unit_q[:], ALU.mult)
                        v.tensor_tensor(g_cross[:, :, 0:P], sums[:, :, 0:P], unit_q[:, :, P:2 * P], ALU.mult)
                        v.tensor_tensor(g_cross[:, :, P:2 * P], sums[:, :, P:2 * P], unit_q[:, :, 0:P],
                                        ALU.mult).then_inc(g_products, 1)
                    if slot == 15 and st.live(1):
                        wait(v, k_left, st.after(1))
                        v.tensor_copy(k_parts[:, K_MID], k_rest[:]).then_inc(k_mid, 1)
                    if slot == 15 and st.live(0):
                        wait(v, g_products, st.after(0))
                        wait(v, pe_done["turn_g"], st.after(0, 1))
                        v.tensor_tensor(bins(g_sb, 0), bins(g_direct, 0), bins(g_direct, 1), ALU.add)
                        v.tensor_tensor(bins(g_sb, 1), bins(g_cross, 1), bins(g_cross, 0), ALU.subtract)
                        v.tensor_copy(ends(g_sb), ends(g_direct)).then_inc(g_done, 1)

            v.memset(max_parts[:], 0.0).then_inc(buffers_set, 1)
            v.memset(k_stack[KROWS:P].rearrange("p r h n -> p (r h n)"), 1.0).then_inc(buffers_set, 1)
            run_steps(v, step, FIRST_STEP, LOOP_FIRST, LOOP_STEPS, END_STEP)

        @block.gpsimd
        def _(pool):
            def inv_std(st, off, n):
                wait(pool, rstd_done[n], st.after(off, 1))
                wait(pool, moments_done[n], st.after(off))
                pool.tensor_tensor(var_eps[:, n], moments[:, n, :, 1], w.eps[:], ALU.add).then_inc(var_done[n], 1)
                wait(pool, (h_done, h2_done)[n], st.after(off, 1))
                wait(pool, var_done[n], st.after(off))
                pool.tensor_tensor(rstd[:, n], var_eps[:, n], w.half_neg[:], ALU.pow).then_inc(rstd_done[n], 1)

            def scale_spectrum(st, to, a, factors, done):
                both = to[:].rearrange("p s (c n) -> p s c n", c=2)[:, :, :, 1:P]
                wide = factors[:, :, 1:P].unsqueeze(2).to_broadcast([P, ST, 2, P - 1])
                pool.tensor_tensor(both, a.rearrange("p s (c n) -> p s c n", c=2)[:, :, :, 1:P], wide, ALU.mult)
                pool.tensor_tensor(ends(to), ends(a), factors[:, :, 0:P + 1:P], ALU.mult).then_inc(done, 1)

            def step(st):
                for slot in range(SLOTS):
                    if slot in (1, 3) and st.live(5):
                        add_heads(st, slot // 2)
                    if slot in (2, 4, 6) and st.live(0):
                        i = slot // 2 - 1
                        wait(pool, mag_done, st.after(0, 1))
                        wait(pool, spec_done[i], st.after(0))
                        pool.tensor_tensor(sq[:, i], spec[:, i], spec[:, i], ALU.mult).then_inc(sq_done[i], 1)
                    if slot == 7 and st.live(3):
                        wait(pool, pe_done["turn_m"], st.after(3, 1))
                        wait(pool, max_done[-1], st.after_head(3, H - 1))
                        hi, mid, lo = (max_parts[:, :, i * H:(i + 1) * H] for i in range(3))
                        pool.tensor_tensor(hi, neg_max[:, st.slot(3)], zeros[:], ALU.add).then_inc(m_hi, 1)
                        wait(pool, m_hi, st.after(3))
                        pool.tensor_tensor(max_rest[:], neg_max[:, st.slot(3)], hi, ALU.subtract).then_inc(m_left, 1)
                        wait(pool, m_left, st.after(3))
                        pool.tensor_tensor(mid, max_rest[:], zeros[:], ALU.add).then_inc(m_mid, 1)
                        wait(pool, m_mid, st.after(3))
                        pool.tensor_tensor(lo, max_rest[:], mid, ALU.subtract).then_inc(m_lo, 1)
                    if slot == 8 and st.live(1):
                        inv_std(st, 1, 1)
                    if slot == 8 and st.live(-1):
                        inv_std(st, -1, 0)
                    if slot == 9 and st.live(0):
                        wait(pool, log2_done, st.after(0))
                        pool.tensor_tensor(mag2[:, 1], mag2[:, 0], mag2[:, 1], ALU.add).then_inc(log_kv_done, 1)
                    if slot == 10 and st.live(0):
                        wait(pool, pe_done["cumsum"], st.after(0, 1))
                        wait(pool, kv_done, st.after(0))
                        wait(pool, inv_done, st.after(0))
                        scale_spectrum(st, bound, kv, inv[:, 0], bound_done)
                    if slot == 11 and st.live(0):
                        wait(pool, g_products, st.after(0, 1))
                        wait(pool, spec_done[2], st.after(0))
                        scale_spectrum(st, unit_q, spec[:, 2], inv[:, 1], unit_q_done)
                    if slot == 13 and st.live(1):
                        wait(pool, k_lo, st.after(1, 1))
                        wait(pool, k_hi, st.after(1))
                        pool.tensor_tensor(k_rest[:], kT[:], k_parts[:, K_HI], ALU.subtract).then_inc(k_left, 1)
                    if slot == 15 and st.live(1):
                        wait(pool, k_mid, st.after(1))
                        pool.tensor_tensor(k_parts[:, K_LO], k_rest[:], k_parts[:, K_MID], ALU.subtract) \
                            .then_inc(k_lo, 1)

            def add_heads(st, half):
                r = st.slot(5)
                cols = slice(half * P, (half + 1) * P)
                if st.live(6):
                    wait(pool, o_out[st.slot(6)], st.dma_after(6))
                wait(pool, o_set, st.after(5))
                wait(pool, heads_done[half], st.after(5))
                pool.tensor_tensor(o_sb[:, :, cols], q_rows[:, r, :, cols], heads[:, half].rearrange("p s h d -> p s (h d)"), ALU.add) \
                    .then_inc(o_added[half], 1)

            pool.memset(v_sb[:, :, :, :, DH:2 * DH].rearrange("p r s h d -> p (r s h) d"), 1.0).then_inc(buffers_set, 1)
            pool.memset(zeros[:], 0.0).then_inc(buffers_set, 1)
            pool.wait_ge(buffers_set, 4)
            run_steps(pool, step, FIRST_STEP, LOOP_FIRST, LOOP_STEPS, END_STEP)

    nc.all_engine_barrier()
    nc.clear_and_free_semaphores(sems)
    nc.all_engine_barrier()


def feed_forward(nc, w, psum, x1_dram, o_dram, out):
    with ExitStack() as stack:
        def sb(name, shape, dt=F32):
            return stack.enter_context(nc.sbuf_tensor(name, list(shape), dt))

        def sem(name):
            return stack.enter_context(nc.semaphore(name))

        x1 = sb("f_x1", [P, R, ST, D])
        o = sb("f_o", [P, R, ST, D])
        on = sb("f_on", [P, ST, D])
        onT = sb("f_onT", [P, DC, S])
        gelu = sb("f_gelu", [P, ST, D])
        scaled = sb("f_scaled", [P, ST, D])
        scaled_b = sb("f_scaled_b", [P, ST, D])
        o2 = sb("f_o2", [P, ST, D])
        x1b = sb("f_x1b", [P, ST, D])
        centred = sb("f_centred", [P, ST, D])
        x2 = sb("f_x2", [P, R, ST, D])
        h = sb("f_h", [P, ST, D])
        hT = sb("f_hT", [P, DC, S + 2])
        diff = sb("f_diff", [P, DC, S])
        xr = sb("f_xr", [P, DC, S])
        xk = sb("f_xk", [P, DC, S])
        tanh = sb("f_tanh", [P, ST, D])
        relu = sb("f_relu", [P, DC, S])
        k2 = sb("f_k2", [P, DC, S])
        gated = sb("f_gated", [P, ST, D])
        y = sb("f_y", [P, R, ST, D])
        stats = sb("f_stats", [P, 3, ST, 6])
        moments = sb("f_moments", [P, 3, ST, 2])
        guard = sb("f_guard", [P, 3])
        var_eps = sb("f_var_eps", [P, 3, ST])
        rstd = sb("f_rstd", [P, 3, ST])

        v_bank, r_bank, k_bank, on_bank, wo_bank, h_bank = psum[0:6]

        x1_in = [sem(f"f_x1_in{r}") for r in range(R)]
        o_in = [sem(f"f_o_in{r}") for r in range(R)]
        y_out = [sem(f"f_y_out{r}") for r in range(R)]
        pad_set = sem("f_pad_set")
        stats_done = [sem(f"f_stats_done{n}") for n in range(3)]
        moments_done = [sem(f"f_moments_done{n}") for n in range(3)]
        guard_set = [sem(f"f_guard_set{n}") for n in range(3)]
        var_done = [sem(f"f_var_done{n}") for n in range(3)]
        rstd_done = [sem(f"f_rstd_done{n}") for n in range(3)]
        names = ("on_done on_turned onT_done wo_done gelu_done scaled_done scaled_b_done o2_done x1b_done "
                 "centred_done x2_done h_done h_turned hT_done diff_done xr_done xk_done r_done k_done tanh_done "
                 "relu_done k2_done v_done gated_done y_done").split()
        (on_done, on_turned, onT_done, wo_done, gelu_done, scaled_done, scaled_b_done, o2_done, x1b_done,
         centred_done, x2_done, h_done, h_turned, hT_done, diff_done, xr_done, xk_done, r_done, k_done, tanh_done,
         relu_done, k2_done, v_done, gated_done, y_done) = (sem("f_" + name) for name in names)

        FIRST, LOOP, STEPS, END = -1, 7, 24, B + 3
        block = stack.enter_context(nc.Block())

        def wide(row):
            return row.unsqueeze(1).to_broadcast([P, ST, D])

        @block.sync
        def _(sp):
            def step(st):
                if st.live(-1):
                    r = st.slot(-1)
                    wait_all(sp, (scaled_done, st.after(-1, R)))
                    sp.dma_start(o[:, r], rows_of(o_dram, st.batch(-1))).then_inc(o_in[r], 16)
                    wait_all(sp, (x1b_done, st.after(-1, R)))
                    sp.dma_start(x1[:, r], rows_of(x1_dram, st.batch(-1))).then_inc(x1_in[r], 16)
                if st.live(3):
                    r = st.slot(3)
                    wait_all(sp, (y_done, st.after(3)))
                    sp.dma_start(rows_of(out, st.batch(3)), y[:, r]).then_inc(y_out[r], 16)

            run_steps(sp, step, FIRST, LOOP, STEPS, END)
            for r in range(R):
                sp.wait_ge(y_out[r], 16 * len(range(r, B, R)))

        @block.tensor
        def _(pe):
            def turn(bank, source, done):
                for s in range(ST):
                    for c in range(DC):
                        last = pe.transpose(bank[:, c * S + s * P:c * S + (s + 1) * P],
                                            source[:, s, c * P:(c + 1) * P], w.ident[:])
                last.then_inc(done, 1)

            def rows_times(bank, left, right, done, first=True):
                for s in range(ST):
                    for c in range(DC):
                        last = pe.matmul(bank[:, s * D:(s + 1) * D], left[:, c, s * P:(s + 1) * P], right[:, c],
                                         start=(first and s == 0 and c == 0), stop=(c == DC - 1),
                                         skip_group_check=True)
                last.then_inc(done, 1)

            def step(st):
                if st.live(3):
                    wait(pe, gated_done, st.after(3, 1))
                    wait(pe, k2_done, st.after(3))
                    rows_times(v_bank, k2, w.wvf, v_done)
                if st.live(0):
                    wait(pe, onT_done, st.after(0, 1))
                    wait(pe, on_done, st.after(0))
                    turn(on_bank, on, on_turned)
                if st.live(2):
                    wait(pe, tanh_done, st.after(2, 1))
                    wait(pe, xr_done, st.after(2))
                    rows_times(r_bank, xr, w.wr, r_done)
                    wait(pe, relu_done, st.after(2, 1))
                    wait(pe, xk_done, st.after(2))
                    for m in range(DC):
                        for c in range(DC):
                            last = pe.matmul(k_bank[:, m * S:(m + 1) * S], w.wkf[:, c, m * P:(m + 1) * P], xk[:, c],
                                             start=(m == 0 and c == 0), stop=(c == DC - 1), skip_group_check=True)
                    last.then_inc(k_done, 1)
                if st.live(0):
                    wait(pe, gelu_done, st.after(0, 1))
                    wait(pe, onT_done, st.after(0))
                    pe.matmul(wo_bank[:], w.ones[:, 0:P], w.bias[:, B_O].rearrange("p a n -> p (a n)"), start=True,
                              stop=False, skip_group_check=True)
                    rows_times(wo_bank, onT, w.wo, wo_done, first=False)
                if st.live(1):
                    wait(pe, hT_done, st.after(1, 1))
                    wait(pe, h_done, st.after(1))
                    turn(h_bank, h, h_turned)

            run_steps(pe, step, FIRST, LOOP, STEPS, END)

        @block.scalar
        def _(act):
            def flat(a):
                return a.rearrange("p a n -> p (a n)")

            def step(st):
                if st.live(0):
                    wait(act, wo_done, st.after(0, 1))
                    wait(act, on_turned, st.after(0))
                    act.activation(flat(onT[:]), on_bank[:], ACT.Copy).then_inc(onT_done, 1)
                if st.live(2):
                    wait(act, gated_done, st.after(2, 1))
                    wait(act, r_done, st.after(2))
                    act.activation(flat(tanh[:]), r_bank[:], ACT.Tanh, scale=0.5).then_inc(tanh_done, 1)
                    wait(act, k2_done, st.after(2, 1))
                    wait(act, k_done, st.after(2))
                    act.activation(flat(relu[:]), k_bank[:], ACT.Relu).then_inc(relu_done, 1)
                if st.live(0):
                    wait(act, o2_done, st.after(0, 1))
                    wait(act, wo_done, st.after(0))
                    act.activation(flat(gelu[:]), wo_bank[:], ACT.Gelu).then_inc(gelu_done, 1)
                if st.live(1):
                    wait(act, xr_done, st.after(1, 1))
                    wait(act, xk_done, st.after(1, 1))
                    wait(act, h_turned, st.after(1))
                    act.activation(hT[:, :, 2:S + 2], h_bank[:].rearrange("p (c n) -> p c n", c=DC), ACT.Copy) \
                        .then_inc(hT_done, 1)

            nc.scalar.preload_act_table_set("gelu_and_others")
            act.wait_ge(pad_set, 1)
            run_steps(act, step, FIRST, LOOP, STEPS, END)

        @block.vector
        def _(v):
            def row_stats(st, off, n, tile, ready):
                wait(v, *ready)
                for s in range(ST):
                    last = v.bn_stats(stats[:, n, s], tile[:, s])
                last.then_inc(stats_done[n], 1)

            def row_moments(st, off, n, reader_done):
                wait(v, *reader_done)
                wait(v, stats_done[n], st.after(off))
                wait(v, guard_set[n], st.after(off, 1))
                v.memset(guard[:, n:n + 1], 0.0).then_inc(guard_set[n], 1)
                for s in range(ST):
                    last = v.bn_aggr(moments[:, n, s], stats[:, n, s])
                last.then_inc(moments_done[n], 1)

            def normalise(st, off, n, tile, to, done, free):
                wait(v, *free)
                wait(v, rstd_done[n], st.after(off))
                for s in range(ST):
                    last = v.tensor_scalar(to[:, s], tile[:, s], moments[:, n, s, 0:1], rstd[:, n, s:s + 1],
                                           ALU.subtract, ALU.mult)
                last.then_inc(done, 1)

            def step(st):
                r0, r1, r2, r3 = (st.slot(off) for off in range(4))
                if st.live(1):
                    wait(v, centred_done, st.after(1, 1))
                    wait(v, gelu_done, st.after(1))
                    wait(v, scaled_b_done, st.after(1))
                    v.tensor_tensor(o2[:], gelu[:], scaled_b[:], ALU.add).then_inc(o2_done, 1)
                if st.live(0):
                    row_stats(st, 0, 0, o[:, r0], (o_in[r0], st.dma_after(0)))
                if st.live(1):
                    row_stats(st, 1, 1, o2, (o2_done, st.after(1)))
                if st.live(0):
                    row_moments(st, 0, 0, (on_done, st.after(0, 1)))
                if st.live(1):
                    row_moments(st, 1, 1, (x2_done, st.after(1, 1)))
                if st.live(2):
                    wait(v, xk_done, st.after(2, 1))
                    wait(v, hT_done, st.after(2))
                    v.tensor_tensor(diff[:], hT[:, :, 2:S + 2], hT[:, :, 1:S + 1], ALU.subtract) \
                        .then_inc(diff_done, 1)
                if st.live(0):
                    normalise(st, 0, 0, o[:, r0], on, on_done, (scaled_done, st.after(0, 1)))
                if st.live(2):
                    wait(v, r_done, st.after(2, 1))
                    wait(v, k_done, st.after(2, 1))
                    wait(v, diff_done, st.after(2))
                    for to, mu, done in ((xr, w.mu_r, xr_done), (xk, w.mu_k, xk_done)):
                        for c in range(DC):
                            last = v.scalar_tensor_tensor(to[:, c], diff[:, c], mu[:, c:c + 1], hT[:, c, 1:S + 1],
                                                          ALU.mult, ALU.add)
                        last.then_inc(done, 1)
                if st.live(1):
                    wait(v, x2_done, st.after(1, 1))
                    wait(v, moments_done[1], st.after(1))
                    for s in range(ST):
                        last = v.scalar_tensor_tensor(centred[:, s], o2[:, s], moments[:, 1, s, 0:1], w.g1,
                                                      ALU.subtract, ALU.mult)
                    last.then_inc(centred_done, 1)
                if st.live(3):
                    wait(v, y_done, st.after(3, 1))
                    wait(v, tanh_done, st.after(3))
                    wait(v, v_done, st.after(3))
                    v.scalar_tensor_tensor(gated[:].rearrange("p s n -> p (s n)"),
                                           tanh[:].rearrange("p s n -> p (s n)"), 1.0, v_bank[:], ALU.add, ALU.mult) \
                        .then_inc(gated_done, 1)
                if st.live(1):
                    wait(v, x1b_done, st.after(1))
                    wait(v, centred_done, st.after(1))
                    wait(v, y_done, st.after(1, R))
                    wait(v, rstd_done[1], st.after(1))
                    for s in range(ST):
                        last = v.scalar_tensor_tensor(x2[:, r1, s], centred[:, s], rstd[:, 1, s:s + 1], x1b[:, s],
                                                      ALU.mult, ALU.add)
                    last.then_inc(x2_done, 1)
                if st.live(3):
                    wait(v, y_out[r3], st.dma_after(3, lag=1))
                    wait(v, gated_done, st.after(3))
                    v.tensor_tensor(y[:, r3], gated[:], x2[:, r3], ALU.add).then_inc(y_done, 1)
                if st.live(1):
                    row_stats(st, 1, 2, x2[:, r1], (x2_done, st.after(1)))
                    row_moments(st, 1, 2, (h_done, st.after(1, 1)))
                    normalise(st, 1, 2, x2[:, r1], h, h_done, (h_turned, st.after(1, 1)))

            v.memset(hT[:, :, 0:2], 0.0).then_inc(pad_set, 1)
            run_steps(v, step, FIRST, LOOP, STEPS, END)

        @block.gpsimd
        def _(pool):
            def inv_std(st, off, n, reader_done):
                wait(pool, moments_done[n], st.after(off))
                pool.tensor_tensor(var_eps[:, n], moments[:, n, :, 1], w.eps[:], ALU.add).then_inc(var_done[n], 1)
                wait(pool, reader_done, st.after(off, 1))
                wait(pool, var_done[n], st.after(off))
                pool.tensor_tensor(rstd[:, n], var_eps[:, n], w.half_neg[:], ALU.pow).then_inc(rstd_done[n], 1)

            def step(st):
                if st.live(0):
                    inv_std(st, 0, 0, on_done)
                if st.live(1):
                    inv_std(st, 1, 1, x2_done)
                    r = st.slot(1)
                    wait(pool, x2_done, st.after(1, 1))
                    wait(pool, x1_in[r], st.dma_after(1))
                    pool.tensor_tensor(x1b[:], x1[:, r], wide(w.b1), ALU.add).then_inc(x1b_done, 1)
                if st.live(0):
                    wait(pool, scaled_b_done, st.after(0, 1))
                    wait(pool, on_done, st.after(0))
                    pool.tensor_tensor(scaled[:], on[:], wide(w.g0), ALU.mult).then_inc(scaled_done, 1)
                if st.live(1):
                    inv_std(st, 1, 2, h_done)
                if st.live(0):
                    wait(pool, o2_done, st.after(0, 1))
                    wait(pool, scaled_done, st.after(0))
                    pool.tensor_tensor(scaled_b[:], scaled[:], wide(w.b0), ALU.add).then_inc(scaled_b_done, 1)
                if st.live(2):
                    wait(pool, v_done, st.after(2, 1))
                    wait(pool, relu_done, st.after(2))
                    pool.tensor_tensor(k2[:], relu[:], relu[:], ALU.mult).then_inc(k2_done, 1)

            run_steps(pool, step, FIRST, LOOP, STEPS, END)


def rows_of(a, b):
    if isinstance(b, int):
        return a[b].rearrange("(s p) n -> p s n", p=P)
    return a[bass.ds(b, 1)].rearrange("a (s p) n -> p (a s) n", p=P)


def one_of(a, b):
    if isinstance(b, int):
        return a[b]
    return a[bass.ds(b, 1)].rearrange("a p c n -> p (a c) n")


def constants():
    n = np.arange(D)
    angle = 2 * np.pi * np.outer(n, n) / D
    dft = np.concatenate([np.cos(angle[:, :P]), np.cos(angle[:, P:P + 1]), -np.sin(angle[:, 1:P])], axis=1)
    twice = np.where((n == 0) | (n == P), 1.0, 2.0)[:, None] / D
    idft = dft.T * twice
    tri = np.stack([np.triu(np.ones((P, P))), np.ones((P, P))], axis=1)
    masks = np.zeros((P, 4))
    masks[np.arange(3), np.arange(3)] = 1.0
    masks[:, 3] = EPS_UNIT
    return [a.astype(np.float32) for a in (dft, idft, tri, np.eye(P), masks)]


def kernel(**inputs):
    import concourse.bacc as bacc
    from concourse.bass_utils import run_bass_kernel_spmd

    a = {k: np.asarray(v) for k, v in inputs.items()}
    order = np.arange(D).reshape(HP, DC, DH).transpose(1, 2, 0).reshape(-1)
    dft, idft, tri, ident, masks = constants()

    def columns(v):
        return v.reshape(DC, P).T

    arrays = {
        "x": a["x"], "ctx": a["ctx_1024"].transpose(0, 2, 1).reshape(B, DC, P, S).transpose(0, 2, 1, 3),
        "attn_w": np.stack([a["L0_attn_Wk"], a["L0_attn_Wv"], a["L0_attn_Wq"]]),
        "attn_b": np.stack([columns(a[k]) for k in ("L0_attn_bk", "L0_attn_bv", "L0_attn_bq")], axis=1),
        "wq": a["L0_xattn_Wq"][:, order], "wk": a["L0_xattn_Wk"][:, order], "wv": a["L0_xattn_Wv"][order, :],
        "wo": a["L0_xattn_Wo"],
        "rows": np.stack([a["L0_xattn_bq"][order], a["L0_xattn_bk"][order], a["L0_xattn_bv"], a["L0_xattn_bo"],
                          a["L0_xattn_b0"], a["L0_xattn_g1"], a["L0_xattn_b1"], a["L0_xattn_g0"]]),
        "g0c": np.stack([columns(a[k]) for k in ("L0_xattn_g0", "L0_xattn_b0", "L0_ffn_mu_r", "L0_ffn_mu_k")], axis=1),
        "wr_t": a["L0_ffn_W_r"].T, "wk_t": a["L0_ffn_W_k"].T, "wv_t": a["L0_ffn_W_v"].T,
        "dft": dft, "idft": idft, "tri": tri, "ident": ident, "masks": masks,
    }
    arrays = {"in_" + k: np.ascontiguousarray(v) for k, v in arrays.items()}
    nc = bacc.Bacc("TRN2", target_bir_lowering=False, num_devices=1)
    aps = {k[3:]: nc.dram_tensor(k, v.shape, mybir.dt.from_np(v.dtype), kind="ExternalInput").ap()
           for k, v in arrays.items()}
    out = nc.dram_tensor("out_rows", (B, S, D), F32, kind="ExternalOutput").ap()
    decoder_kernel(nc, *(aps[k] for k in ("x", "ctx", "attn_w", "attn_b", "wq", "wk", "wv", "wo", "rows", "g0c",
                                          "wr_t", "wk_t", "wv_t", "dft", "idft", "tri",
                                          "ident", "masks")), out)
    return run_bass_kernel_spmd(nc, [arrays], core_ids=[0]).results[0]["out_rows"]
```

```python
from contextlib import ExitStack

import numpy as np

import concourse.bass as bass
from concourse import mybir

ALU = mybir.AluOpType
ACT = mybir.ActivationFunctionType
AX = mybir.AxisListType
F32 = mybir.dt.float32
BF16 = mybir.dt.bfloat16

P = 128
B = 32
S = 256
D = 256
H = 16
DH = D // H
ST = S // P
DC = D // P
HP = P // DH
SPLITS = 6
KROWS = SPLITS * DH
R = 3
EPS_UNIT = 1e-8
EPS_LN = 1e-5
LN_FLOOR = float(2.0 ** -64)
SOFTMAX_SCALE = float(DH) ** -0.5
NBINS = D // 2 + 1

Q_LO, Q_HI, Q_MID = 0, 1, 2
K_MID, K_HI, K_LO = 0, 1, 2
Q_RUNS = [(0, Q_HI, 2), (2, Q_LO, 2), (4, Q_HI, 2)]
K_RUNS = [(0, K_MID, 2), (2, K_HI, 2), (4, K_HI, 1), (5, K_MID, 1)]

NB = 7
BK_F, BV_F, BQ_F, B_Q, B_K, B_V, B_O = range(NB)

HEAD_SEMS = 8

SLOTS = 16
LAST_OFF = 5
FIRST_STEP = -1
LOOP_FIRST = 7
LOOP_STEPS = 24
END_STEP = B + LAST_OFF


class Shared:
    pass


class Step:

    def __init__(self, t, i=None, batches=B):
        self.t, self.i, self.batches = t, i, batches

    def live(self, off):
        return self.i is not None or 0 <= self.t - off < self.batches

    def past(self, off, lag=1):
        return self.i is not None or self.t - off - lag >= 0

    def batch(self, off):
        return self.t - off if self.i is None else R * self.i + (self.t - off)

    def slot(self, off):
        return (self.t - off) % R

    def after(self, off, lag=0):
        n = self.t - off - lag + 1
        return min(n, self.batches) if self.i is None else R * self.i + n

    def after_head(self, off, h, lag=0):
        n = self.t - off - lag
        if self.i is None:
            return 2 * self.batches if n >= self.batches else 2 * n + h // HEAD_SEMS + 1
        return 2 * R * self.i + 2 * n + h // HEAD_SEMS + 1

    def dma_after(self, off, dmas=1, lag=0):
        n = 16 * dmas * ((self.t - off) // R + 1 - lag)
        return n if self.i is None else 16 * dmas * self.i + n


def in_registers(eng, *values):
    for value in values:
        if not isinstance(value, int):
            eng.to_reg(value)


def run_steps(eng, step, first, loop_first, loop_steps, end, batches=B):
    for t in range(first, loop_first):
        step(Step(t, batches=batches))
    with eng.Fori(0, loop_steps // R) as i:
        for j in range(R):
            step(Step(loop_first + j, i, batches))
    for t in range(loop_first + loop_steps, end):
        step(Step(t, batches=batches))


def decoder_kernel(nc, x, ctx, attn_w, attn_b, wq, wk, wv, wo, rows, g0c, wr_t, wk_t, wv_t, dft, idft, tri,
                   ident, masks, ones_rows, out):
    q_dram = nc.dram_tensor("q_scratch", (R, 3, P, DC * S), BF16)
    k_dram = nc.dram_tensor("k_scratch", (R, 3, P, DC * S), BF16)
    m_dram = nc.dram_tensor("m_scratch", (R, 3, H * S), BF16)
    x1_dram = nc.dram_tensor("x1_rows", (B, S, D), F32)
    o_dram = nc.dram_tensor("o_rows", (B, S, D), F32)

    with ExitStack() as stack:
        def sb(name, shape, dt=F32):
            return stack.enter_context(nc.sbuf_tensor(name, list(shape), dt))

        def sem(name):
            return stack.enter_context(nc.semaphore(name))

        wf = sb("wf", [P, 3, DC, D])
        wq_sb = sb("wq_sb", [P, DC, D])
        wk_sb = sb("wk_sb", [P, DC, D])
        wv_sb = sb("wv_sb", [P, DC, D])
        wo_sb = sb("wo_sb", [P, DC, D])
        wr_sb = sb("wr_sb", [P, DC, D])
        wkf_sb = sb("wkf_sb", [P, DC, D])
        wvf_sb = sb("wvf_sb", [P, DC, D])
        idft_sb = sb("idft_sb", [P, DC, D])
        tri_sb = sb("tri_sb", [P, 2, P])
        id_sb = sb("id_sb", [P, P])
        idb_sb = sb("idb_sb", [P, P], BF16)
        bias_rows = sb("bias_rows", [P, NB, 2, D], BF16)
        ones_bf = sb("ones_bf", [P, S], BF16)
        vec = sb("vec", [P, 3, D])
        g0_row = sb("g0_row", [P, D])
        cols = sb("cols", [P, 4, DC])
        mask_sb = sb("mask_sb", [P, 4])
        eps_sb = sb("eps_sb", [P, ST])
        half_neg = sb("half_neg", [P, ST])
        minus_one = sb("minus_one", [P, ST])

        psum = [stack.enter_context(nc.psum_tensor(f"bank{i}", [P, 512], F32)) for i in range(8)]

        w_in = sem("w_in")
        setup_mm = sem("setup_mm")
        setup_pe = sem("setup_pe")
        setup_v = sem("setup_v")
        setup_g = sem("setup_g")

        with ExitStack() as tmp:
            def tb(name, shape, dt=F32):
                return tmp.enter_context(nc.sbuf_tensor(name, list(shape), dt))

            aw = tb("aw", [P, 3, DC, D])
            ab = tb("ab", [P, 3, DC])
            dft_sb = tb("dft_sb", [P, DC, D])
            bo_row = tb("bo_row", [P, D])
            abw = tb("abw", [P, 3, DC, P])
            b0w = tb("b0w", [P, DC, P])
            full = tb("full", [P, NB, D])
            hi = tb("hi", [P, NB, D], BF16)
            rest = tb("rest", [P, NB, D])
            mid = tb("mid", [P, NB, D], BF16)
            rest2 = tb("rest2", [P, NB, D])
            acc1 = tb("acc1", [P, NB, D])
            acc2 = tb("acc2", [P, NB, D])
            wo_raw = tb("wo_raw", [P, DC, D])
            wv_raw = tb("wv_raw", [P, DC, D])
            N_LOADS = 21

            with nc.Block() as block:
                @block.sync
                def _(sp):
                    def load(dst, src):
                        sp.dma_start(dst, src).then_inc(w_in, 16)

                    for i in range(3):
                        load(aw[:, i], attn_w[i].rearrange("(c p) n -> p c n", p=P))
                    load(ab[:], attn_b)
                    load(dft_sb[:], dft.rearrange("(c p) n -> p c n", p=P))
                    load(idft_sb[:], idft.rearrange("(c p) n -> p c n", p=P))
                    for dst, src in ((wq_sb, wq), (wk_sb, wk), (wv_sb, wv), (wo_raw, wo), (wr_sb, wr_t),
                                     (wkf_sb, wk_t), (wv_raw, wv_t)):
                        load(dst[:], src.rearrange("(c p) n -> p c n", p=P))
                    load(tri_sb[:], tri)
                    load(id_sb[:], ident)
                    load(full[:, B_Q:B_O], rows[0:3].partition_broadcast(P))
                    load(bo_row[:], rows[3].partition_broadcast(P))
                    load(g0_row[:], rows[7].partition_broadcast(P))
                    load(vec[:], rows[4:7].partition_broadcast(P))
                    load(cols[:], g0c)
                    load(mask_sb[:], masks)
                    sp.wait_ge(w_in, 16 * N_LOADS)
                    sp.wait_ge(setup_v, SETUP_V)

                @block.gpsimd
                def _(pool):
                    pool.memset(ones_bf[:], 1.0).then_inc(setup_g, 1)
                    pool.memset(eps_sb[:], EPS_LN).then_inc(setup_g, 1)
                    pool.memset(half_neg[:], -0.5).then_inc(setup_g, 1)
                    pool.memset(minus_one[:], -1.0).then_inc(setup_g, 1)
                    pool.wait_ge(setup_g, 4)

                @block.tensor
                def _(pe):
                    pe.wait_ge(w_in, 16 * N_LOADS)
                    for i in range(3):
                        for c in range(DC):
                            for e in range(DC):
                                last = pe.matmul(psum[i][:, c * D:(c + 1) * D], aw[:, i, e, c * P:(c + 1) * P],
                                                 dft_sb[:, e, :], start=(e == 0), stop=(e == DC - 1))
                        last.then_inc(setup_mm, 1)
                    pe.wait_ge(setup_pe, 1)
                    for i in range(3):
                        for e in range(DC):
                            last = pe.matmul(psum[3 + i][:, 0:D], abw[:, i, e, :], dft_sb[:, e, :],
                                             start=(e == 0), stop=(e == DC - 1))
                        last.then_inc(setup_mm, 1)
                    for e in range(DC):
                        last = pe.matmul(psum[6][:, 0:D], b0w[:, e, :], wo_raw[:, e, :],
                                         start=(e == 0), stop=(e == DC - 1))
                    last.then_inc(setup_mm, 1)

                n_v = [0]

                @block.vector
                def _(v):
                    def chain(ins):
                        n_v[0] += 1
                        ins.then_inc(setup_v, 1)
                        v.wait_ge(setup_v, n_v[0])

                    v.wait_ge(w_in, 16 * N_LOADS)
                    v.wait_ge(setup_g, 4)
                    for i in range(3):
                        for c in range(DC):
                            chain(v.tensor_scalar(abw[:, i, c, :], tri_sb[:, 1, :], ab[:, i, c:c + 1], None, ALU.mult))
                    for c in range(DC):
                        chain(v.tensor_scalar(b0w[:, c, :], tri_sb[:, 1, :], cols[:, 1, c:c + 1], None, ALU.mult))
                    v.tensor_copy(idb_sb[:], id_sb[:]).then_inc(setup_pe, 1)
                    v.wait_ge(setup_pe, 1)
                    for c in range(DC):
                        chain(v.tensor_scalar(wo_sb[:, c, :], wo_raw[:, c, :], cols[:, 0, c:c + 1], None, ALU.mult))
                    chain(v.tensor_scalar(wvf_sb[:], wv_raw[:], 0.5, None, ALU.mult))
                    for i in range(3):
                        v.wait_ge(setup_mm, i + 1)
                        chain(v.tensor_copy(wf[:, i], psum[i][:, :].rearrange("p (c n) -> p c n", c=DC)))

                    for i in range(3):
                        v.wait_ge(setup_mm, 4 + i)
                        chain(v.tensor_copy(full[:, BK_F + i], psum[3 + i][:, 0:D]))
                    v.wait_ge(setup_mm, 7)
                    chain(v.tensor_tensor(full[:, B_O], psum[6][:, 0:D], bo_row[:], ALU.add))
                    chain(v.tensor_copy(hi[:], full[:]))
                    chain(v.tensor_tensor(rest[:], full[:], hi[:], ALU.subtract))
                    chain(v.tensor_copy(mid[:], rest[:]))
                    chain(v.tensor_tensor(rest2[:], rest[:], mid[:], ALU.subtract))
                    chain(v.tensor_scalar(acc1[:], hi[:], mask_sb[:, 0:1], None, ALU.mult))
                    chain(v.scalar_tensor_tensor(acc2[:], mid[:], mask_sb[:, 1:2], acc1[:], ALU.mult, ALU.add))
                    chain(v.scalar_tensor_tensor(bias_rows[:, :, 0], rest2[:], mask_sb[:, 2:3], acc2[:],
                                                 ALU.mult, ALU.add))
                    chain(v.tensor_copy(bias_rows[:, :, 1], bias_rows[:, :, 0]))
                    assert n_v[0] == SETUP_V, n_v[0]

        w = Shared()
        w.wf = wf
        w.wq = wq_sb
        w.wk = wk_sb
        w.wv = wv_sb
        w.wo = wo_sb
        w.wr = wr_sb
        w.wkf = wkf_sb
        w.wvf = wvf_sb
        w.idft = idft_sb
        w.tri = tri_sb
        w.ident = id_sb
        w.ident_bf = idb_sb
        w.bias = bias_rows
        w.ones = ones_bf
        w.g0 = g0_row[:]
        w.b0 = vec[:, 0]
        w.g1 = vec[:, 1]
        w.b1 = vec[:, 2]
        w.mu_r = cols[:, 2]
        w.mu_k = cols[:, 3]
        w.eps_unit = mask_sb[:, 3:4]
        w.eps = eps_sb
        w.half_neg = half_neg
        w.minus_one = minus_one
        attention(nc, w, psum, x, ctx, ones_rows, q_dram, k_dram, m_dram, x1_dram, o_dram)
        feed_forward(nc, w, psum, x1_dram, o_dram, out)


SETUP_V = 6 + 2 + 2 + 1 + 3 + 3 + 1 + 8


PIECES = [(0, "spec_k"), (5, "turn_o1"), (0, "spec_v"), (1, "turn_g"), (0, "spec_q"), (2, "turn_q"), (1, "inverse"),
          (0, None), (2, "proj_v"), (3, "turn_m"), (1, "proj_k"), (1, "turn_h2"), (0, "cumsum"), (-1, "turn_h"),
          (1, "proj_q"), (4, "turn_o0")]
N_FIRST = 8
T_FIRST = 14
PV_SLOT = {3: (0, 4), 7: (1, 4), 11: (2, 4), 15: (3, 4)}
O_OFF = (4, 5)
N_OFF = 2
T_OFF = 3


def n_head(slot):
    return (slot - N_FIRST, N_OFF) if slot >= N_FIRST else (slot - N_FIRST + SLOTS, N_OFF + 1)


def t_head(slot):
    return (slot - T_FIRST, T_OFF) if slot >= T_FIRST else (slot - T_FIRST + SLOTS, T_OFF + 1)


def attention(nc, w, psum, x, ctx, ones_rows, q_dram, k_dram, m_dram, x1_dram, o_dram):
    with ExitStack() as stack:
        def sb(name, shape, dt=F32):
            return stack.enter_context(nc.sbuf_tensor(name, list(shape), dt))

        sems = []

        def sem(name):
            sems.append(nc.alloc_semaphore(name))
            return sems[-1]

        x_sb = sb("x_sb", [P, R, ST, D])
        h_sb = sb("h_sb", [P, ST, D])
        hT = sb("hT", [P, DC, S])
        spec = sb("spec", [P, 3, ST, D])
        sq = sb("sq", [P, 3, ST, D])
        mag = sb("mag", [P, 3, ST, NBINS])
        mag2 = sb("mag2", [P, 3, ST, NBINS])
        inv = sb("inv", [P, 2, ST, NBINS])
        kv_direct = sb("kv_direct", [P, ST, D])
        kv_cross = sb("kv_cross", [P, ST, D])
        kv = sb("kv", [P, ST, D])
        bound = sb("bound", [P, ST, D])
        unit_q = sb("unit_q", [P, ST, D])
        sums = sb("sums", [P, ST, D])
        g_direct = sb("g_direct", [P, ST, D])
        g_cross = sb("g_cross", [P, ST, D])
        g_sb = sb("g_sb", [P, ST, D])
        gT = sb("gT", [P, DC, S])
        x1 = sb("x1", [P, ST, D])
        x1b = sb("x1b", [P, ST, D])
        h2 = sb("h2", [P, ST, D])
        h2T = sb("h2T", [P, DC, S])
        cT = sb("cT", [P, DC, S])
        kT = sb("kT", [P, DC * S])
        qT = sb("qT", [P, DC * S])
        q_parts = sb("q_parts", [P, 3, DC * S], BF16)
        k_parts = sb("k_parts", [P, 3, DC * S], BF16)
        q_rest = sb("q_rest", [P, DC * S])
        k_rest = sb("k_rest", [P, DC * S])
        q_stack = sb("q_stack", [P, R, H, S], BF16)
        k_stack = sb("k_stack", [P, R, H, S], BF16)
        v_sb = sb("v_sb", [P, R, ST, H, 2 * DH])
        neg_max = sb("neg_max", [P, R, ST, H])
        max_rest = sb("max_rest", [P, ST, H])
        max_parts = sb("max_parts", [P, ST, P], BF16)
        mT = sb("mT", [3 * H, ST, P], BF16)
        probs = sb("probs", [P, 8, ST, S])
        oT = sb("oT", [P, 2, 2, S])
        den = sb("den", [P, 2, ST, 8])
        heads = sb("heads", [P, 2, ST, 8, DH])
        q_rows = sb("q_rows", [P, R, ST, D])
        o_sb = sb("o_sb", [P, ST, D])
        stats = sb("stats", [P, 2, ST, 6])
        moments = sb("moments", [P, 2, ST, 2])
        guard = sb("guard", [P, 2])
        var_eps = sb("var_eps", [P, 2, ST])
        rstd = sb("rstd", [P, 2, ST])
        zeros = sb("zeros", [P, ST, H])

        n_bank = psum[0:2]
        t_bank = psum[2:4]
        pv_bank = psum[4:6]
        work = psum[6:8]

        x_in = [sem(f"x_in{r}") for r in range(R)]
        c_in = [sem(f"c_in{r}") for r in range(R)]
        q_out = [sem(f"q_out{r}") for r in range(R)]
        k_out = [sem(f"k_out{r}") for r in range(R)]
        q_in = [sem(f"q_in{r}") for r in range(R)]
        k_in = [sem(f"k_in{r}") for r in range(R)]
        m_out = [sem(f"m_out{r}") for r in range(R)]
        m_in = [sem(f"m_in{r}") for r in range(R)]
        x1_out = [sem(f"x1_out{r}") for r in range(R)]
        o_out = [sem(f"o_out{r}") for r in range(R)]
        buffers_set = sem("buffers_set")
        ones_in = sem("ones_in")
        stats_done = [sem("stats_done0"), sem("stats_done1")]
        moments_done = [sem("moments_done0"), sem("moments_done1")]
        guard_set = [sem("guard_set0"), sem("guard_set1")]
        var_done = [sem("var_done0"), sem("var_done1")]
        rstd_done = [sem("rstd_done0"), sem("rstd_done1")]
        h_done, h2_done = sem("h_done"), sem("h2_done")
        pe_done = {name: sem("pe_" + name) for _, name in PIECES if name}
        hT_done, h2T_done, gT_done = sem("hT_done"), sem("h2T_done"), sem("gT_done")
        spec_done = [sem(f"spec_done{i}") for i in range(3)]
        sq_done = [sem(f"sq_done{i}") for i in range(3)]
        mag_done, log_done, abs_done, log2_done = sem("mag_done"), sem("log_done"), sem("abs_done"), sem("log2_done")
        log_kv_done, inv_done = sem("log_kv_done"), sem("inv_done")
        kv_products, kv_done, bound_done, unit_q_done = (sem("kv_products"), sem("kv_done"), sem("bound_done"),
                                                         sem("unit_q_done"))
        sums_done, g_products, g_done = sem("sums_done"), sem("g_products"), sem("g_done")
        x1_done, x1b_done = sem("x1_done"), sem("x1b_done")
        qT_done, kT_done = sem("qT_done"), sem("kT_done")
        q_hi, q_left, q_mid, q_lo = sem("q_hi"), sem("q_left"), sem("q_mid"), sem("q_lo")
        k_hi, k_left, k_mid, k_lo = sem("k_hi"), sem("k_left"), sem("k_mid"), sem("k_lo")
        v_done = sem("v_done")
        n_scores = [sem(f"n_scores{h}") for h in range(HEAD_SEMS)]
        max_done = [sem(f"max_done{h}") for h in range(HEAD_SEMS)]
        m_hi, m_left, m_mid, m_lo, mT_done = (sem("m_hi"), sem("m_left"), sem("m_mid"), sem("m_lo"),
                                              sem("mT_done"))
        t_scores = [sem(f"t_scores{h}") for h in range(HEAD_SEMS)]
        exp_done = [sem(f"exp_done{h}") for h in range(HEAD_SEMS)]
        pv_done = [sem(f"pv_done{g}") for g in range(4)]
        oT_done = [sem("oT_done0"), sem("oT_done1")]
        o_set = sem("o_set")
        den_done = [sem("den_done0"), sem("den_done1")]
        heads_done = [sem("heads_done0"), sem("heads_done1")]
        o_added = [sem("o_added0"), sem("o_added1")]

        emptied = {"turn_h": hT_done, "turn_q": o_set, "turn_g": gT_done, "spec_k": spec_done[0],
                   "spec_v": spec_done[1], "turn_m": mT_done, "spec_q": spec_done[2], "inverse": x1_done,
                   "turn_o0": heads_done[0], "turn_h2": h2T_done, "proj_k": kT_done,
                   "proj_q": qT_done, "cumsum": sums_done, "turn_o1": heads_done[1], "proj_v": v_done}

        def ends(a):
            return a[:, :, 0:2 * P:P]

        def bins(a, half):
            return a[:, :, half * P + 1:(half + 1) * P]

        block = stack.enter_context(nc.Block())

        @block.sync
        def _(sp):
            def step(st):
                if st.live(2):
                    r = st.slot(2)
                    for parts_done, parts, dram, out_sem, in_sem, to, runs in (
                            (k_lo, k_parts, k_dram, k_out, k_in, k_stack, K_RUNS),
                            (q_lo, q_parts, q_dram, q_out, q_in, q_stack, Q_RUNS)):
                        in_registers(sp, st.after(2, R), st.after(2), st.dma_after(2, dmas=len(runs), lag=1))
                        if st.past(2, R):
                            sp.wait_ge(pv_done[-1], st.after(2, R))
                        sp.wait_ge(parts_done, st.after(2))
                        if st.past(2, R):
                            sp.wait_ge(in_sem[r], st.dma_after(2, dmas=len(runs), lag=1))
                        sp.dma_start(dram[r].rearrange("s p n -> p s n"), parts[:]).then_inc(out_sem[r], 16)
                        in_registers(sp, st.dma_after(2))
                        sp.wait_ge(out_sem[r], st.dma_after(2))
                        for group, part, n in runs:
                            sp.dma_start(to[DH * group:DH * (group + n), r].rearrange("p h n -> p (h n)"),
                                         dram[r, part:part + n].rearrange("s (d h) n -> (s d) (h n)", h=HP)) \
                                .then_inc(in_sem[r], 16)
                if st.live(2):
                    in_registers(sp, st.after(2))
                    sp.wait_ge(x1b_done, st.after(2))
                    sp.dma_start(rows_of(x1_dram, st.batch(2)), x1b[:]).then_inc(x1_out[st.slot(2)], 16)
                if st.live(-1):
                    in_registers(sp, st.after(-1, R))
                    if st.past(-1, R):
                        sp.wait_ge(x1_done, st.after(-1, R))
                    r = st.slot(-1)
                    sp.dma_start(x_sb[:, r], rows_of(x, st.batch(-1))).then_inc(x_in[r], 16)
                if st.live(5):
                    in_registers(sp, st.after(5), st.after(5))
                    sp.wait_ge(o_added[0], st.after(5))
                    sp.wait_ge(o_added[1], st.after(5))
                    sp.dma_start(rows_of(o_dram, st.batch(5)), o_sb[:]).then_inc(o_out[st.slot(5)], 16)
                if st.live(3):
                    r = st.slot(3)
                    in_registers(sp, st.after(3), st.dma_after(3, lag=1))
                    sp.wait_ge(mT_done, st.after(3))
                    if st.past(3, R):
                        sp.wait_ge(m_in[r], st.dma_after(3, lag=1))
                    sp.dma_start(m_dram[r].rearrange("s (h n) -> (s h) n", n=S), mT[:].rearrange("p a b -> p (a b)")) \
                        .then_inc(m_out[r], 16)
                    in_registers(sp, st.dma_after(3), st.after(3, R))
                    sp.wait_ge(m_out[r], st.dma_after(3))
                    if st.past(3, R):
                        sp.wait_ge(pv_done[-1], st.after(3, R))
                    sp.dma_start(q_stack[KROWS:KROWS + 3, r].rearrange("p h n -> p (h n)"), m_dram[r]) \
                        .then_inc(m_in[r], 16)
                if st.live(0):
                    in_registers(sp, st.after(0, 1))
                    if st.past(0):
                        sp.wait_ge(pe_done["proj_k"], st.after(0, 1))
                    sp.dma_start(cT[:], one_of(ctx, st.batch(0))).then_inc(c_in[st.slot(0)], 16)

            sp.dma_start(k_stack[KROWS:KROWS + 3].rearrange("p r h n -> p (r h n)"), ones_rows).then_inc(ones_in, 16)
            run_steps(sp, step, FIRST_STEP, LOOP_FIRST, LOOP_STEPS, END_STEP)
            for r in range(R):
                n = 16 * len(range(r, B, R))
                sp.wait_ge(x1_out[r], n)
                sp.wait_ge(o_out[r], n)
                sp.wait_ge(m_out[r], n)
                sp.wait_ge(k_out[r], n)
                sp.wait_ge(q_out[r], n)

        @block.tensor
        def _(pe):
            def bank_free(st, slot):
                for back in range(2, SLOTS + 1, 2):
                    before = Step(st.t - (slot < back), st.i)
                    off, name = PIECES[(slot - back) % SLOTS]
                    if name and before.live(off):
                        pe.wait_ge(emptied[name], before.after(off))
                        return

            def turn(bank, source, name):
                for s in range(ST):
                    for c in range(DC):
                        last = pe.transpose(bank[:, c * S + s * P:c * S + (s + 1) * P],
                                            source[:, s, c * P:(c + 1) * P], w.ident[:])
                last.then_inc(pe_done[name], 1)

            def rows_times(bank, left, right, name, bias=None):
                if bias is not None:
                    pe.matmul(bank[:], w.ones[:, 0:P], w.bias[:, bias].rearrange("p a n -> p (a n)"), start=True,
                              stop=False, skip_group_check=True)
                for s in range(ST):
                    for c in range(DC):
                        last = pe.matmul(bank[:, s * D:(s + 1) * D], left[:, c, s * P:(s + 1) * P], right[:, c],
                                         start=(bias is None and s == 0 and c == 0), stop=(c == DC - 1),
                                         skip_group_check=True)
                last.then_inc(pe_done[name], 1)

            def turned_times(bank, right, weight, name, bias):
                for m in range(DC):
                    pe.matmul(bank[:, m * S:(m + 1) * S], w.bias[:, bias, 0, m * P:(m + 1) * P], w.ones[:],
                              start=(m == 0), stop=False, skip_group_check=True)
                    for c in range(DC):
                        last = pe.matmul(bank[:, m * S:(m + 1) * S], weight[:, c, m * P:(m + 1) * P], right[:, c],
                                         start=False, stop=(c == DC - 1), skip_group_check=True)
                last.then_inc(pe_done[name], 1)

            def piece(st, slot):
                off, name = PIECES[slot]
                if name is None or not st.live(off):
                    return
                bank = work[slot % 2]
                bank_free(st, slot)
                if name == "turn_h":
                    pe.wait_ge(h_done, st.after(-1))
                    turn(bank, h_sb, name)
                elif name == "turn_q":
                    pe.wait_ge(qT_done, st.after(2))
                    for s in range(ST):
                        for c in range(DC):
                            last = pe.transpose(bank[:, s * D + c * P:s * D + (c + 1) * P],
                                                qT[:, c * S + s * P:c * S + (s + 1) * P], w.ident[:])
                    last.then_inc(pe_done[name], 1)
                elif name == "turn_g":
                    pe.wait_ge(g_done, st.after(1))
                    turn(bank, g_sb, name)
                elif name in ("spec_k", "spec_v", "spec_q"):
                    i = ("spec_k", "spec_v", "spec_q").index(name)
                    pe.wait_ge(hT_done, st.after(0))
                    rows_times(bank, hT, w.wf[:, i], name, BK_F + i)
                elif name == "turn_m":
                    pe.wait_ge(m_lo, st.after(3))
                    to = bank[:].bitcast(BF16)
                    for s in range(ST):
                        last = pe.transpose(to[:, s * P:(s + 1) * P], max_parts[:, s], w.ident_bf[:])
                    last.then_inc(pe_done[name], 1)
                elif name == "inverse":
                    pe.wait_ge(gT_done, st.after(1))
                    rows_times(bank, gT, w.idft, name)
                elif name in ("turn_o0", "turn_o1"):
                    half = int(name[-1])
                    pe.wait_ge(oT_done[half], st.after(off))
                    for s in range(ST):
                        for g in range(2):
                            last = pe.transpose(bank[:, s * 2 * P + g * P:s * 2 * P + (g + 1) * P],
                                                oT[:, half, g, s * P:(s + 1) * P], w.ident[:])
                    last.then_inc(pe_done[name], 1)
                elif name == "turn_h2":
                    pe.wait_ge(h2_done, st.after(1))
                    turn(bank, h2, name)
                elif name == "proj_k":
                    pe.wait_ge(c_in[st.slot(1)], st.dma_after(1))
                    turned_times(bank, cT, w.wk, name, B_K)
                elif name == "proj_q":
                    pe.wait_ge(h2T_done, st.after(1))
                    turned_times(bank, h2T, w.wq, name, B_Q)
                elif name == "proj_v":
                    pe.wait_ge(kT_done, st.after(2))
                    rows_times(bank, kT[:].rearrange("p (c n) -> p c n", c=DC), w.wv, name, B_V)
                elif name == "cumsum":
                    pe.wait_ge(bound_done, st.after(0))
                    pe.matmul(bank[:, 0:D], w.tri[:, 0], bound[:, 0], start=True, stop=True, skip_group_check=True)
                    pe.matmul(bank[:, D:2 * D], w.tri[:, 1], bound[:, 0], start=False, stop=False,
                              skip_group_check=True)
                    pe.matmul(bank[:, D:2 * D], w.tri[:, 0], bound[:, 1], start=False, stop=True,
                              skip_group_check=True).then_inc(pe_done[name], 1)

            def max_scores(st, slot):
                h, off = n_head(slot)
                if not st.live(off):
                    return
                r = st.slot(off)
                if h == 0:
                    pe.wait_ge(q_in[r], st.dma_after(off, dmas=len(Q_RUNS)))
                    pe.wait_ge(k_in[r], st.dma_after(off, dmas=len(K_RUNS)))
                if h >= 2 or st.past(off):
                    pe.wait_ge(max_done[(h - 2) % HEAD_SEMS], st.after_head(off, (h - 2) % H, int(h < 2)))
                for s in range(ST):
                    last = pe.matmul(n_bank[h % 2][:, s * S:(s + 1) * S], q_stack[0:KROWS, r, h, s * P:(s + 1) * P],
                                     k_stack[0:KROWS, r, h], start=True, stop=True, skip_group_check=True)
                last.then_inc(n_scores[h % HEAD_SEMS], 1)

            def exp_scores(st, slot):
                h, off = t_head(slot)
                if not st.live(off):
                    return
                r = st.slot(off)
                if h == 0:
                    pe.wait_ge(m_in[r], st.dma_after(off))
                if h >= 2 or st.past(off):
                    pe.wait_ge(exp_done[(h - 2) % HEAD_SEMS], st.after_head(off, (h - 2) % H, int(h < 2)))
                for s in range(ST):
                    last = pe.matmul(t_bank[h % 2][:, s * S:(s + 1) * S], k_stack[0:KROWS + 3, r, h, s * P:(s + 1) * P],
                                     q_stack[0:KROWS + 3, r, h], start=True, stop=True, skip_group_check=True)
                last.then_inc(t_scores[h % HEAD_SEMS], 1)

            def attend(st, slot):
                if slot not in PV_SLOT:
                    return
                g, off = PV_SLOT[slot]
                if not st.live(off):
                    return
                if g == 0:
                    pe.wait_ge(v_done, st.after(off))
                if g % 2 == 0:
                    if st.past(off):
                        pe.wait_ge(oT_done[g // 2], st.after(off, 1))
                pe.wait_ge(exp_done[(4 * g + 3) % HEAD_SEMS], st.after_head(off, 4 * g + 3))
                for s in range(ST):
                    for j in range(4):
                        h = 4 * g + j
                        last = pe.matmul(pv_bank[g // 2][32 * j:32 * j + 32, (g % 2) * S:(g % 2 + 1) * S],
                                         v_sb[:, st.slot(off), s, h], probs[:, h % 8, s], start=(s == 0),
                                         stop=(s == ST - 1), skip_group_check=True)
                last.then_inc(pv_done[g], 1)

            def step(st):
                for slot in range(SLOTS):
                    max_scores(st, slot)
                    exp_scores(st, slot)
                    attend(st, slot)
                    piece(st, slot)

            pe.wait_ge(buffers_set, 3)
            pe.wait_ge(ones_in, 16)
            run_steps(pe, step, FIRST_STEP, LOOP_FIRST, LOOP_STEPS, END_STEP)

        @block.scalar
        def _(act):
            def exps(st, slot):
                h, off = t_head(slot)
                if not st.live(off):
                    return
                if h >= 8 or st.past(off):
                    act.wait_ge(pv_done[(h - 8) % H // 4], st.after(off, int(h < 8)))
                act.wait_ge(t_scores[h % HEAD_SEMS], st.after_head(off, h))
                act.activation(probs[:, h % 8].rearrange("p s n -> p (s n)"), t_bank[h % 2][:], ACT.Exp,
                               scale=SOFTMAX_SCALE).then_inc(exp_done[h % HEAD_SEMS], 1)

            def flat(a):
                return a.rearrange("p a n -> p (a n)")

            def step(st):
                for slot in range(SLOTS):
                    bank = work[slot % 2][:]
                    exps(st, slot)
                    off, name = PIECES[slot]
                    if slot in (0, 8):
                        half = 0 if slot == 8 else 1
                        at = O_OFF[half]
                        if st.live(at):
                            if st.past(at):
                                act.wait_ge(pe_done[f"turn_o{half}"], st.after(at, 1))
                            act.wait_ge(pv_done[2 * half + 1], st.after(at))
                            act.activation(flat(oT[:, half]), pv_bank[half][:], ACT.Copy).then_inc(oT_done[half], 1)
                    if slot == 7 and st.live(0):
                        if st.past(0):
                            act.wait_ge(inv_done, st.after(0, 1))
                        act.wait_ge(mag_done, st.after(0))
                        act.activation(mag2[:], mag[:], ACT.Ln).then_inc(log_done, 1)
                    if slot == 8 and st.live(0):
                        act.wait_ge(log_done, st.after(0))
                        act.activation(mag[:], mag2[:], ACT.Exp, scale=0.5).then_inc(abs_done, 1)
                        act.wait_ge(abs_done, st.after(0))
                        act.activation(mag2[:], mag[:], ACT.Ln, bias=w.eps_unit).then_inc(log2_done, 1)
                    if slot == 9 and st.live(0):
                        if st.past(0):
                            act.wait_ge(bound_done, st.after(0, 1))
                        if st.past(0):
                            act.wait_ge(unit_q_done, st.after(0, 1))
                        act.wait_ge(log_kv_done, st.after(0))
                        act.activation(inv[:], mag2[:, 1:3], ACT.Exp, scale=-1.0).then_inc(inv_done, 1)
                    if name is None or not st.live(off):
                        continue
                    if name == "turn_h":
                        if st.past(-1):
                            act.wait_ge(pe_done["spec_q"], st.after(-1, 1))
                        act.wait_ge(pe_done[name], st.after(-1))
                        act.activation(flat(hT[:]), bank, ACT.Copy).then_inc(hT_done, 1)
                    elif name == "turn_q":
                        r = st.slot(2)
                        if st.past(2, R):
                            act.wait_ge(o_added[1], st.after(2, R))
                        act.wait_ge(pe_done[name], st.after(2))
                        for s in range(ST):
                            to = q_rows[:, r, s].rearrange("p (h c d) -> p c d h", c=DC, d=DH)
                            last = act.activation(to, work[slot % 2][:, s * D:(s + 1) * D]
                                                  .rearrange("p (c d h) -> p c d h", c=DC, d=DH), ACT.Copy)
                        last.then_inc(o_set, 1)
                    elif name == "turn_g":
                        if st.past(1):
                            act.wait_ge(pe_done["inverse"], st.after(1, 1))
                        act.wait_ge(pe_done[name], st.after(1))
                        act.activation(flat(gT[:]), bank, ACT.Copy).then_inc(gT_done, 1)
                    elif name in ("spec_k", "spec_v", "spec_q"):
                        i = ("spec_k", "spec_v", "spec_q").index(name)
                        if st.past(0):
                            act.wait_ge(sq_done[i], st.after(0, 1))
                        if st.past(0):
                            act.wait_ge(unit_q_done if i == 2 else kv_products, st.after(0, 1))
                        act.wait_ge(pe_done[name], st.after(0))
                        act.activation(flat(spec[:, i]), bank, ACT.Copy).then_inc(spec_done[i], 1)
                    elif name == "turn_m":
                        if st.live(4):
                            act.wait_ge(m_out[st.slot(4)], st.dma_after(4))
                        act.wait_ge(pe_done[name], st.after(3))
                        act.activation(flat(mT[:]), work[slot % 2][0:3 * H].bitcast(BF16)[:, 0:2 * P], ACT.Copy) \
                            .then_inc(mT_done, 1)
                    elif name == "turn_h2":
                        if st.past(1):
                            act.wait_ge(pe_done["proj_q"], st.after(1, 1))
                        act.wait_ge(pe_done[name], st.after(1))
                        act.activation(flat(h2T[:]), bank, ACT.Copy).then_inc(h2T_done, 1)
                    elif name == "proj_k":
                        if st.past(1):
                            act.wait_ge(k_left, st.after(1, 1))
                        if st.past(1):
                            act.wait_ge(pe_done["proj_v"], st.after(1, 1))
                        act.wait_ge(pe_done[name], st.after(1))
                        act.activation(kT[:], bank, ACT.Copy).then_inc(kT_done, 1)
                    elif name == "proj_q":
                        if st.past(1):
                            act.wait_ge(q_left, st.after(1, 1))
                        if st.past(1):
                            act.wait_ge(pe_done["turn_q"], st.after(1, 1))
                        act.wait_ge(pe_done[name], st.after(1))
                        act.activation(qT[:], bank, ACT.Copy).then_inc(qT_done, 1)
                    elif name == "cumsum":
                        if st.past(0):
                            act.wait_ge(g_products, st.after(0, 1))
                        act.wait_ge(pe_done[name], st.after(0))
                        act.activation(flat(sums[:]), bank, ACT.Copy).then_inc(sums_done, 1)
                    elif name == "proj_v":
                        r = st.slot(2)
                        if st.past(2, R):
                            act.wait_ge(pv_done[3], st.after(2, R))
                        act.wait_ge(pe_done[name], st.after(2))
                        act.activation(v_sb[:, r, :, :, 0:DH].rearrange("p s h d -> p (s h) d"),
                                       bank.rearrange("p (a d) -> p a d", d=DH), ACT.Copy).then_inc(v_done, 1)

            nc.scalar.preload_act_table_set("natural_log_exp_and_others")
            act.wait_ge(buffers_set, 3)
            run_steps(act, step, FIRST_STEP, LOOP_FIRST, LOOP_STEPS, END_STEP)

        @block.vector
        def _(v):
            def row_moments(st, off, n, tile, reader_done):
                if st.past(off):
                    v.wait_ge(moments_done[n], st.after(off, 1))
                for s in range(ST):
                    last = v.bn_stats(stats[:, n, s], tile[:, s])
                last.then_inc(stats_done[n], 1)
                if st.past(off):
                    v.wait_ge(reader_done, st.after(off, 1))
                v.wait_ge(stats_done[n], st.after(off))
                if st.past(off):
                    v.wait_ge(guard_set[n], st.after(off, 1))
                v.memset(guard[:, n:n + 1], 0.0).then_inc(guard_set[n], 1)
                for s in range(ST):
                    last = v.bn_aggr(moments[:, n, s], stats[:, n, s])
                last.then_inc(moments_done[n], 1)

            def normalise(st, off, n, tile, to, done):
                v.wait_ge(rstd_done[n], st.after(off))
                for s in range(ST):
                    last = v.tensor_scalar(to[:, s], tile[:, s], moments[:, n, s, 0:1], rstd[:, n, s:s + 1],
                                           ALU.subtract, ALU.mult)
                last.then_inc(done, 1)

            def maxima(st, slot):
                h, off = n_head(slot)
                if not st.live(off):
                    return
                if h == 0:
                    if st.past(off, R):
                        v.wait_ge(m_left, st.after(off, R))
                v.wait_ge(n_scores[h % HEAD_SEMS], st.after_head(off, h))
                v.tensor_reduce(neg_max[:, st.slot(off), :, h:h + 1], n_bank[h % 2][:].rearrange("p (s n) -> p s n", s=ST), AX.X,
                                ALU.max, negate=True).then_inc(max_done[h % HEAD_SEMS], 1)

            def hi_part(st, off, full, parts, at, done, out_sem, ready):
                if st.live(off + 1):
                    v.wait_ge(out_sem[st.slot(off + 1)], st.dma_after(off + 1))
                v.wait_ge(ready, st.after(off))
                v.tensor_copy(parts[:, at], full[:]).then_inc(done, 1)

            def take_heads(st, half):
                bank = work[1]
                view = bank[:].rearrange("p (s h e) -> p s h e", s=ST, e=2 * DH)
                if st.past(5):
                    v.wait_ge(heads_done[half], st.after(5, 1))
                v.wait_ge(pe_done[f"turn_o{half}"], st.after(5))
                v.reciprocal(den[:, half], view[:, :, :, DH]).then_inc(den_done[half], 1)
                if st.past(5):
                    v.wait_ge(o_added[half], st.after(5, 1))
                v.wait_ge(den_done[half], st.after(5))
                v.tensor_tensor(heads[:, half], view[:, :, :, 0:DH],
                                den[:, half].unsqueeze(3).to_broadcast([P, ST, 8, DH]), ALU.mult) \
                    .then_inc(heads_done[half], 1)

            def step(st):
                for slot in range(SLOTS):
                    maxima(st, slot)
                    if slot == 0 and st.live(5):
                        take_heads(st, 0)
                    if slot == 0 and st.live(2):
                        hi_part(st, 2, qT, q_parts, Q_HI, q_hi, q_out, qT_done)
                        if st.past(2):
                            v.wait_ge(q_lo, st.after(2, 1))
                        v.wait_ge(q_hi, st.after(2))
                        v.tensor_tensor(q_rest[:], qT[:], q_parts[:, Q_HI], ALU.subtract).then_inc(q_left, 1)
                    if slot == 1 and st.live(2):
                        v.wait_ge(q_left, st.after(2))
                        v.tensor_copy(q_parts[:, Q_MID], q_rest[:]).then_inc(q_mid, 1)
                        v.wait_ge(q_mid, st.after(2))
                        v.tensor_tensor(q_parts[:, Q_LO], q_rest[:], q_parts[:, Q_MID], ALU.subtract) \
                            .then_inc(q_lo, 1)
                    if slot == 2 and st.live(5):
                        take_heads(st, 1)
                    if slot == 4 and st.live(0):
                        if st.past(0):
                            v.wait_ge(kv_done, st.after(0, 1))
                        v.wait_ge(spec_done[0], st.after(0))
                        v.wait_ge(spec_done[1], st.after(0))
                        v.tensor_tensor(kv_direct[:], spec[:, 0], spec[:, 1], ALU.mult)
                        v.tensor_tensor(kv_cross[:, :, 0:P], spec[:, 0, :, 0:P], spec[:, 1, :, P:2 * P], ALU.mult)
                        v.tensor_tensor(kv_cross[:, :, P:2 * P], spec[:, 0, :, P:2 * P], spec[:, 1, :, 0:P],
                                        ALU.mult).then_inc(kv_products, 1)
                    if slot == 5 and st.live(0):
                        if st.past(0):
                            v.wait_ge(bound_done, st.after(0, 1))
                        v.wait_ge(kv_products, st.after(0))
                        v.tensor_tensor(bins(kv, 0), bins(kv_direct, 0), bins(kv_direct, 1), ALU.subtract)
                        v.tensor_tensor(bins(kv, 1), bins(kv_cross, 0), bins(kv_cross, 1), ALU.add)
                        v.tensor_copy(ends(kv), ends(kv_direct)).then_inc(kv_done, 1)
                    if slot == 6 and st.live(0):
                        for i in range(3):
                            v.wait_ge(sq_done[i], st.after(0))
                        if st.past(0):
                            v.wait_ge(log2_done, st.after(0, 1))
                        sq6 = sq[:].rearrange("p i s n -> p (i s) n")
                        mag6 = mag[:].rearrange("p i s n -> p (i s) n")
                        v.scalar_tensor_tensor(mag6[:, :, 1:P], sq6[:, :, 1:P], LN_FLOOR, sq6[:, :, P + 1:2 * P],
                                               ALU.max, ALU.add)
                        v.tensor_scalar(mag6[:, :, 0:P + 1:P], sq6[:, :, 0:P + 1:P], LN_FLOOR, None, ALU.max) \
                            .then_inc(mag_done, 1)
                    if slot == 7 and st.live(1):
                        if st.past(1):
                            v.wait_ge(x1b_done, st.after(1, 1))
                        v.wait_ge(pe_done["inverse"], st.after(1))
                        v.tensor_tensor(x1[:], x_sb[:, st.slot(1)], work[0][:].rearrange("p (s n) -> p s n", s=ST),
                                        ALU.add).then_inc(x1_done, 1)
                        v.wait_ge(x1_done, st.after(1))
                        row_moments(st, 1, 1, x1[:], h2_done)
                    if slot == 8 and st.live(-1):
                        r = st.slot(-1)
                        v.wait_ge(x_in[r], st.dma_after(-1))
                        row_moments(st, -1, 0, x_sb[:, r], h_done)
                    if slot == 9 and st.live(1):
                        if st.past(1):
                            v.wait_ge(pe_done["turn_h2"], st.after(1, 1))
                        normalise(st, 1, 1, x1, h2, h2_done)
                    if slot == 11 and st.live(-1):
                        if st.past(-1):
                            v.wait_ge(pe_done["turn_h"], st.after(-1, 1))
                        normalise(st, -1, 0, x_sb[:, st.slot(-1)], h_sb, h_done)
                    if slot == 12 and st.live(1):
                        hi_part(st, 1, kT, k_parts, K_HI, k_hi, k_out, kT_done)
                    if slot == 14 and st.live(0):
                        if st.live(1):
                            if st.past(0):
                                v.wait_ge(g_done, st.after(0, 1))
                        v.wait_ge(unit_q_done, st.after(0))
                        v.wait_ge(sums_done, st.after(0))
                        v.tensor_tensor(g_direct[:], sums[:], unit_q[:], ALU.mult)
                        v.tensor_tensor(g_cross[:, :, 0:P], sums[:, :, 0:P], unit_q[:, :, P:2 * P], ALU.mult)
                        v.tensor_tensor(g_cross[:, :, P:2 * P], sums[:, :, P:2 * P], unit_q[:, :, 0:P],
                                        ALU.mult).then_inc(g_products, 1)
                    if slot == 15 and st.live(1):
                        v.wait_ge(k_left, st.after(1))
                        v.tensor_copy(k_parts[:, K_MID], k_rest[:]).then_inc(k_mid, 1)
                    if slot == 15 and st.live(0):
                        v.wait_ge(g_products, st.after(0))
                        if st.past(0):
                            v.wait_ge(pe_done["turn_g"], st.after(0, 1))
                        v.tensor_tensor(bins(g_sb, 0), bins(g_direct, 0), bins(g_direct, 1), ALU.add)
                        v.tensor_tensor(bins(g_sb, 1), bins(g_cross, 1), bins(g_cross, 0), ALU.subtract)
                        v.tensor_copy(ends(g_sb), ends(g_direct)).then_inc(g_done, 1)

            v.memset(max_parts[:], 0.0).then_inc(buffers_set, 1)
            run_steps(v, step, FIRST_STEP, LOOP_FIRST, LOOP_STEPS, END_STEP)

        @block.gpsimd
        def _(pool):
            def inv_std(st, off, n):
                if st.past(off):
                    pool.wait_ge(rstd_done[n], st.after(off, 1))
                pool.wait_ge(moments_done[n], st.after(off))
                pool.tensor_tensor(var_eps[:, n], moments[:, n, :, 1], w.eps[:], ALU.add).then_inc(var_done[n], 1)
                if st.past(off):
                    pool.wait_ge((h_done, h2_done)[n], st.after(off, 1))
                pool.wait_ge(var_done[n], st.after(off))
                pool.tensor_tensor(rstd[:, n], var_eps[:, n], w.half_neg[:], ALU.pow).then_inc(rstd_done[n], 1)

            def scale_spectrum(st, to, a, factors, done):
                both = to[:].rearrange("p s (c n) -> p s c n", c=2)[:, :, :, 1:P]
                wide = factors[:, :, 1:P].unsqueeze(2).to_broadcast([P, ST, 2, P - 1])
                pool.tensor_tensor(both, a.rearrange("p s (c n) -> p s c n", c=2)[:, :, :, 1:P], wide, ALU.mult)
                pool.tensor_tensor(ends(to), ends(a), factors[:, :, 0:P + 1:P], ALU.mult).then_inc(done, 1)

            def step(st):
                for slot in range(SLOTS):
                    if slot in (1, 3) and st.live(5):
                        add_heads(st, slot // 2)
                    if slot in (2, 4, 6) and st.live(0):
                        i = slot // 2 - 1
                        if st.past(0):
                            pool.wait_ge(mag_done, st.after(0, 1))
                        pool.wait_ge(spec_done[i], st.after(0))
                        pool.tensor_tensor(sq[:, i], spec[:, i], spec[:, i], ALU.mult).then_inc(sq_done[i], 1)
                    if slot == 8 and st.live(3):
                        if st.past(3):
                            pool.wait_ge(pe_done["turn_m"], st.after(3, 1))
                        pool.wait_ge(max_done[-1], st.after_head(3, H - 1))
                        hi, mid, lo = (max_parts[:, :, i * H:(i + 1) * H] for i in range(3))
                        pool.tensor_tensor(hi, neg_max[:, st.slot(3)], zeros[:], ALU.add).then_inc(m_hi, 1)
                        pool.wait_ge(m_hi, st.after(3))
                        pool.tensor_tensor(max_rest[:], neg_max[:, st.slot(3)], hi, ALU.subtract).then_inc(m_left, 1)
                        pool.wait_ge(m_left, st.after(3))
                        pool.tensor_tensor(mid, max_rest[:], zeros[:], ALU.add).then_inc(m_mid, 1)
                        pool.wait_ge(m_mid, st.after(3))
                        pool.tensor_tensor(lo, max_rest[:], mid, ALU.subtract).then_inc(m_lo, 1)
                    if slot == 8 and st.live(1):
                        inv_std(st, 1, 1)
                    if slot == 8 and st.live(-1):
                        inv_std(st, -1, 0)
                    if slot == 9 and st.live(0):
                        pool.wait_ge(log2_done, st.after(0))
                        pool.tensor_tensor(mag2[:, 1], mag2[:, 0], mag2[:, 1], ALU.add).then_inc(log_kv_done, 1)
                    if slot == 10 and st.live(0):
                        if st.past(0):
                            pool.wait_ge(pe_done["cumsum"], st.after(0, 1))
                        pool.wait_ge(kv_done, st.after(0))
                        pool.wait_ge(inv_done, st.after(0))
                        scale_spectrum(st, bound, kv, inv[:, 0], bound_done)
                    if slot == 11 and st.live(0):
                        if st.past(0):
                            pool.wait_ge(g_products, st.after(0, 1))
                        pool.wait_ge(spec_done[2], st.after(0))
                        scale_spectrum(st, unit_q, spec[:, 2], inv[:, 1], unit_q_done)
                    if slot == 12 and st.live(1):
                        if st.live(2):
                            pool.wait_ge(x1_out[st.slot(2)], st.dma_after(2))
                        pool.wait_ge(x1_done, st.after(1))
                        pool.tensor_tensor(x1b[:], x1[:], w.b1.unsqueeze(1).to_broadcast([P, ST, D]), ALU.add) \
                            .then_inc(x1b_done, 1)
                    if slot == 13 and st.live(1):
                        if st.past(1):
                            pool.wait_ge(k_lo, st.after(1, 1))
                        pool.wait_ge(k_hi, st.after(1))
                        pool.tensor_tensor(k_rest[:], kT[:], k_parts[:, K_HI], ALU.subtract).then_inc(k_left, 1)
                    if slot == 15 and st.live(1):
                        pool.wait_ge(k_mid, st.after(1))
                        pool.tensor_tensor(k_parts[:, K_LO], k_rest[:], k_parts[:, K_MID], ALU.subtract) \
                            .then_inc(k_lo, 1)

            def add_heads(st, half):
                r = st.slot(5)
                cols = slice(half * P, (half + 1) * P)
                if st.live(6):
                    pool.wait_ge(o_out[st.slot(6)], st.dma_after(6))
                pool.wait_ge(o_set, st.after(5))
                pool.wait_ge(heads_done[half], st.after(5))
                pool.tensor_tensor(o_sb[:, :, cols], q_rows[:, r, :, cols], heads[:, half].rearrange("p s h d -> p s (h d)"), ALU.add) \
                    .then_inc(o_added[half], 1)

            pool.memset(v_sb[:, :, :, :, DH:2 * DH].rearrange("p r s h d -> p (r s h) d"), 1.0).then_inc(buffers_set, 1)
            pool.memset(zeros[:], 0.0).then_inc(buffers_set, 1)
            pool.wait_ge(buffers_set, 3)
            run_steps(pool, step, FIRST_STEP, LOOP_FIRST, LOOP_STEPS, END_STEP)

    nc.all_engine_barrier()
    nc.clear_and_free_semaphores(sems)
    nc.all_engine_barrier()


def feed_forward(nc, w, psum, x1_dram, o_dram, out):
    with ExitStack() as stack:
        def sb(name, shape, dt=F32):
            return stack.enter_context(nc.sbuf_tensor(name, list(shape), dt))

        def sem(name):
            return stack.enter_context(nc.semaphore(name))

        x1b = sb("f_x1b", [P, R, ST, D])
        o = sb("f_o", [P, R, ST, D])
        on = sb("f_on", [P, ST, D])
        onT = sb("f_onT", [P, DC, S])
        gelu = sb("f_gelu", [P, ST, D])
        scaled = sb("f_scaled", [P, ST, D])
        scaled_b = sb("f_scaled_b", [P, ST, D])
        o2 = sb("f_o2", [P, ST, D])
        centred = sb("f_centred", [P, ST, D])
        x2 = sb("f_x2", [P, R, ST, D])
        h = sb("f_h", [P, ST, D])
        hT = sb("f_hT", [P, DC, S + 2])
        diff = sb("f_diff", [P, DC, S])
        xr = sb("f_xr", [P, DC, S])
        xk = sb("f_xk", [P, DC, S])
        tanh = sb("f_tanh", [P, ST, D])
        relu = sb("f_relu", [P, DC, S])
        k2 = sb("f_k2", [P, DC, S])
        gated = sb("f_gated", [P, ST, D])
        y = sb("f_y", [P, R, ST, D])
        stats = sb("f_stats", [P, 3, ST, 6])
        moments = sb("f_moments", [P, 3, ST, 2])
        guard = sb("f_guard", [P, 3])
        var_eps = sb("f_var_eps", [P, 3, ST])
        rstd = sb("f_rstd", [P, 3, ST])
        neg_mean = sb("f_neg_mean", [P, 3, ST])
        shift = sb("f_shift", [P, 3, ST])

        v_bank, r_bank, k_bank, on_bank, wo_bank, h_bank = psum[0:6]

        x1b_in = [sem(f"f_x1_in{r}") for r in range(R)]
        o_in = [sem(f"f_o_in{r}") for r in range(R)]
        y_out = [sem(f"f_y_out{r}") for r in range(R)]
        pad_set = sem("f_pad_set")
        stats_done = [sem(f"f_stats_done{n}") for n in range(3)]
        moments_done = [sem(f"f_moments_done{n}") for n in range(3)]
        guard_set = [sem(f"f_guard_set{n}") for n in range(3)]
        var_done = [sem(f"f_var_done{n}") for n in range(3)]
        rstd_done = [sem(f"f_rstd_done{n}") for n in range(3)]
        neg_mean_done = [sem(f"f_neg_mean_done{n}") for n in range(3)]
        shift_done = [sem(f"f_shift_done{n}") for n in range(3)]
        names = ("on_done on_turned onT_done wo_done gelu_done scaled_done scaled_b_done o2_done "
                 "centred_done x2_done h_done h_turned hT_done diff_done xr_done xk_done r_done k_done tanh_done "
                 "relu_done k2_done v_done gated_done y_done").split()
        (on_done, on_turned, onT_done, wo_done, gelu_done, scaled_done, scaled_b_done, o2_done,
         centred_done, x2_done, h_done, h_turned, hT_done, diff_done, xr_done, xk_done, r_done, k_done, tanh_done,
         relu_done, k2_done, v_done, gated_done, y_done) = (sem("f_" + name) for name in names)

        FIRST, LOOP, STEPS, END = -1, 5, 24, B + 4
        block = stack.enter_context(nc.Block())

        def wide(row):
            return row.unsqueeze(1).to_broadcast([P, ST, D])

        @block.sync
        def _(sp):
            def step(st):
                if st.live(-1):
                    r = st.slot(-1)
                    in_registers(sp, st.after(-1, R))
                    if st.past(-1, R):
                        sp.wait_ge(on_done, st.after(-1, R))
                    sp.dma_start(o[:, r], rows_of(o_dram, st.batch(-1))).then_inc(o_in[r], 16)
                if st.live(0):
                    r = st.slot(0)
                    in_registers(sp, st.after(0, R))
                    if st.past(0, R):
                        sp.wait_ge(x2_done, st.after(0, R))
                    sp.dma_start(x1b[:, r], rows_of(x1_dram, st.batch(0))).then_inc(x1b_in[r], 16)
                if st.live(4):
                    r = st.slot(4)
                    in_registers(sp, st.after(4))
                    sp.wait_ge(y_done, st.after(4))
                    sp.dma_start(rows_of(out, st.batch(4)), y[:, r]).then_inc(y_out[r], 16)

            run_steps(sp, step, FIRST, LOOP, STEPS, END)
            for r in range(R):
                sp.wait_ge(y_out[r], 16 * len(range(r, B, R)))

        @block.tensor
        def _(pe):
            def turn(bank, source, done):
                for s in range(ST):
                    for c in range(DC):
                        last = pe.transpose(bank[:, c * S + s * P:c * S + (s + 1) * P],
                                            source[:, s, c * P:(c + 1) * P], w.ident[:])
                last.then_inc(done, 1)

            def rows_times(bank, left, right, done, first=True):
                for s in range(ST):
                    for c in range(DC):
                        last = pe.matmul(bank[:, s * D:(s + 1) * D], left[:, c, s * P:(s + 1) * P], right[:, c],
                                         start=(first and s == 0 and c == 0), stop=(c == DC - 1),
                                         skip_group_check=True)
                last.then_inc(done, 1)

            def step(st):
                if st.live(3):
                    if st.past(3):
                        pe.wait_ge(hT_done, st.after(3, 1))
                    pe.wait_ge(h_done, st.after(3))
                    turn(h_bank, h, h_turned)
                if st.live(1):
                    if st.past(1):
                        pe.wait_ge(gelu_done, st.after(1, 1))
                    pe.wait_ge(onT_done, st.after(1))
                    pe.matmul(wo_bank[:], w.ones[:, 0:P], w.bias[:, B_O].rearrange("p a n -> p (a n)"), start=True,
                              stop=False, skip_group_check=True)
                    rows_times(wo_bank, onT, w.wo, wo_done, first=False)
                if st.live(4):
                    if st.past(4):
                        pe.wait_ge(gated_done, st.after(4, 1))
                    pe.wait_ge(k2_done, st.after(4))
                    rows_times(v_bank, k2, w.wvf, v_done)
                if st.live(3):
                    if st.past(3):
                        pe.wait_ge(relu_done, st.after(3, 1))
                    pe.wait_ge(xk_done, st.after(3))
                    for m in range(DC):
                        for c in range(DC):
                            last = pe.matmul(k_bank[:, m * S:(m + 1) * S], w.wkf[:, c, m * P:(m + 1) * P], xk[:, c],
                                             start=(m == 0 and c == 0), stop=(c == DC - 1), skip_group_check=True)
                    last.then_inc(k_done, 1)
                if st.live(0):
                    if st.past(0):
                        pe.wait_ge(onT_done, st.after(0, 1))
                    pe.wait_ge(on_done, st.after(0))
                    turn(on_bank, on, on_turned)
                if st.live(3):
                    if st.past(3):
                        pe.wait_ge(tanh_done, st.after(3, 1))
                    pe.wait_ge(xr_done, st.after(3))
                    rows_times(r_bank, xr, w.wr, r_done)

            run_steps(pe, step, FIRST, LOOP, STEPS, END)

        @block.scalar
        def _(act):
            def flat(a):
                return a.rearrange("p a n -> p (a n)")

            def normalise(st, off, n, tile, to, done):
                act.wait_ge(shift_done[n], st.after(off))
                for s in range(ST):
                    last = act.activation(to[:, s], tile[:, s], ACT.Identity, bias=shift[:, n, s:s + 1],
                                          scale=rstd[:, n, s:s + 1])
                last.then_inc(done, 1)

            def step(st):
                if st.live(3):
                    if st.past(3):
                        act.wait_ge(xr_done, st.after(3, 1))
                    if st.past(3):
                        act.wait_ge(xk_done, st.after(3, 1))
                    act.wait_ge(h_turned, st.after(3))
                    act.activation(hT[:, :, 2:S + 2], h_bank[:].rearrange("p (c n) -> p c n", c=DC), ACT.Copy) \
                        .then_inc(hT_done, 1)
                if st.live(4):
                    if st.past(4):
                        act.wait_ge(gated_done, st.after(4, 1))
                    act.wait_ge(r_done, st.after(4))
                    act.activation(flat(tanh[:]), r_bank[:], ACT.Tanh, scale=0.5).then_inc(tanh_done, 1)
                if st.live(1):
                    if st.past(1):
                        act.wait_ge(o2_done, st.after(1, 1))
                    act.wait_ge(wo_done, st.after(1))
                    act.activation(flat(gelu[:]), wo_bank[:], ACT.Gelu).then_inc(gelu_done, 1)
                if st.live(0):
                    if st.past(0):
                        act.wait_ge(on_turned, st.after(0, 1))
                    if st.past(0):
                        act.wait_ge(scaled_done, st.after(0, 1))
                    normalise(st, 0, 0, o[:, st.slot(0)], on, on_done)
                if st.live(2):
                    if st.past(2):
                        act.wait_ge(h_turned, st.after(2, 1))
                    normalise(st, 2, 2, x2[:, st.slot(2)], h, h_done)
                if st.live(3):
                    if st.past(3):
                        act.wait_ge(k2_done, st.after(3, 1))
                    act.wait_ge(k_done, st.after(3))
                    act.activation(flat(relu[:]), k_bank[:], ACT.Relu).then_inc(relu_done, 1)
                if st.live(0):
                    if st.past(0):
                        act.wait_ge(wo_done, st.after(0, 1))
                    act.wait_ge(on_turned, st.after(0))
                    act.activation(flat(onT[:]), on_bank[:], ACT.Copy).then_inc(onT_done, 1)
                if st.live(3):
                    if st.past(3):
                        act.wait_ge(v_done, st.after(3, 1))
                    act.wait_ge(relu_done, st.after(3))
                    act.activation(k2[:], relu[:], ACT.Square).then_inc(k2_done, 1)

            nc.scalar.preload_act_table_set("gelu_and_others")
            act.wait_ge(pad_set, 1)
            run_steps(act, step, FIRST, LOOP, STEPS, END)

        @block.vector
        def _(v):
            def row_stats(st, off, n, tile):
                if st.past(off):
                    v.wait_ge(moments_done[n], st.after(off, 1))
                for s in range(ST):
                    last = v.bn_stats(stats[:, n, s], tile[:, s])
                last.then_inc(stats_done[n], 1)

            def row_moments(st, off, n, reader_done):
                if st.past(off):
                    v.wait_ge(reader_done, st.after(off, 1))
                v.wait_ge(stats_done[n], st.after(off))
                if st.past(off):
                    v.wait_ge(guard_set[n], st.after(off, 1))
                v.memset(guard[:, n:n + 1], 0.0).then_inc(guard_set[n], 1)
                for s in range(ST):
                    last = v.bn_aggr(moments[:, n, s], stats[:, n, s])
                last.then_inc(moments_done[n], 1)

            def token_mix(st, to, mu, done, reader_done):
                if st.past(3):
                    v.wait_ge(reader_done, st.after(3, 1))
                v.wait_ge(diff_done, st.after(3))
                for c in range(DC):
                    last = v.scalar_tensor_tensor(to[:, c], diff[:, c], mu[:, c:c + 1], hT[:, c, 1:S + 1],
                                                  ALU.mult, ALU.add)
                last.then_inc(done, 1)

            def step(st):
                if st.live(2):
                    if st.past(2):
                        v.wait_ge(x2_done, st.after(2, 1))
                    v.wait_ge(moments_done[1], st.after(2))
                    for s in range(ST):
                        last = v.scalar_tensor_tensor(centred[:, s], o2[:, s], moments[:, 1, s, 0:1], w.g1,
                                                      ALU.subtract, ALU.mult)
                    last.then_inc(centred_done, 1)
                if st.live(0):
                    r = st.slot(0)
                    v.wait_ge(o_in[r], st.dma_after(0))
                    row_stats(st, 0, 0, o[:, r])
                if st.live(2):
                    r = st.slot(2)
                    v.wait_ge(x1b_in[r], st.dma_after(2))
                    if st.past(2, R):
                        v.wait_ge(y_done, st.after(2, R))
                    v.wait_ge(rstd_done[1], st.after(2))
                    v.wait_ge(centred_done, st.after(2))
                    for s in range(ST):
                        last = v.scalar_tensor_tensor(x2[:, r, s], centred[:, s], rstd[:, 1, s:s + 1], x1b[:, r, s],
                                                      ALU.mult, ALU.add)
                    last.then_inc(x2_done, 1)
                if st.live(0):
                    row_moments(st, 0, 0, on_done)
                if st.live(2):
                    v.wait_ge(x2_done, st.after(2))
                    row_stats(st, 2, 2, x2[:, st.slot(2)])
                if st.live(2):
                    row_moments(st, 2, 2, h_done)
                if st.live(3):
                    token_mix(st, xk, w.mu_k, xk_done, k_done)
                if st.live(1):
                    if st.past(1):
                        v.wait_ge(centred_done, st.after(1, 1))
                    v.wait_ge(gelu_done, st.after(1))
                    v.wait_ge(scaled_b_done, st.after(1))
                    v.tensor_tensor(o2[:], gelu[:], scaled_b[:], ALU.add).then_inc(o2_done, 1)
                if st.live(3):
                    token_mix(st, xr, w.mu_r, xr_done, r_done)
                if st.live(1):
                    v.wait_ge(o2_done, st.after(1))
                    row_stats(st, 1, 1, o2)
                if st.live(4):
                    if st.past(4):
                        v.wait_ge(y_done, st.after(4, 1))
                    v.wait_ge(tanh_done, st.after(4))
                    v.wait_ge(v_done, st.after(4))
                    v.scalar_tensor_tensor(gated[:].rearrange("p s n -> p (s n)"),
                                           tanh[:].rearrange("p s n -> p (s n)"), 1.0, v_bank[:], ALU.add, ALU.mult) \
                        .then_inc(gated_done, 1)
                if st.live(1):
                    row_moments(st, 1, 1, x2_done)
                if st.live(4):
                    r = st.slot(4)
                    if st.past(4, R):
                        v.wait_ge(y_out[r], st.dma_after(4, lag=1))
                    v.wait_ge(gated_done, st.after(4))
                    v.tensor_tensor(y[:, r], gated[:], x2[:, r], ALU.add).then_inc(y_done, 1)

            v.memset(hT[:, :, 0:2], 0.0).then_inc(pad_set, 1)
            run_steps(v, step, FIRST, LOOP, STEPS, END)

        @block.gpsimd
        def _(pool):
            def inv_std(st, off, n, reader_done):
                pool.wait_ge(moments_done[n], st.after(off))
                pool.tensor_tensor(var_eps[:, n], moments[:, n, :, 1], w.eps[:], ALU.add).then_inc(var_done[n], 1)
                if n != 1:
                    pool.tensor_tensor(neg_mean[:, n], moments[:, n, :, 0], w.minus_one[:], ALU.mult) \
                        .then_inc(neg_mean_done[n], 1)
                if st.past(off):
                    pool.wait_ge(reader_done, st.after(off, 1))
                pool.wait_ge(var_done[n], st.after(off))
                pool.tensor_tensor(rstd[:, n], var_eps[:, n], w.half_neg[:], ALU.pow).then_inc(rstd_done[n], 1)
                if n != 1:
                    pool.wait_ge(rstd_done[n], st.after(off))
                    pool.wait_ge(neg_mean_done[n], st.after(off))
                    pool.tensor_tensor(shift[:, n], neg_mean[:, n], rstd[:, n], ALU.mult).then_inc(shift_done[n], 1)

            def step(st):
                if st.live(1):
                    if st.past(1):
                        pool.wait_ge(o2_done, st.after(1, 1))
                    pool.wait_ge(scaled_done, st.after(1))
                    pool.tensor_tensor(scaled_b[:], scaled[:], wide(w.b0), ALU.add).then_inc(scaled_b_done, 1)
                if st.live(3):
                    if st.past(3):
                        pool.wait_ge(xr_done, st.after(3, 1))
                    pool.wait_ge(hT_done, st.after(3))
                    pool.tensor_tensor(diff[:], hT[:, :, 2:S + 2], hT[:, :, 1:S + 1], ALU.subtract) \
                        .then_inc(diff_done, 1)
                if st.live(0):
                    inv_std(st, 0, 0, on_done)
                if st.live(2):
                    inv_std(st, 2, 2, h_done)
                if st.live(0):
                    if st.past(0):
                        pool.wait_ge(scaled_b_done, st.after(0, 1))
                    pool.wait_ge(on_done, st.after(0))
                    pool.tensor_tensor(scaled[:], on[:], wide(w.g0), ALU.mult).then_inc(scaled_done, 1)
                if st.live(1):
                    inv_std(st, 1, 1, x2_done)

            run_steps(pool, step, FIRST, LOOP, STEPS, END)


def rows_of(a, b):
    if isinstance(b, int):
        return a[b].rearrange("(s p) n -> p s n", p=P)
    return a[bass.ds(b, 1)].rearrange("a (s p) n -> p (a s) n", p=P)


def one_of(a, b):
    if isinstance(b, int):
        return a[b]
    return a[bass.ds(b, 1)].rearrange("a p c n -> p (a c) n")


def constants():
    n = np.arange(D)
    angle = 2 * np.pi * np.outer(n, n) / D
    dft = np.concatenate([np.cos(angle[:, :P]), np.cos(angle[:, P:P + 1]), -np.sin(angle[:, 1:P])], axis=1)
    twice = np.where((n == 0) | (n == P), 1.0, 2.0)[:, None] / D
    idft = dft.T * twice
    tri = np.stack([np.triu(np.ones((P, P))), np.ones((P, P))], axis=1)
    masks = np.zeros((P, 4))
    masks[np.arange(3), np.arange(3)] = 1.0
    masks[:, 3] = EPS_UNIT
    return [a.astype(np.float32) for a in (dft, idft, tri, np.eye(P), masks)]


def kernel(**inputs):
    import concourse.bacc as bacc
    from concourse.bass_utils import run_bass_kernel_spmd

    a = {k: np.asarray(v) for k, v in inputs.items()}
    order = np.arange(D).reshape(HP, DC, DH).transpose(1, 2, 0).reshape(-1)
    dft, idft, tri, ident, masks = constants()

    def columns(v):
        return v.reshape(DC, P).T

    arrays = {
        "x": a["x"], "ctx": a["ctx_1024"].transpose(0, 2, 1).reshape(B, DC, P, S).transpose(0, 2, 1, 3),
        "attn_w": np.stack([a["L0_attn_Wk"], a["L0_attn_Wv"], a["L0_attn_Wq"]]),
        "attn_b": np.stack([columns(a[k]) for k in ("L0_attn_bk", "L0_attn_bv", "L0_attn_bq")], axis=1),
        "wq": a["L0_xattn_Wq"][:, order], "wk": a["L0_xattn_Wk"][:, order], "wv": a["L0_xattn_Wv"][order, :],
        "wo": a["L0_xattn_Wo"],
        "rows": np.stack([a["L0_xattn_bq"][order], a["L0_xattn_bk"][order], a["L0_xattn_bv"], a["L0_xattn_bo"],
                          a["L0_xattn_b0"], a["L0_xattn_g1"], a["L0_xattn_b1"], a["L0_xattn_g0"]]),
        "g0c": np.stack([columns(a[k]) for k in ("L0_xattn_g0", "L0_xattn_b0", "L0_ffn_mu_r", "L0_ffn_mu_k")], axis=1),
        "wr_t": a["L0_ffn_W_r"].T, "wk_t": a["L0_ffn_W_k"].T, "wv_t": a["L0_ffn_W_v"].T,
        "dft": dft, "idft": idft, "tri": tri, "ident": ident, "masks": masks,
        "ones_rows": np.ones((3, R * H * S), mybir.dt.np(BF16)),
    }
    arrays = {"in_" + k: np.ascontiguousarray(v) for k, v in arrays.items()}
    nc = bacc.Bacc("TRN2", target_bir_lowering=False, num_devices=1)
    aps = {k[3:]: nc.dram_tensor(k, v.shape, mybir.dt.from_np(v.dtype), kind="ExternalInput").ap()
           for k, v in arrays.items()}
    out = nc.dram_tensor("out_rows", (B, S, D), F32, kind="ExternalOutput").ap()
    decoder_kernel(nc, *(aps[k] for k in ("x", "ctx", "attn_w", "attn_b", "wq", "wk", "wv", "wo", "rows", "g0c",
                                          "wr_t", "wk_t", "wv_t", "dft", "idft", "tri",
                                          "ident", "masks", "ones_rows")), out)
    return run_bass_kernel_spmd(nc, [arrays], core_ids=[0]).results[0]["out_rows"]
```

```python
from contextlib import ExitStack

import numpy as np

import concourse.bass as bass
from concourse import mybir

ALU = mybir.AluOpType
ACT = mybir.ActivationFunctionType
AX = mybir.AxisListType
F32 = mybir.dt.float32
F32R = mybir.dt.float32r
BF16 = mybir.dt.bfloat16

P = 128
B = 32
S = 256
D = 256
H = 16
DH = D // H
ST = S // P
DC = D // P
HP = P // DH
SPLITS = 6
KROWS = SPLITS * DH
R = 3
EPS_UNIT = 1e-8
EPS_LN = 1e-5
LN_FLOOR = float(2.0 ** -64)
SOFTMAX_SCALE = float(DH) ** -0.5
NBINS = D // 2 + 1

Q_LO, Q_HI, Q_MID = 0, 1, 2
K_MID, K_HI, K_LO = 0, 1, 2
Q_RUNS = [(0, Q_HI, 2), (2, Q_LO, 2), (4, Q_HI, 2)]
K_RUNS = [(0, K_MID, 2), (2, K_HI, 2), (4, K_HI, 1), (5, K_MID, 1)]

NB = 5
BK_F, BV_F, BQ_F, B_V, B_O = range(NB)
PARTS_AT = (0, 32, 64)

HEAD_SEMS = 8

SLOTS = 16
LAST_OFF = 5
FIRST_STEP = -1
LOOP_FIRST = 7
LOOP_STEPS = 24
END_STEP = B + LAST_OFF


class Shared:
    pass


class Step:

    def __init__(self, t, i=None, batches=B):
        self.t, self.i, self.batches = t, i, batches

    def live(self, off):
        return self.i is not None or 0 <= self.t - off < self.batches

    def past(self, off, lag=1):
        return self.i is not None or self.t - off - lag >= 0

    def batch(self, off):
        return self.t - off if self.i is None else R * self.i + (self.t - off)

    def slot(self, off):
        return (self.t - off) % R

    def after(self, off, lag=0):
        n = self.t - off - lag + 1
        return min(n, self.batches) if self.i is None else R * self.i + n

    def after_head(self, off, h, lag=0):
        n = self.t - off - lag
        if self.i is None:
            return 2 * self.batches if n >= self.batches else 2 * n + h // HEAD_SEMS + 1
        return 2 * R * self.i + 2 * n + h // HEAD_SEMS + 1

    def dma_after(self, off, dmas=1, lag=0):
        n = 16 * dmas * ((self.t - off) // R + 1 - lag)
        return n if self.i is None else 16 * dmas * self.i + n


def in_registers(eng, *values):
    for value in values:
        if not isinstance(value, int):
            eng.to_reg(value)


def run_steps(eng, step, first, loop_first, loop_steps, end, batches=B):
    for t in range(first, loop_first):
        step(Step(t, batches=batches))
    with eng.Fori(0, loop_steps // R) as i:
        for j in range(R):
            step(Step(loop_first + j, i, batches))
    for t in range(loop_first + loop_steps, end):
        step(Step(t, batches=batches))


def decoder_kernel(nc, x, ctx, attn_w, attn_b, wq, wk, wv, wo, rows, columns, wr_t, wk_t, wv_t, dft, idft, tri,
                   ident, picks, ones_rows, out):
    q_dram = nc.dram_tensor("q_scratch", (R, 3, P, DC * S), BF16)
    k_dram = nc.dram_tensor("k_scratch", (R, 3, P, DC * S), BF16)
    m_dram = nc.dram_tensor("m_scratch", (R, 3, H * S), BF16)
    x1_dram = nc.dram_tensor("x1_rows", (B, S, D), F32)
    o_dram = nc.dram_tensor("o_rows", (B, S, D), F32)

    with ExitStack() as stack:
        def sb(name, shape, dt=F32):
            return stack.enter_context(nc.sbuf_tensor(name, list(shape), dt))

        def sem(name):
            return stack.enter_context(nc.semaphore(name))

        wf = sb("wf", [P, 2, 3, DC, D], F32R)
        wq_sb = sb("wq_sb", [P, 2, DC, D], F32R)
        wk_sb = sb("wk_sb", [P, DC, D])
        wv_sb = sb("wv_sb", [P, DC, D])
        wo_sb = sb("wo_sb", [P, DC, D])
        idft_sb = sb("idft_sb", [P, 2, DC, D], F32R)
        tri_sb = sb("tri_sb", [P, 2, P])
        id_sb = sb("id_sb", [P, P])
        idb_sb = sb("idb_sb", [P, P], BF16)
        bias_rows = sb("bias_rows", [P, NB, D], BF16)
        picks_sb = sb("picks_sb", [P, P], BF16)
        vec = sb("vec", [P, 4, D])
        cols = sb("cols", [P, 6, DC])
        unit_eps = sb("unit_eps", [P, 1])
        eps_sb = sb("eps_sb", [P, ST])
        half_neg = sb("half_neg", [P, ST])
        minus_one = sb("minus_one", [P, ST])

        psum = [stack.enter_context(nc.psum_tensor(f"bank{i}", [P, 512], F32)) for i in range(8)]

        first_in = sem("first_in")
        w_in = sem("w_in")
        setup_mm = sem("setup_mm")
        setup_v = sem("setup_v")
        setup_g = sem("setup_g")

        with ExitStack() as tmp:
            def tb(name, shape, dt=F32):
                return tmp.enter_context(nc.sbuf_tensor(name, list(shape), dt))

            aw = tb("aw", [P, 3, DC, D])
            ab = tb("ab", [P, 3, DC])
            dft_sb = tb("dft_sb", [P, DC, D])
            bo_row = tb("bo_row", [P, D])
            abw = tb("abw", [P, 3, DC, P])
            b0w = tb("b0w", [P, DC, P])
            full = tb("full", [P, NB, D])
            hi = tb("hi", [P, NB, D], BF16)
            rest = tb("rest", [P, NB, D])
            mid = tb("mid", [P, NB, D], BF16)
            wf_raw = tb("wf_raw", [P, 3, DC, D])
            wq_raw = tb("wq_raw", [P, DC, D])
            idft_raw = tb("idft_raw", [P, DC, D])
            wo_raw = tb("wo_raw", [P, DC, D])
            N_FIRST_LOADS, N_LOADS = 7, 17

            with nc.Block() as block:
                @block.sync
                def _(sp):
                    loads = [0]

                    def load(dst, src):
                        loads[0] += 1
                        sp.dma_start(dst, src).then_inc(first_in if loads[0] <= N_FIRST_LOADS else w_in, 16)

                    def load_weight(dst, src):
                        load(dst, src.rearrange("(c p) n -> p c n", p=P))

                    load(ab[:], attn_b)
                    load(cols[:], columns)
                    load(tri_sb[:], tri)
                    load_weight(dft_sb[:], dft)
                    for i in range(3):
                        load_weight(aw[:, i], attn_w[i])
                    load_weight(wo_raw[:], wo)
                    load(bo_row[:], rows[1].partition_broadcast(P))
                    load(full[:, B_V], rows[0].partition_broadcast(P))
                    load(id_sb[:], ident)
                    for dst, src in ((wq_raw, wq), (wk_sb, wk), (wv_sb, wv), (idft_raw, idft)):
                        load_weight(dst[:], src)
                    load(vec[:], rows[2:6].partition_broadcast(P))
                    load(picks_sb[:], picks)
                    assert loads[0] == N_LOADS, loads
                    sp.wait_ge(w_in, 16 * (N_LOADS - N_FIRST_LOADS))
                    sp.wait_ge(setup_v, SETUP_V)

                @block.gpsimd
                def _(pool):
                    pool.memset(eps_sb[:], EPS_LN).then_inc(setup_g, 1)
                    pool.memset(half_neg[:], -0.5).then_inc(setup_g, 1)
                    pool.memset(minus_one[:], -1.0).then_inc(setup_g, 1)
                    pool.memset(unit_eps[:], EPS_UNIT).then_inc(setup_g, 1)
                    pool.wait_ge(setup_g, 4)
                    pool.memset(bias_rows[96:P], 0.0).then_inc(setup_g, 1)
                    pool.wait_ge(setup_g, 5)

                @block.tensor
                def _(pe):
                    pe.wait_ge(first_in, 16 * N_FIRST_LOADS)
                    for i in range(3):
                        for c in range(DC):
                            for e in range(DC):
                                last = pe.matmul(psum[i][:, c * D:(c + 1) * D], aw[:, i, e, c * P:(c + 1) * P],
                                                 dft_sb[:, e, :], start=(e == 0), stop=(e == DC - 1))
                        last.then_inc(setup_mm, 1)
                    pe.wait_ge(setup_v, 6 + 2)
                    for i in range(3):
                        for e in range(DC):
                            last = pe.matmul(psum[3 + i][:, 0:D], abw[:, i, e, :], dft_sb[:, e, :],
                                             start=(e == 0), stop=(e == DC - 1))
                        last.then_inc(setup_mm, 1)
                    pe.wait_ge(w_in, 16 * (N_LOADS - N_FIRST_LOADS))
                    for e in range(DC):
                        last = pe.matmul(psum[6][:, 0:D], b0w[:, e, :], wo_raw[:, e, :],
                                         start=(e == 0), stop=(e == DC - 1))
                    last.then_inc(setup_mm, 1)

                n_v = [0]

                @block.vector
                def _(v):
                    def chain(ins):
                        n_v[0] += 1
                        ins.then_inc(setup_v, 1)
                        v.wait_ge(setup_v, n_v[0])

                    v.wait_ge(first_in, 16 * N_FIRST_LOADS)
                    for i in range(3):
                        for c in range(DC):
                            chain(v.tensor_scalar(abw[:, i, c, :], tri_sb[:, 1, :], ab[:, i, c:c + 1], None, ALU.mult))
                    for c in range(DC):
                        chain(v.tensor_scalar(b0w[:, c, :], tri_sb[:, 1, :], cols[:, 1, c:c + 1], None, ALU.mult))
                    for i in range(3):
                        v.wait_ge(setup_mm, i + 1)
                        chain(v.tensor_copy(wf_raw[:, i], psum[i][:, :].rearrange("p (c n) -> p c n", c=DC)))
                    chain(v.tensor_copy(wf[:, 0], wf_raw[:]))
                    chain(v.tensor_tensor(wf[:, 1], wf_raw[:], wf[:, 0], ALU.subtract))
                    v.wait_ge(w_in, 16 * (N_LOADS - N_FIRST_LOADS))
                    chain(v.tensor_copy(idb_sb[:], id_sb[:]))
                    for c in range(DC):
                        chain(v.tensor_scalar(wo_sb[:, c, :], wo_raw[:, c, :], cols[:, 0, c:c + 1], None, ALU.mult))
                    for parts, raw in ((wq_sb, wq_raw), (idft_sb, idft_raw)):
                        chain(v.tensor_copy(parts[:, 0], raw[:]))
                        chain(v.tensor_tensor(parts[:, 1], raw[:], parts[:, 0], ALU.subtract))
                    for i in range(3):
                        v.wait_ge(setup_mm, 4 + i)
                        chain(v.tensor_copy(full[:, BK_F + i], psum[3 + i][:, 0:D]))
                    v.wait_ge(setup_mm, 7)
                    chain(v.tensor_tensor(full[:, B_O], psum[6][:, 0:D], bo_row[:], ALU.add))
                    chain(v.tensor_copy(hi[:], full[:]))
                    chain(v.tensor_tensor(rest[:], full[:], hi[:], ALU.subtract))
                    chain(v.tensor_copy(mid[:], rest[:]))
                    at_hi, at_mid, at_lo = (slice(at, at + 32) for at in PARTS_AT)
                    chain(v.tensor_copy(bias_rows[at_hi], hi[at_hi]))
                    chain(v.tensor_copy(bias_rows[at_mid], mid[at_mid]))
                    chain(v.tensor_tensor(bias_rows[at_lo], rest[at_lo], mid[at_lo], ALU.subtract))
                    assert n_v[0] == SETUP_V, n_v[0]

        w = Shared()
        w.wf = wf
        w.wq = wq_sb
        w.wk = wk_sb
        w.wv = wv_sb
        w.wo = wo_sb
        w.idft = idft_sb
        w.tri = tri_sb
        w.ident = id_sb
        w.ident_bf = idb_sb
        w.bias = bias_rows
        w.picks = picks_sb
        w.g0 = vec[:, 0]
        w.b0 = vec[:, 1]
        w.g1 = vec[:, 2]
        w.b1 = vec[:, 3]
        w.mu_r = cols[:, 2]
        w.mu_k = cols[:, 3]
        w.bq = cols[:, 4]
        w.bk = cols[:, 5]
        w.eps_unit = unit_eps[:]
        w.eps = eps_sb
        w.half_neg = half_neg
        w.minus_one = minus_one
        attention(nc, w, psum, x, ctx, ones_rows, q_dram, k_dram, m_dram, x1_dram, o_dram)
        feed_forward(nc, w, psum, x1_dram, o_dram, wr_t, wk_t, wv_t, out)


SETUP_V = 6 + 2 + 3 + 2 + 1 + 2 + 4 + 3 + 1 + 6


PIECES = [(0, "spec_k"), (5, "turn_o1"), (0, "spec_v"), (1, "turn_g"), (0, "spec_q"), (2, "turn_q"), (1, "inverse"),
          (0, None), (2, "proj_v"), (3, "turn_m"), (1, "proj_k"), (1, "turn_h2"), (0, "cumsum"), (-1, "turn_h"),
          (1, "proj_q"), (4, "turn_o0")]
N_FIRST = 8
T_FIRST = 14
PV_SLOT = {3: (0, 4), 7: (1, 4), 11: (2, 4), 15: (3, 4)}
O_OFF = (4, 5)
N_OFF = 2
T_OFF = 3


def n_head(slot):
    return (slot - N_FIRST, N_OFF) if slot >= N_FIRST else (slot - N_FIRST + SLOTS, N_OFF + 1)


def t_head(slot):
    return (slot - T_FIRST, T_OFF) if slot >= T_FIRST else (slot - T_FIRST + SLOTS, T_OFF + 1)


def attention(nc, w, psum, x, ctx, ones_rows, q_dram, k_dram, m_dram, x1_dram, o_dram):
    with ExitStack() as stack:
        def sb(name, shape, dt=F32):
            return stack.enter_context(nc.sbuf_tensor(name, list(shape), dt))

        sems = []

        def sem(name):
            sems.append(nc.alloc_semaphore(name))
            return sems[-1]

        x_sb = sb("x_sb", [P, R, ST, D])
        h_sb = sb("h_sb", [P, ST, D])
        hT = sb("hT", [P, 2, DC, S], F32R)
        spec = sb("spec", [P, 3, ST, D])
        sq = sb("sq", [P, 3, ST, D])
        mag = sb("mag", [P, 3, ST, NBINS])
        mag2 = sb("mag2", [P, 3, ST, NBINS])
        inv = sb("inv", [P, 2, ST, NBINS])
        kv_direct = sb("kv_direct", [P, ST, D])
        kv_cross = sb("kv_cross", [P, ST, D])
        kv = sb("kv", [P, ST, D])
        bound = sb("bound", [P, ST, D])
        unit_q = sb("unit_q", [P, ST, D])
        sums = sb("sums", [P, ST, D])
        g_direct = sb("g_direct", [P, ST, D])
        g_cross = sb("g_cross", [P, ST, D])
        g_sb = sb("g_sb", [P, ST, D])
        gT = sb("gT", [P, 2, DC, S], F32R)
        x1 = sb("x1", [P, ST, D])
        x1b = sb("x1b", [P, ST, D])
        h2 = sb("h2", [P, ST, D])
        h2T = sb("h2T", [P, 2, DC, S], F32R)
        cT = sb("cT", [P, DC, S])
        kT = sb("kT", [P, DC * S])
        qT = sb("qT", [P, DC * S])
        q_parts = sb("q_parts", [P, 3, DC * S], BF16)
        k_parts = sb("k_parts", [P, 3, DC * S], BF16)
        q_rest = sb("q_rest", [P, DC * S])
        k_rest = sb("k_rest", [P, DC * S])
        q_stack = sb("q_stack", [P, R, H, S], BF16)
        k_stack = sb("k_stack", [P, R, H, S], BF16)
        v_sb = sb("v_sb", [P, R, ST, H, 2 * DH])
        neg_max = sb("neg_max", [P, R, ST, H])
        max_rest = sb("max_rest", [P, ST, H])
        max_parts = sb("max_parts", [P, ST, P], BF16)
        mT = sb("mT", [3 * H, ST, P], BF16)
        probs = sb("probs", [P, 8, ST, S])
        oT = sb("oT", [P, 2, 2, S])
        den = sb("den", [P, 2, ST, 8])
        heads = sb("heads", [P, 2, ST, 8, DH])
        q_rows = sb("q_rows", [P, R, ST, D])
        o_sb = sb("o_sb", [P, ST, D])
        stats = sb("stats", [P, 2, ST, 6])
        moments = sb("moments", [P, 2, ST, 2])
        guard = sb("guard", [P, 2])
        var_eps = sb("var_eps", [P, 2, ST])
        rstd = sb("rstd", [P, 2, ST])
        zeros = sb("zeros", [P, ST, H])

        n_bank = psum[0:2]
        t_bank = psum[2:4]
        pv_bank = psum[4:6]
        work = psum[6:8]

        x_in = [sem(f"x_in{r}") for r in range(R)]
        c_in = [sem(f"c_in{r}") for r in range(R)]
        q_out = [sem(f"q_out{r}") for r in range(R)]
        k_out = [sem(f"k_out{r}") for r in range(R)]
        q_in = [sem(f"q_in{r}") for r in range(R)]
        k_in = [sem(f"k_in{r}") for r in range(R)]
        m_out = [sem(f"m_out{r}") for r in range(R)]
        m_in = [sem(f"m_in{r}") for r in range(R)]
        x1_out = [sem(f"x1_out{r}") for r in range(R)]
        o_out = [sem(f"o_out{r}") for r in range(R)]
        buffers_set = sem("buffers_set")
        ones_in = sem("ones_in")
        stats_done = [sem("stats_done0"), sem("stats_done1")]
        moments_done = [sem("moments_done0"), sem("moments_done1")]
        guard_set = [sem("guard_set0"), sem("guard_set1")]
        var_done = [sem("var_done0"), sem("var_done1")]
        rstd_done = [sem("rstd_done0"), sem("rstd_done1")]
        h_done, h2_done = sem("h_done"), sem("h2_done")
        pe_done = {name: sem("pe_" + name) for _, name in PIECES if name}
        hT_hi, hT_lo, h2T_hi, h2T_lo, gT_hi, gT_lo = (sem(name) for name in (
            "hT_hi", "hT_lo", "h2T_hi", "h2T_lo", "gT_hi", "gT_lo"))
        spec_done = [sem(f"spec_done{i}") for i in range(3)]
        sq_done = [sem(f"sq_done{i}") for i in range(3)]
        mag_done, log_done, abs_done, log2_done = sem("mag_done"), sem("log_done"), sem("abs_done"), sem("log2_done")
        log_kv_done, inv_done = sem("log_kv_done"), sem("inv_done")
        kv_products, kv_done, bound_done, unit_q_done = (sem("kv_products"), sem("kv_done"), sem("bound_done"),
                                                         sem("unit_q_done"))
        sums_done, g_products, g_done = sem("sums_done"), sem("g_products"), sem("g_done")
        x1_done, x1b_done = sem("x1_done"), sem("x1b_done")
        qT_done, kT_done = sem("qT_done"), sem("kT_done")
        q_hi, q_left, q_mid, q_lo = sem("q_hi"), sem("q_left"), sem("q_mid"), sem("q_lo")
        k_hi, k_left, k_mid, k_lo = sem("k_hi"), sem("k_left"), sem("k_mid"), sem("k_lo")
        v_done = sem("v_done")
        n_scores = [sem(f"n_scores{h}") for h in range(HEAD_SEMS)]
        max_done = [sem(f"max_done{h}") for h in range(HEAD_SEMS)]
        m_hi, m_left, m_mid, m_lo, mT_done = (sem("m_hi"), sem("m_left"), sem("m_mid"), sem("m_lo"),
                                              sem("mT_done"))
        t_scores = [sem(f"t_scores{h}") for h in range(HEAD_SEMS)]
        exp_done = [sem(f"exp_done{h}") for h in range(HEAD_SEMS)]
        pv_done = [sem(f"pv_done{g}") for g in range(4)]
        oT_done = [sem("oT_done0"), sem("oT_done1")]
        o_set = sem("o_set")
        den_done = [sem("den_done0"), sem("den_done1")]
        heads_done = [sem("heads_done0"), sem("heads_done1")]
        o_added = [sem("o_added0"), sem("o_added1")]

        emptied = {"turn_h": hT_lo, "turn_q": o_set, "turn_g": gT_lo, "spec_k": spec_done[0],
                   "spec_v": spec_done[1], "turn_m": mT_done, "spec_q": spec_done[2], "inverse": x1_done,
                   "turn_o0": heads_done[0], "turn_h2": h2T_lo, "proj_k": kT_done,
                   "proj_q": qT_done, "cumsum": sums_done, "turn_o1": heads_done[1], "proj_v": v_done}

        def ends(a):
            return a[:, :, 0:2 * P:P]

        def bins(a, half):
            return a[:, :, half * P + 1:(half + 1) * P]

        block = stack.enter_context(nc.Block())

        @block.sync
        def _(sp):
            def step(st):
                if st.live(2):
                    r = st.slot(2)
                    in_registers(sp, st.after(2), st.dma_after(2, dmas=len(K_RUNS), lag=1))
                    sp.wait_ge(k_lo, st.after(2))
                    if st.past(2, R):
                        sp.wait_ge(k_in[r], st.dma_after(2, dmas=len(K_RUNS), lag=1))
                    sp.dma_start(k_dram[r].rearrange("s p n -> p s n"), k_parts[:]).then_inc(k_out[r], 16)
                    in_registers(sp, st.after(2), st.dma_after(2, dmas=len(Q_RUNS), lag=1))
                    sp.wait_ge(q_lo, st.after(2))
                    if st.past(2, R):
                        sp.wait_ge(q_in[r], st.dma_after(2, dmas=len(Q_RUNS), lag=1))
                    sp.dma_start(q_dram[r].rearrange("s p n -> p s n"), q_parts[:]).then_inc(q_out[r], 16)
                    in_registers(sp, st.after(2, R), st.dma_after(2))
                    if st.past(2, R):
                        sp.wait_ge(pv_done[-1], st.after(2, R))
                    sp.wait_ge(k_out[r], st.dma_after(2))
                    for group, part, n in K_RUNS:
                        sp.dma_start(k_stack[DH * group:DH * (group + n), r].rearrange("p h n -> p (h n)"),
                                     k_dram[r, part:part + n].rearrange("s (d h) n -> (s d) (h n)", h=HP)) \
                            .then_inc(k_in[r], 16)
                    in_registers(sp, st.dma_after(2))
                    sp.wait_ge(q_out[r], st.dma_after(2))
                    for group, part, n in Q_RUNS:
                        sp.dma_start(q_stack[DH * group:DH * (group + n), r].rearrange("p h n -> p (h n)"),
                                     q_dram[r, part:part + n].rearrange("s (d h) n -> (s d) (h n)", h=HP)) \
                            .then_inc(q_in[r], 16)
                if st.live(2):
                    in_registers(sp, st.after(2))
                    sp.wait_ge(x1b_done, st.after(2))
                    sp.dma_start(rows_of(x1_dram, st.batch(2)), x1b[:]).then_inc(x1_out[st.slot(2)], 16)
                if st.live(-1):
                    in_registers(sp, st.after(-1, R))
                    if st.past(-1, R):
                        sp.wait_ge(x1_done, st.after(-1, R))
                    r = st.slot(-1)
                    sp.dma_start(x_sb[:, r], rows_of(x, st.batch(-1))).then_inc(x_in[r], 16)
                if st.live(5):
                    in_registers(sp, st.after(5), st.after(5))
                    sp.wait_ge(o_added[0], st.after(5))
                    sp.wait_ge(o_added[1], st.after(5))
                    sp.dma_start(rows_of(o_dram, st.batch(5)), o_sb[:]).then_inc(o_out[st.slot(5)], 16)
                if st.live(3):
                    r = st.slot(3)
                    in_registers(sp, st.after(3), st.dma_after(3, lag=1))
                    sp.wait_ge(mT_done, st.after(3))
                    if st.past(3, R):
                        sp.wait_ge(m_in[r], st.dma_after(3, lag=1))
                    sp.dma_start(m_dram[r].rearrange("s (h n) -> (s h) n", n=S), mT[:].rearrange("p a b -> p (a b)")) \
                        .then_inc(m_out[r], 16)
                    in_registers(sp, st.dma_after(3), st.after(3, R))
                    sp.wait_ge(m_out[r], st.dma_after(3))
                    if st.past(3, R):
                        sp.wait_ge(pv_done[-1], st.after(3, R))
                    sp.dma_start(q_stack[KROWS:KROWS + 3, r].rearrange("p h n -> p (h n)"), m_dram[r]) \
                        .then_inc(m_in[r], 16)
                if st.live(0):
                    in_registers(sp, st.after(0, 1))
                    if st.past(0):
                        sp.wait_ge(pe_done["proj_k"], st.after(0, 1))
                    sp.dma_start(cT[:], one_of(ctx, st.batch(0))).then_inc(c_in[st.slot(0)], 16)

            sp.dma_start(k_stack[KROWS:KROWS + 3].rearrange("p r h n -> p (r h n)"), ones_rows).then_inc(ones_in, 16)
            run_steps(sp, step, FIRST_STEP, LOOP_FIRST, LOOP_STEPS, END_STEP)
            for r in range(R):
                n = 16 * len(range(r, B, R))
                sp.wait_ge(x1_out[r], n)
                sp.wait_ge(o_out[r], n)
                sp.wait_ge(m_out[r], n)
                sp.wait_ge(k_out[r], n)
                sp.wait_ge(q_out[r], n)

        @block.tensor
        def _(pe):
            def bank_free(st, slot):
                for back in range(2, SLOTS + 1, 2):
                    before = Step(st.t - (slot < back), st.i)
                    off, name = PIECES[(slot - back) % SLOTS]
                    if name and before.live(off):
                        pe.wait_ge(emptied[name], before.after(off))
                        return

            def turn(bank, source, name):
                for s in range(ST):
                    for c in range(DC):
                        last = pe.transpose(bank[:, c * S + s * P:c * S + (s + 1) * P],
                                            source[:, s, c * P:(c + 1) * P], w.ident[:])
                last.then_inc(pe_done[name], 1)

            def add_bias(bank, bias):
                pe.matmul(bank[:].rearrange("p (s n) -> p s n", s=ST), w.picks[:],
                          w.bias[:, bias].unsqueeze(1).to_broadcast([P, ST, D]), start=True, stop=False,
                          skip_group_check=True)

            def rows_times(bank, left, right, name, start=False):
                for s in range(ST):
                    for c in range(DC):
                        for part, other in ((0, 0), (0, 1), (1, 0)):
                            last = pe.matmul(bank[:, s * D:(s + 1) * D], left[:, part, c, s * P:(s + 1) * P],
                                             right[:, other, c], start=(start and s + c + part + other == 0),
                                             stop=(c == DC - 1 and part == 1), skip_group_check=True)
                last.then_inc(pe_done[name], 1)

            def turned_times(bank, right, weight, name):
                for m in range(DC):
                    for c in range(DC):
                        for part, other in ((0, 0), (0, 1), (1, 0)):
                            last = pe.matmul(bank[:, m * S:(m + 1) * S], weight[:, other, c, m * P:(m + 1) * P],
                                             right[:, part, c], start=(m + c + part + other == 0),
                                             stop=(c == DC - 1 and part == 1), skip_group_check=True)
                last.then_inc(pe_done[name], 1)

            def piece(st, slot):
                off, name = PIECES[slot]
                if name is None or not st.live(off):
                    return
                bank = work[slot % 2]
                bank_free(st, slot)
                if name == "turn_h":
                    pe.wait_ge(h_done, st.after(-1))
                    turn(bank, h_sb, name)
                elif name == "turn_q":
                    pe.wait_ge(qT_done, st.after(2))
                    for s in range(ST):
                        for c in range(DC):
                            last = pe.transpose(bank[:, s * D + c * P:s * D + (c + 1) * P],
                                                qT[:, c * S + s * P:c * S + (s + 1) * P], w.ident[:])
                    last.then_inc(pe_done[name], 1)
                elif name == "turn_g":
                    pe.wait_ge(g_done, st.after(1))
                    turn(bank, g_sb, name)
                elif name in ("spec_k", "spec_v", "spec_q"):
                    i = ("spec_k", "spec_v", "spec_q").index(name)
                    add_bias(bank, BK_F + i)
                    pe.wait_ge(hT_lo, st.after(0))
                    rows_times(bank, hT, w.wf[:, :, i], name)
                elif name == "turn_m":
                    pe.wait_ge(m_lo, st.after(3))
                    to = bank[:].bitcast(BF16)
                    for s in range(ST):
                        last = pe.transpose(to[:, s * P:(s + 1) * P], max_parts[:, s], w.ident_bf[:])
                    last.then_inc(pe_done[name], 1)
                elif name == "inverse":
                    pe.wait_ge(gT_lo, st.after(1))
                    rows_times(bank, gT, w.idft, name, start=True)
                elif name in ("turn_o0", "turn_o1"):
                    half = int(name[-1])
                    pe.wait_ge(oT_done[half], st.after(off))
                    for s in range(ST):
                        for g in range(2):
                            last = pe.transpose(bank[:, s * 2 * P + g * P:s * 2 * P + (g + 1) * P],
                                                oT[:, half, g, s * P:(s + 1) * P], w.ident[:])
                    last.then_inc(pe_done[name], 1)
                elif name == "turn_h2":
                    pe.wait_ge(h2_done, st.after(1))
                    turn(bank, h2, name)
                elif name == "proj_k":
                    pe.wait_ge(c_in[st.slot(1)], st.dma_after(1))
                    for m in range(DC):
                        for c in range(DC):
                            last = pe.matmul(bank[:, m * S:(m + 1) * S], w.wk[:, c, m * P:(m + 1) * P], cT[:, c],
                                             start=(m + c == 0), stop=(c == DC - 1), skip_group_check=True)
                    last.then_inc(pe_done[name], 1)
                elif name == "proj_q":
                    pe.wait_ge(h2T_lo, st.after(1))
                    turned_times(bank, h2T, w.wq, name)
                elif name == "proj_v":
                    pe.wait_ge(kT_done, st.after(2))
                    add_bias(bank, B_V)
                    for s in range(ST):
                        for c in range(DC):
                            last = pe.matmul(bank[:, s * D:(s + 1) * D], kT[:, c * S + s * P:c * S + (s + 1) * P],
                                             w.wv[:, c], start=False, stop=(c == DC - 1), skip_group_check=True)
                    last.then_inc(pe_done[name], 1)
                elif name == "cumsum":
                    pe.wait_ge(bound_done, st.after(0))
                    pe.matmul(bank[:, 0:D], w.tri[:, 0], bound[:, 0], start=True, stop=True, skip_group_check=True)
                    pe.matmul(bank[:, D:2 * D], w.tri[:, 1], bound[:, 0], start=False, stop=False,
                              skip_group_check=True)
                    pe.matmul(bank[:, D:2 * D], w.tri[:, 0], bound[:, 1], start=False, stop=True,
                              skip_group_check=True).then_inc(pe_done[name], 1)

            def max_scores(st, slot):
                h, off = n_head(slot)
                if not st.live(off):
                    return
                r = st.slot(off)
                if h == 0:
                    pe.wait_ge(q_in[r], st.dma_after(off, dmas=len(Q_RUNS)))
                    pe.wait_ge(k_in[r], st.dma_after(off, dmas=len(K_RUNS)))
                if h >= 2 or st.past(off):
                    pe.wait_ge(max_done[(h - 2) % HEAD_SEMS], st.after_head(off, (h - 2) % H, int(h < 2)))
                for s in range(ST):
                    last = pe.matmul(n_bank[h % 2][:, s * S:(s + 1) * S], q_stack[0:KROWS, r, h, s * P:(s + 1) * P],
                                     k_stack[0:KROWS, r, h], start=True, stop=True, skip_group_check=True)
                last.then_inc(n_scores[h % HEAD_SEMS], 1)

            def exp_scores(st, slot):
                h, off = t_head(slot)
                if not st.live(off):
                    return
                r = st.slot(off)
                if h == 0:
                    pe.wait_ge(m_in[r], st.dma_after(off))
                if h >= 2 or st.past(off):
                    pe.wait_ge(exp_done[(h - 2) % HEAD_SEMS], st.after_head(off, (h - 2) % H, int(h < 2)))
                for s in range(ST):
                    last = pe.matmul(t_bank[h % 2][:, s * S:(s + 1) * S], k_stack[0:KROWS + 3, r, h, s * P:(s + 1) * P],
                                     q_stack[0:KROWS + 3, r, h], start=True, stop=True, skip_group_check=True)
                last.then_inc(t_scores[h % HEAD_SEMS], 1)

            def attend(st, slot):
                if slot not in PV_SLOT:
                    return
                g, off = PV_SLOT[slot]
                if not st.live(off):
                    return
                if g == 0:
                    pe.wait_ge(v_done, st.after(off))
                if g % 2 == 0:
                    if st.past(off):
                        pe.wait_ge(oT_done[g // 2], st.after(off, 1))
                pe.wait_ge(exp_done[(4 * g + 3) % HEAD_SEMS], st.after_head(off, 4 * g + 3))
                for s in range(ST):
                    for j in range(4):
                        h = 4 * g + j
                        last = pe.matmul(pv_bank[g // 2][32 * j:32 * j + 32, (g % 2) * S:(g % 2 + 1) * S],
                                         v_sb[:, st.slot(off), s, h], probs[:, h % 8, s], start=(s == 0),
                                         stop=(s == ST - 1), skip_group_check=True)
                last.then_inc(pv_done[g], 1)

            def step(st):
                for slot in range(SLOTS):
                    max_scores(st, slot)
                    exp_scores(st, slot)
                    attend(st, slot)
                    piece(st, slot)

            pe.wait_ge(buffers_set, 3)
            pe.wait_ge(ones_in, 16)
            run_steps(pe, step, FIRST_STEP, LOOP_FIRST, LOOP_STEPS, END_STEP)

        @block.scalar
        def _(act):
            def exps(st, slot):
                h, off = t_head(slot)
                if not st.live(off):
                    return
                if h >= 8 or st.past(off):
                    act.wait_ge(pv_done[(h - 8) % H // 4], st.after(off, int(h < 8)))
                act.wait_ge(t_scores[h % HEAD_SEMS], st.after_head(off, h))
                act.activation(probs[:, h % 8].rearrange("p s n -> p (s n)"), t_bank[h % 2][:], ACT.Exp,
                               scale=SOFTMAX_SCALE).then_inc(exp_done[h % HEAD_SEMS], 1)

            def flat(a):
                return a.rearrange("p a n -> p (a n)")

            def step(st):
                for slot in range(SLOTS):
                    bank = work[slot % 2][:]
                    if slot == 9 and st.live(0):
                        act.wait_ge(abs_done, st.after(0))
                        act.activation(mag2[:], mag[:], ACT.Ln, bias=w.eps_unit).then_inc(log2_done, 1)
                    exps(st, slot)
                    off, name = PIECES[slot]
                    if slot in (0, 8):
                        half = 0 if slot == 8 else 1
                        at = O_OFF[half]
                        if st.live(at):
                            if st.past(at):
                                act.wait_ge(pe_done[f"turn_o{half}"], st.after(at, 1))
                            act.wait_ge(pv_done[2 * half + 1], st.after(at))
                            act.activation(flat(oT[:, half]), pv_bank[half][:], ACT.Copy).then_inc(oT_done[half], 1)
                    if slot == 7 and st.live(0):
                        if st.past(0):
                            act.wait_ge(inv_done, st.after(0, 1))
                        act.wait_ge(mag_done, st.after(0))
                        act.activation(mag2[:], mag[:], ACT.Ln).then_inc(log_done, 1)
                    if slot == 8 and st.live(0):
                        act.wait_ge(log_done, st.after(0))
                        act.activation(mag[:], mag2[:], ACT.Exp, scale=0.5).then_inc(abs_done, 1)
                    if slot == 9 and st.live(0):
                        if st.past(0):
                            act.wait_ge(bound_done, st.after(0, 1))
                            act.wait_ge(unit_q_done, st.after(0, 1))
                        act.wait_ge(log_kv_done, st.after(0))
                        act.activation(inv[:], mag2[:, 1:3], ACT.Exp, scale=-1.0).then_inc(inv_done, 1)
                    if name is None or not st.live(off):
                        continue
                    if name == "turn_h":
                        if st.past(-1):
                            act.wait_ge(pe_done["spec_q"], st.after(-1, 1))
                        act.wait_ge(pe_done[name], st.after(-1))
                        act.activation(flat(hT[:, 0]), bank, ACT.Copy).then_inc(hT_hi, 1)
                    elif name == "turn_q":
                        r = st.slot(2)
                        if st.past(2, R):
                            act.wait_ge(o_added[1], st.after(2, R))
                        act.wait_ge(pe_done[name], st.after(2))
                        for s in range(ST):
                            to = q_rows[:, r, s].rearrange("p (h c d) -> p c d h", c=DC, d=DH)
                            last = act.activation(to, work[slot % 2][:, s * D:(s + 1) * D]
                                                  .rearrange("p (c d h) -> p c d h", c=DC, d=DH), ACT.Copy)
                        last.then_inc(o_set, 1)
                    elif name == "turn_g":
                        if st.past(1):
                            act.wait_ge(pe_done["inverse"], st.after(1, 1))
                        act.wait_ge(pe_done[name], st.after(1))
                        act.activation(flat(gT[:, 0]), bank, ACT.Copy).then_inc(gT_hi, 1)
                    elif name in ("spec_k", "spec_v", "spec_q"):
                        i = ("spec_k", "spec_v", "spec_q").index(name)
                        if st.past(0):
                            act.wait_ge(sq_done[i], st.after(0, 1))
                        if st.past(0):
                            act.wait_ge(unit_q_done if i == 2 else kv_products, st.after(0, 1))
                        act.wait_ge(pe_done[name], st.after(0))
                        act.activation(flat(spec[:, i]), bank, ACT.Copy).then_inc(spec_done[i], 1)
                    elif name == "turn_m":
                        if st.live(4):
                            act.wait_ge(m_out[st.slot(4)], st.dma_after(4))
                        act.wait_ge(pe_done[name], st.after(3))
                        act.activation(flat(mT[:]), work[slot % 2][0:3 * H].bitcast(BF16)[:, 0:2 * P], ACT.Copy) \
                            .then_inc(mT_done, 1)
                    elif name == "turn_h2":
                        if st.past(1):
                            act.wait_ge(pe_done["proj_q"], st.after(1, 1))
                        act.wait_ge(pe_done[name], st.after(1))
                        act.activation(flat(h2T[:, 0]), bank, ACT.Copy).then_inc(h2T_hi, 1)
                    elif name == "proj_k":
                        if st.past(1):
                            act.wait_ge(k_left, st.after(1, 1))
                        if st.past(1):
                            act.wait_ge(pe_done["proj_v"], st.after(1, 1))
                        act.wait_ge(pe_done[name], st.after(1))
                        for c in range(DC):
                            last = act.activation(kT[:, c * S:(c + 1) * S], bank[:, c * S:(c + 1) * S], ACT.Identity,
                                                  bias=w.bk[:, c:c + 1])
                        last.then_inc(kT_done, 1)
                    elif name == "proj_q":
                        if st.past(1):
                            act.wait_ge(q_left, st.after(1, 1))
                        if st.past(1):
                            act.wait_ge(pe_done["turn_q"], st.after(1, 1))
                        act.wait_ge(pe_done[name], st.after(1))
                        for c in range(DC):
                            last = act.activation(qT[:, c * S:(c + 1) * S], bank[:, c * S:(c + 1) * S], ACT.Identity,
                                                  bias=w.bq[:, c:c + 1])
                        last.then_inc(qT_done, 1)
                    elif name == "cumsum":
                        if st.past(0):
                            act.wait_ge(g_products, st.after(0, 1))
                        act.wait_ge(pe_done[name], st.after(0))
                        act.activation(flat(sums[:]), bank, ACT.Copy).then_inc(sums_done, 1)
                    elif name == "proj_v":
                        r = st.slot(2)
                        if st.past(2, R):
                            act.wait_ge(pv_done[3], st.after(2, R))
                        act.wait_ge(pe_done[name], st.after(2))
                        act.activation(v_sb[:, r, :, :, 0:DH].rearrange("p s h d -> p (s h) d"),
                                       bank.rearrange("p (a d) -> p a d", d=DH), ACT.Copy).then_inc(v_done, 1)

            nc.scalar.preload_act_table_set("natural_log_exp_and_others")
            act.wait_ge(buffers_set, 3)
            run_steps(act, step, FIRST_STEP, LOOP_FIRST, LOOP_STEPS, END_STEP)

        @block.vector
        def _(v):
            def row_moments(st, off, n, tile, reader_done):
                if st.past(off):
                    v.wait_ge(moments_done[n], st.after(off, 1))
                for s in range(ST):
                    last = v.bn_stats(stats[:, n, s], tile[:, s])
                last.then_inc(stats_done[n], 1)
                if st.past(off):
                    v.wait_ge(reader_done, st.after(off, 1))
                v.wait_ge(stats_done[n], st.after(off))
                if st.past(off):
                    v.wait_ge(guard_set[n], st.after(off, 1))
                v.memset(guard[:, n:n + 1], 0.0).then_inc(guard_set[n], 1)
                for s in range(ST):
                    last = v.bn_aggr(moments[:, n, s], stats[:, n, s])
                last.then_inc(moments_done[n], 1)

            def normalise(st, off, n, tile, to, done):
                v.wait_ge(rstd_done[n], st.after(off))
                for s in range(ST):
                    last = v.tensor_scalar(to[:, s], tile[:, s], moments[:, n, s, 0:1], rstd[:, n, s:s + 1],
                                           ALU.subtract, ALU.mult)
                last.then_inc(done, 1)

            def rest_of(parts, bank):
                return v.tensor_tensor(parts[:, 1], bank[:].rearrange("p (c n) -> p c n", c=DC), parts[:, 0],
                                       ALU.subtract)

            def maxima(st, slot):
                h, off = n_head(slot)
                if not st.live(off):
                    return
                if h == 0:
                    if st.past(off, R):
                        v.wait_ge(m_left, st.after(off, R))
                v.wait_ge(n_scores[h % HEAD_SEMS], st.after_head(off, h))
                v.tensor_reduce(neg_max[:, st.slot(off), :, h:h + 1], n_bank[h % 2][:].rearrange("p (s n) -> p s n", s=ST), AX.X,
                                ALU.max, negate=True).then_inc(max_done[h % HEAD_SEMS], 1)

            def hi_part(st, off, full, parts, at, done, out_sem, ready):
                if st.live(off + 1):
                    v.wait_ge(out_sem[st.slot(off + 1)], st.dma_after(off + 1))
                v.wait_ge(ready, st.after(off))
                v.tensor_copy(parts[:, at], full[:]).then_inc(done, 1)

            def take_heads(st, half):
                bank = work[1]
                view = bank[:].rearrange("p (s h e) -> p s h e", s=ST, e=2 * DH)
                if st.past(5):
                    v.wait_ge(heads_done[half], st.after(5, 1))
                v.wait_ge(pe_done[f"turn_o{half}"], st.after(5))
                v.reciprocal(den[:, half], view[:, :, :, DH]).then_inc(den_done[half], 1)
                if st.past(5):
                    v.wait_ge(o_added[half], st.after(5, 1))
                v.wait_ge(den_done[half], st.after(5))
                v.tensor_tensor(heads[:, half], view[:, :, :, 0:DH],
                                den[:, half].unsqueeze(3).to_broadcast([P, ST, 8, DH]), ALU.mult) \
                    .then_inc(heads_done[half], 1)

            def step(st):
                for slot in range(SLOTS):
                    maxima(st, slot)
                    if slot == 0 and st.live(5):
                        take_heads(st, 0)
                    if slot == 0 and st.live(2):
                        hi_part(st, 2, qT, q_parts, Q_HI, q_hi, q_out, qT_done)
                        if st.past(2):
                            v.wait_ge(q_lo, st.after(2, 1))
                        v.wait_ge(q_hi, st.after(2))
                        v.tensor_tensor(q_rest[:], qT[:], q_parts[:, Q_HI], ALU.subtract).then_inc(q_left, 1)
                    if slot == 1 and st.live(2):
                        v.wait_ge(q_left, st.after(2))
                        v.tensor_copy(q_parts[:, Q_MID], q_rest[:]).then_inc(q_mid, 1)
                        v.wait_ge(q_mid, st.after(2))
                        v.tensor_tensor(q_parts[:, Q_LO], q_rest[:], q_parts[:, Q_MID], ALU.subtract) \
                            .then_inc(q_lo, 1)
                    if slot == 1 and st.live(5):
                        take_heads(st, 1)
                    if slot == 4 and st.live(1):
                        if st.past(1):
                            v.wait_ge(pe_done["inverse"], st.after(1, 1))
                        v.wait_ge(gT_hi, st.after(1))
                        rest_of(gT, work[1]).then_inc(gT_lo, 1)
                    if slot == 4 and st.live(0):
                        if st.past(0):
                            v.wait_ge(kv_done, st.after(0, 1))
                        v.wait_ge(spec_done[0], st.after(0))
                        v.wait_ge(spec_done[1], st.after(0))
                        v.tensor_tensor(kv_direct[:], spec[:, 0], spec[:, 1], ALU.mult)
                        v.tensor_tensor(kv_cross[:, :, 0:P], spec[:, 0, :, 0:P], spec[:, 1, :, P:2 * P], ALU.mult)
                        v.tensor_tensor(kv_cross[:, :, P:2 * P], spec[:, 0, :, P:2 * P], spec[:, 1, :, 0:P],
                                        ALU.mult).then_inc(kv_products, 1)
                    if slot == 6 and st.live(0):
                        for i in range(3):
                            v.wait_ge(sq_done[i], st.after(0))
                        if st.past(0):
                            v.wait_ge(log2_done, st.after(0, 1))
                        sq6 = sq[:].rearrange("p i s n -> p (i s) n")
                        mag6 = mag[:].rearrange("p i s n -> p (i s) n")
                        v.scalar_tensor_tensor(mag6[:, :, 1:P], sq6[:, :, 1:P], LN_FLOOR, sq6[:, :, P + 1:2 * P],
                                               ALU.max, ALU.add)
                        v.tensor_scalar(mag6[:, :, 0:P + 1:P], sq6[:, :, 0:P + 1:P], LN_FLOOR, None, ALU.max) \
                            .then_inc(mag_done, 1)
                    if slot == 6 and st.live(1):
                        if st.past(1):
                            v.wait_ge(x1b_done, st.after(1, 1))
                        v.wait_ge(pe_done["inverse"], st.after(1))
                        v.tensor_tensor(x1[:], x_sb[:, st.slot(1)], work[0][:].rearrange("p (s n) -> p s n", s=ST),
                                        ALU.add).then_inc(x1_done, 1)
                    if slot == 7 and st.live(1):
                        v.wait_ge(x1_done, st.after(1))
                        row_moments(st, 1, 1, x1[:], h2_done)
                    if slot == 8 and st.live(-1):
                        r = st.slot(-1)
                        v.wait_ge(x_in[r], st.dma_after(-1))
                        row_moments(st, -1, 0, x_sb[:, r], h_done)
                    if slot == 9 and st.live(1):
                        if st.past(1):
                            v.wait_ge(pe_done["turn_h2"], st.after(1, 1))
                        normalise(st, 1, 1, x1, h2, h2_done)
                    if slot == 9 and st.live(0):
                        if st.past(0):
                            v.wait_ge(bound_done, st.after(0, 1))
                        v.wait_ge(kv_products, st.after(0))
                        v.tensor_tensor(bins(kv, 0), bins(kv_direct, 0), bins(kv_direct, 1), ALU.subtract)
                        v.tensor_tensor(bins(kv, 1), bins(kv_cross, 0), bins(kv_cross, 1), ALU.add)
                        v.tensor_copy(ends(kv), ends(kv_direct)).then_inc(kv_done, 1)
                    if slot == 11 and st.live(-1):
                        if st.past(-1):
                            v.wait_ge(pe_done["turn_h"], st.after(-1, 1))
                        normalise(st, -1, 0, x_sb[:, st.slot(-1)], h_sb, h_done)
                    if slot == 12 and st.live(1):
                        if st.past(1):
                            v.wait_ge(pe_done["proj_q"], st.after(1, 1))
                        v.wait_ge(h2T_hi, st.after(1))
                        rest_of(h2T, work[1]).then_inc(h2T_lo, 1)
                        hi_part(st, 1, kT, k_parts, K_HI, k_hi, k_out, kT_done)
                    if slot == 14 and st.live(-1):
                        if st.past(-1):
                            v.wait_ge(pe_done["spec_q"], st.after(-1, 1))
                        v.wait_ge(hT_hi, st.after(-1))
                        rest_of(hT, work[1]).then_inc(hT_lo, 1)
                    if slot == 14 and st.live(0):
                        if st.past(0):
                            v.wait_ge(g_done, st.after(0, 1))
                        v.wait_ge(unit_q_done, st.after(0))
                        v.wait_ge(sums_done, st.after(0))
                        v.tensor_tensor(g_direct[:], sums[:], unit_q[:], ALU.mult)
                        v.tensor_tensor(g_cross[:, :, 0:P], sums[:, :, 0:P], unit_q[:, :, P:2 * P], ALU.mult)
                        v.tensor_tensor(g_cross[:, :, P:2 * P], sums[:, :, P:2 * P], unit_q[:, :, 0:P],
                                        ALU.mult).then_inc(g_products, 1)
                    if slot == 15 and st.live(1):
                        v.wait_ge(k_left, st.after(1))
                        v.tensor_copy(k_parts[:, K_MID], k_rest[:]).then_inc(k_mid, 1)
                    if slot == 15 and st.live(0):
                        v.wait_ge(g_products, st.after(0))
                        if st.past(0):
                            v.wait_ge(pe_done["turn_g"], st.after(0, 1))
                        v.tensor_tensor(bins(g_sb, 0), bins(g_direct, 0), bins(g_direct, 1), ALU.add)
                        v.tensor_tensor(bins(g_sb, 1), bins(g_cross, 1), bins(g_cross, 0), ALU.subtract)
                        v.tensor_copy(ends(g_sb), ends(g_direct)).then_inc(g_done, 1)

            v.memset(max_parts[:], 0.0).then_inc(buffers_set, 1)
            run_steps(v, step, FIRST_STEP, LOOP_FIRST, LOOP_STEPS, END_STEP)

        @block.gpsimd
        def _(pool):
            def inv_std(st, off, n):
                if st.past(off):
                    pool.wait_ge(rstd_done[n], st.after(off, 1))
                pool.wait_ge(moments_done[n], st.after(off))
                pool.tensor_tensor(var_eps[:, n], moments[:, n, :, 1], w.eps[:], ALU.add).then_inc(var_done[n], 1)
                if st.past(off):
                    pool.wait_ge((h_done, h2_done)[n], st.after(off, 1))
                pool.wait_ge(var_done[n], st.after(off))
                pool.tensor_tensor(rstd[:, n], var_eps[:, n], w.half_neg[:], ALU.pow).then_inc(rstd_done[n], 1)

            def scale_spectrum(st, to, a, factors, done):
                both = to[:].rearrange("p s (c n) -> p s c n", c=2)[:, :, :, 1:P]
                wide = factors[:, :, 1:P].unsqueeze(2).to_broadcast([P, ST, 2, P - 1])
                pool.tensor_tensor(both, a.rearrange("p s (c n) -> p s c n", c=2)[:, :, :, 1:P], wide, ALU.mult)
                pool.tensor_tensor(ends(to), ends(a), factors[:, :, 0:P + 1:P], ALU.mult).then_inc(done, 1)

            def step(st):
                for slot in range(SLOTS):
                    if slot in (1, 3) and st.live(5):
                        add_heads(st, slot // 2)
                    if slot in (2, 4, 6) and st.live(0):
                        i = slot // 2 - 1
                        if st.past(0):
                            pool.wait_ge(mag_done, st.after(0, 1))
                        pool.wait_ge(spec_done[i], st.after(0))
                        pool.tensor_tensor(sq[:, i], spec[:, i], spec[:, i], ALU.mult).then_inc(sq_done[i], 1)
                    if slot == 8 and st.live(3):
                        if st.past(3):
                            pool.wait_ge(pe_done["turn_m"], st.after(3, 1))
                        pool.wait_ge(max_done[-1], st.after_head(3, H - 1))
                        hi, mid, lo = (max_parts[:, :, i * H:(i + 1) * H] for i in range(3))
                        pool.tensor_tensor(hi, neg_max[:, st.slot(3)], zeros[:], ALU.add).then_inc(m_hi, 1)
                        pool.wait_ge(m_hi, st.after(3))
                        pool.tensor_tensor(max_rest[:], neg_max[:, st.slot(3)], hi, ALU.subtract).then_inc(m_left, 1)
                        pool.wait_ge(m_left, st.after(3))
                        pool.tensor_tensor(mid, max_rest[:], zeros[:], ALU.add).then_inc(m_mid, 1)
                        pool.wait_ge(m_mid, st.after(3))
                        pool.tensor_tensor(lo, max_rest[:], mid, ALU.subtract).then_inc(m_lo, 1)
                    if slot == 8 and st.live(1):
                        inv_std(st, 1, 1)
                    if slot == 8 and st.live(0):
                        pool.wait_ge(log2_done, st.after(0))
                        pool.tensor_tensor(mag2[:, 1], mag2[:, 0], mag2[:, 1], ALU.add).then_inc(log_kv_done, 1)
                    if slot == 8 and st.live(-1):
                        inv_std(st, -1, 0)
                    if slot == 10 and st.live(0):
                        if st.past(0):
                            pool.wait_ge(pe_done["cumsum"], st.after(0, 1))
                        pool.wait_ge(kv_done, st.after(0))
                        pool.wait_ge(inv_done, st.after(0))
                        scale_spectrum(st, bound, kv, inv[:, 0], bound_done)
                    if slot == 11 and st.live(0):
                        if st.past(0):
                            pool.wait_ge(g_products, st.after(0, 1))
                        pool.wait_ge(spec_done[2], st.after(0))
                        scale_spectrum(st, unit_q, spec[:, 2], inv[:, 1], unit_q_done)
                    if slot == 12 and st.live(1):
                        if st.live(2):
                            pool.wait_ge(x1_out[st.slot(2)], st.dma_after(2))
                        pool.wait_ge(x1_done, st.after(1))
                        pool.tensor_tensor(x1b[:], x1[:], w.b1.unsqueeze(1).to_broadcast([P, ST, D]), ALU.add) \
                            .then_inc(x1b_done, 1)
                    if slot == 13 and st.live(1):
                        if st.past(1):
                            pool.wait_ge(k_lo, st.after(1, 1))
                        pool.wait_ge(k_hi, st.after(1))
                        pool.tensor_tensor(k_rest[:], kT[:], k_parts[:, K_HI], ALU.subtract).then_inc(k_left, 1)
                    if slot == 15 and st.live(1):
                        pool.wait_ge(k_mid, st.after(1))
                        pool.tensor_tensor(k_parts[:, K_LO], k_rest[:], k_parts[:, K_MID], ALU.subtract) \
                            .then_inc(k_lo, 1)

            def add_heads(st, half):
                r = st.slot(5)
                cols = slice(half * P, (half + 1) * P)
                if st.live(6):
                    pool.wait_ge(o_out[st.slot(6)], st.dma_after(6))
                pool.wait_ge(o_set, st.after(5))
                pool.wait_ge(heads_done[half], st.after(5))
                pool.tensor_tensor(o_sb[:, :, cols], q_rows[:, r, :, cols], heads[:, half].rearrange("p s h d -> p s (h d)"), ALU.add) \
                    .then_inc(o_added[half], 1)

            pool.memset(v_sb[:, :, :, :, DH:2 * DH].rearrange("p r s h d -> p (r s h) d"), 1.0).then_inc(buffers_set, 1)
            pool.memset(zeros[:], 0.0).then_inc(buffers_set, 1)
            pool.wait_ge(buffers_set, 3)
            run_steps(pool, step, FIRST_STEP, LOOP_FIRST, LOOP_STEPS, END_STEP)

    nc.all_engine_barrier()
    nc.clear_and_free_semaphores(sems)
    nc.all_engine_barrier()


def feed_forward(nc, w, psum, x1_dram, o_dram, wr_t, wk_t, wv_t, out):
    with ExitStack() as stack:
        def sb(name, shape, dt=F32):
            return stack.enter_context(nc.sbuf_tensor(name, list(shape), dt))

        def sem(name):
            return stack.enter_context(nc.semaphore(name))

        wr = sb("f_wr", [P, DC, D])
        wk = sb("f_wk", [P, DC, D])
        wv = sb("f_wv", [P, DC, D])
        x1b = sb("f_x1b", [P, R, ST, D])
        o = sb("f_o", [P, R, ST, D])
        on = sb("f_on", [P, ST, D])
        onT = sb("f_onT", [P, DC, S])
        gelu = sb("f_gelu", [P, ST, D])
        scaled = sb("f_scaled", [P, ST, D])
        scaled_b = sb("f_scaled_b", [P, ST, D])
        o2 = sb("f_o2", [P, ST, D])
        centred = sb("f_centred", [P, ST, D])
        x2 = sb("f_x2", [P, R, ST, D])
        h = sb("f_h", [P, ST, D])
        hT = sb("f_hT", [P, DC, S + 2])
        diff = sb("f_diff", [P, DC, S])
        xr = sb("f_xr", [P, DC, S])
        xk = sb("f_xk", [P, DC, S])
        tanh = sb("f_tanh", [P, ST, D])
        relu = sb("f_relu", [P, DC, S])
        k2 = sb("f_k2", [P, DC, S])
        gated = sb("f_gated", [P, ST, D])
        y = sb("f_y", [P, R, ST, D])
        stats = sb("f_stats", [P, 3, ST, 6])
        moments = sb("f_moments", [P, 3, ST, 2])
        guard = sb("f_guard", [P, 3])
        var_eps = sb("f_var_eps", [P, 3, ST])
        rstd = sb("f_rstd", [P, 3, ST])
        neg_mean = sb("f_neg_mean", [P, 3, ST])
        shift = sb("f_shift", [P, 3, ST])

        v_bank, r_bank, k_bank, on_bank, wo_bank, h_bank = psum[0:6]

        w_in = sem("f_w_in")
        x1b_in = [sem(f"f_x1_in{r}") for r in range(R)]
        o_in = [sem(f"f_o_in{r}") for r in range(R)]
        y_out = [sem(f"f_y_out{r}") for r in range(R)]
        pad_set = sem("f_pad_set")
        stats_done = [sem(f"f_stats_done{n}") for n in range(3)]
        moments_done = [sem(f"f_moments_done{n}") for n in range(3)]
        guard_set = [sem(f"f_guard_set{n}") for n in range(3)]
        var_done = [sem(f"f_var_done{n}") for n in range(3)]
        rstd_done = [sem(f"f_rstd_done{n}") for n in range(3)]
        neg_mean_done = [sem(f"f_neg_mean_done{n}") for n in range(3)]
        shift_done = [sem(f"f_shift_done{n}") for n in range(3)]
        names = ("on_done on_turned onT_done wo_done gelu_done scaled_done scaled_b_done o2_done "
                 "centred_done x2_done h_done h_turned hT_done diff_done xr_done xk_done r_done k_done tanh_done "
                 "relu_done k2_done v_done gated_done y_done").split()
        (on_done, on_turned, onT_done, wo_done, gelu_done, scaled_done, scaled_b_done, o2_done,
         centred_done, x2_done, h_done, h_turned, hT_done, diff_done, xr_done, xk_done, r_done, k_done, tanh_done,
         relu_done, k2_done, v_done, gated_done, y_done) = (sem("f_" + name) for name in names)

        FIRST, LOOP, STEPS, END = -1, 5, 24, B + 4
        block = stack.enter_context(nc.Block())

        def wide(row):
            return row.unsqueeze(1).to_broadcast([P, ST, D])

        @block.sync
        def _(sp):
            def step(st):
                if st.live(-1):
                    r = st.slot(-1)
                    in_registers(sp, st.after(-1, R))
                    if st.past(-1, R):
                        sp.wait_ge(on_done, st.after(-1, R))
                    sp.dma_start(o[:, r], rows_of(o_dram, st.batch(-1))).then_inc(o_in[r], 16)
                if st.live(0):
                    r = st.slot(0)
                    in_registers(sp, st.after(0, R))
                    if st.past(0, R):
                        sp.wait_ge(x2_done, st.after(0, R))
                    sp.dma_start(x1b[:, r], rows_of(x1_dram, st.batch(0))).then_inc(x1b_in[r], 16)
                if st.live(4):
                    r = st.slot(4)
                    in_registers(sp, st.after(4))
                    sp.wait_ge(y_done, st.after(4))
                    sp.dma_start(rows_of(out, st.batch(4)), y[:, r]).then_inc(y_out[r], 16)

            step(Step(FIRST))
            for to, source in ((wk, wk_t), (wr, wr_t), (wv, wv_t)):
                sp.dma_start(to[:], source.rearrange("(c p) n -> p c n", p=P)).then_inc(w_in, 16)
            run_steps(sp, step, FIRST + 1, LOOP, STEPS, END)
            for r in range(R):
                sp.wait_ge(y_out[r], 16 * len(range(r, B, R)))

        @block.tensor
        def _(pe):
            def turn(bank, source, done):
                for s in range(ST):
                    for c in range(DC):
                        last = pe.transpose(bank[:, c * S + s * P:c * S + (s + 1) * P],
                                            source[:, s, c * P:(c + 1) * P], w.ident[:])
                last.then_inc(done, 1)

            def rows_times(bank, left, right, done, first=True):
                for s in range(ST):
                    for c in range(DC):
                        last = pe.matmul(bank[:, s * D:(s + 1) * D], left[:, c, s * P:(s + 1) * P], right[:, c],
                                         start=(first and s == 0 and c == 0), stop=(c == DC - 1),
                                         skip_group_check=True)
                last.then_inc(done, 1)

            def step(st):
                if st.live(3):
                    if st.past(3):
                        pe.wait_ge(hT_done, st.after(3, 1))
                    pe.wait_ge(h_done, st.after(3))
                    turn(h_bank, h, h_turned)
                if st.live(1):
                    if st.past(1):
                        pe.wait_ge(gelu_done, st.after(1, 1))
                    pe.wait_ge(onT_done, st.after(1))
                    pe.matmul(wo_bank[:].rearrange("p (s n) -> p s n", s=ST), w.picks[:],
                              w.bias[:, B_O].unsqueeze(1).to_broadcast([P, ST, D]), start=True, stop=False,
                              skip_group_check=True)
                    rows_times(wo_bank, onT, w.wo, wo_done, first=False)
                if st.live(4):
                    if st.past(4):
                        pe.wait_ge(gated_done, st.after(4, 1))
                    pe.wait_ge(k2_done, st.after(4))
                    rows_times(v_bank, k2, wv, v_done)
                if st.live(3):
                    if st.past(3):
                        pe.wait_ge(relu_done, st.after(3, 1))
                    pe.wait_ge(w_in, 16 * 3)
                    pe.wait_ge(xk_done, st.after(3))
                    for m in range(DC):
                        for c in range(DC):
                            last = pe.matmul(k_bank[:, m * S:(m + 1) * S], wk[:, c, m * P:(m + 1) * P], xk[:, c],
                                             start=(m == 0 and c == 0), stop=(c == DC - 1), skip_group_check=True)
                    last.then_inc(k_done, 1)
                if st.live(0):
                    if st.past(0):
                        pe.wait_ge(onT_done, st.after(0, 1))
                    pe.wait_ge(on_done, st.after(0))
                    turn(on_bank, on, on_turned)
                if st.live(3):
                    if st.past(3):
                        pe.wait_ge(tanh_done, st.after(3, 1))
                    pe.wait_ge(xr_done, st.after(3))
                    rows_times(r_bank, xr, wr, r_done)

            run_steps(pe, step, FIRST, LOOP, STEPS, END)

        @block.scalar
        def _(act):
            def flat(a):
                return a.rearrange("p a n -> p (a n)")

            def normalise(st, off, n, tile, to, done):
                act.wait_ge(shift_done[n], st.after(off))
                for s in range(ST):
                    last = act.activation(to[:, s], tile[:, s], ACT.Identity, bias=shift[:, n, s:s + 1],
                                          scale=rstd[:, n, s:s + 1])
                last.then_inc(done, 1)

            def step(st):
                if st.live(3):
                    if st.past(3):
                        act.wait_ge(xr_done, st.after(3, 1))
                    if st.past(3):
                        act.wait_ge(xk_done, st.after(3, 1))
                    act.wait_ge(h_turned, st.after(3))
                    act.activation(hT[:, :, 2:S + 2], h_bank[:].rearrange("p (c n) -> p c n", c=DC), ACT.Copy) \
                        .then_inc(hT_done, 1)
                if st.live(4):
                    if st.past(4):
                        act.wait_ge(gated_done, st.after(4, 1))
                    act.wait_ge(r_done, st.after(4))
                    act.activation(flat(tanh[:]), r_bank[:], ACT.Tanh, scale=0.5).then_inc(tanh_done, 1)
                if st.live(1):
                    if st.past(1):
                        act.wait_ge(o2_done, st.after(1, 1))
                    act.wait_ge(wo_done, st.after(1))
                    act.activation(flat(gelu[:]), wo_bank[:], ACT.Gelu).then_inc(gelu_done, 1)
                if st.live(0):
                    if st.past(0):
                        act.wait_ge(on_turned, st.after(0, 1))
                    if st.past(0):
                        act.wait_ge(scaled_done, st.after(0, 1))
                    normalise(st, 0, 0, o[:, st.slot(0)], on, on_done)
                if st.live(2):
                    if st.past(2):
                        act.wait_ge(h_turned, st.after(2, 1))
                    normalise(st, 2, 2, x2[:, st.slot(2)], h, h_done)
                if st.live(3):
                    if st.past(3):
                        act.wait_ge(k2_done, st.after(3, 1))
                    act.wait_ge(k_done, st.after(3))
                    act.activation(flat(relu[:]), k_bank[:], ACT.Relu).then_inc(relu_done, 1)
                if st.live(0):
                    if st.past(0):
                        act.wait_ge(wo_done, st.after(0, 1))
                    act.wait_ge(on_turned, st.after(0))
                    act.activation(flat(onT[:]), on_bank[:], ACT.Copy).then_inc(onT_done, 1)
                if st.live(3):
                    if st.past(3):
                        act.wait_ge(v_done, st.after(3, 1))
                    act.wait_ge(relu_done, st.after(3))
                    act.activation(k2[:], relu[:], ACT.Square).then_inc(k2_done, 1)

            nc.scalar.preload_act_table_set("gelu_and_others")
            act.wait_ge(pad_set, 1)
            run_steps(act, step, FIRST, LOOP, STEPS, END)

        @block.vector
        def _(v):
            def row_stats(st, off, n, tile):
                if st.past(off):
                    v.wait_ge(moments_done[n], st.after(off, 1))
                for s in range(ST):
                    last = v.bn_stats(stats[:, n, s], tile[:, s])
                last.then_inc(stats_done[n], 1)

            def row_moments(st, off, n, reader_done):
                if st.past(off):
                    v.wait_ge(reader_done, st.after(off, 1))
                v.wait_ge(stats_done[n], st.after(off))
                if st.past(off):
                    v.wait_ge(guard_set[n], st.after(off, 1))
                v.memset(guard[:, n:n + 1], 0.0).then_inc(guard_set[n], 1)
                for s in range(ST):
                    last = v.bn_aggr(moments[:, n, s], stats[:, n, s])
                last.then_inc(moments_done[n], 1)

            def token_mix(st, to, mu, done, reader_done):
                if st.past(3):
                    v.wait_ge(reader_done, st.after(3, 1))
                v.wait_ge(diff_done, st.after(3))
                for c in range(DC):
                    last = v.scalar_tensor_tensor(to[:, c], diff[:, c], mu[:, c:c + 1], hT[:, c, 1:S + 1],
                                                  ALU.mult, ALU.add)
                last.then_inc(done, 1)

            def step(st):
                if st.live(2):
                    if st.past(2):
                        v.wait_ge(x2_done, st.after(2, 1))
                    v.wait_ge(moments_done[1], st.after(2))
                    for s in range(ST):
                        last = v.scalar_tensor_tensor(centred[:, s], o2[:, s], moments[:, 1, s, 0:1], w.g1,
                                                      ALU.subtract, ALU.mult)
                    last.then_inc(centred_done, 1)
                if st.live(0):
                    r = st.slot(0)
                    v.wait_ge(o_in[r], st.dma_after(0))
                    row_stats(st, 0, 0, o[:, r])
                if st.live(2):
                    r = st.slot(2)
                    v.wait_ge(x1b_in[r], st.dma_after(2))
                    if st.past(2, R):
                        v.wait_ge(y_done, st.after(2, R))
                    v.wait_ge(rstd_done[1], st.after(2))
                    v.wait_ge(centred_done, st.after(2))
                    for s in range(ST):
                        last = v.scalar_tensor_tensor(x2[:, r, s], centred[:, s], rstd[:, 1, s:s + 1], x1b[:, r, s],
                                                      ALU.mult, ALU.add)
                    last.then_inc(x2_done, 1)
                if st.live(0):
                    row_moments(st, 0, 0, on_done)
                if st.live(2):
                    v.wait_ge(x2_done, st.after(2))
                    row_stats(st, 2, 2, x2[:, st.slot(2)])
                if st.live(2):
                    row_moments(st, 2, 2, h_done)
                if st.live(3):
                    token_mix(st, xk, w.mu_k, xk_done, k_done)
                if st.live(1):
                    if st.past(1):
                        v.wait_ge(centred_done, st.after(1, 1))
                    v.wait_ge(gelu_done, st.after(1))
                    v.wait_ge(scaled_b_done, st.after(1))
                    v.tensor_tensor(o2[:], gelu[:], scaled_b[:], ALU.add).then_inc(o2_done, 1)
                if st.live(3):
                    token_mix(st, xr, w.mu_r, xr_done, r_done)
                if st.live(1):
                    v.wait_ge(o2_done, st.after(1))
                    row_stats(st, 1, 1, o2)
                if st.live(4):
                    if st.past(4):
                        v.wait_ge(y_done, st.after(4, 1))
                    v.wait_ge(tanh_done, st.after(4))
                    v.wait_ge(v_done, st.after(4))
                    v.scalar_tensor_tensor(gated[:].rearrange("p s n -> p (s n)"),
                                           tanh[:].rearrange("p s n -> p (s n)"), 1.0, v_bank[:], ALU.add, ALU.mult) \
                        .then_inc(gated_done, 1)
                if st.live(1):
                    row_moments(st, 1, 1, x2_done)
                if st.live(4):
                    r = st.slot(4)
                    if st.past(4, R):
                        v.wait_ge(y_out[r], st.dma_after(4, lag=1))
                    v.wait_ge(gated_done, st.after(4))
                    v.scalar_tensor_tensor(y[:, r].rearrange("p s n -> p (s n)"),
                                           gated[:].rearrange("p s n -> p (s n)"), 0.5,
                                           x2[:, r].rearrange("p s n -> p (s n)"), ALU.mult, ALU.add) \
                        .then_inc(y_done, 1)

            v.memset(hT[:, :, 0:2], 0.0).then_inc(pad_set, 1)
            run_steps(v, step, FIRST, LOOP, STEPS, END)

        @block.gpsimd
        def _(pool):
            def inv_std(st, off, n, reader_done):
                pool.wait_ge(moments_done[n], st.after(off))
                pool.tensor_tensor(var_eps[:, n], moments[:, n, :, 1], w.eps[:], ALU.add).then_inc(var_done[n], 1)
                if n != 1:
                    pool.tensor_tensor(neg_mean[:, n], moments[:, n, :, 0], w.minus_one[:], ALU.mult) \
                        .then_inc(neg_mean_done[n], 1)
                if st.past(off):
                    pool.wait_ge(reader_done, st.after(off, 1))
                pool.wait_ge(var_done[n], st.after(off))
                pool.tensor_tensor(rstd[:, n], var_eps[:, n], w.half_neg[:], ALU.pow).then_inc(rstd_done[n], 1)
                if n != 1:
                    pool.wait_ge(rstd_done[n], st.after(off))
                    pool.wait_ge(neg_mean_done[n], st.after(off))
                    pool.tensor_tensor(shift[:, n], neg_mean[:, n], rstd[:, n], ALU.mult).then_inc(shift_done[n], 1)

            def step(st):
                if st.live(1):
                    if st.past(1):
                        pool.wait_ge(o2_done, st.after(1, 1))
                    pool.wait_ge(scaled_done, st.after(1))
                    pool.tensor_tensor(scaled_b[:], scaled[:], wide(w.b0), ALU.add).then_inc(scaled_b_done, 1)
                if st.live(3):
                    if st.past(3):
                        pool.wait_ge(xr_done, st.after(3, 1))
                    pool.wait_ge(hT_done, st.after(3))
                    pool.tensor_tensor(diff[:], hT[:, :, 2:S + 2], hT[:, :, 1:S + 1], ALU.subtract) \
                        .then_inc(diff_done, 1)
                if st.live(0):
                    inv_std(st, 0, 0, on_done)
                if st.live(2):
                    inv_std(st, 2, 2, h_done)
                if st.live(0):
                    if st.past(0):
                        pool.wait_ge(scaled_b_done, st.after(0, 1))
                    pool.wait_ge(on_done, st.after(0))
                    pool.tensor_tensor(scaled[:], on[:], wide(w.g0), ALU.mult).then_inc(scaled_done, 1)
                if st.live(1):
                    inv_std(st, 1, 1, x2_done)

            run_steps(pool, step, FIRST, LOOP, STEPS, END)


def rows_of(a, b):
    if isinstance(b, int):
        return a[b].rearrange("(s p) n -> p s n", p=P)
    return a[bass.ds(b, 1)].rearrange("a (s p) n -> p (a s) n", p=P)


def one_of(a, b):
    if isinstance(b, int):
        return a[b]
    return a[bass.ds(b, 1)].rearrange("a p c n -> p (a c) n")


def constants():
    n = np.arange(D)
    angle = 2 * np.pi * np.outer(n, n) / D
    dft = np.concatenate([np.cos(angle[:, :P]), np.cos(angle[:, P:P + 1]), -np.sin(angle[:, 1:P])], axis=1)
    twice = np.where((n == 0) | (n == P), 1.0, 2.0)[:, None] / D
    idft = dft.T * twice
    tri = np.stack([np.triu(np.ones((P, P))), np.ones((P, P))], axis=1)
    picks = np.zeros((P, P))
    picks[list(PARTS_AT)] = 1.0
    return [a.astype(np.float32) for a in (dft, idft, tri, np.eye(P), picks)]


def kernel(**inputs):
    import concourse.bacc as bacc
    from concourse.bass_utils import run_bass_kernel_spmd

    a = {k: np.asarray(v) for k, v in inputs.items()}
    order = np.arange(D).reshape(HP, DC, DH).transpose(1, 2, 0).reshape(-1)
    dft, idft, tri, ident, picks = constants()
    picks = picks.astype(mybir.dt.np(BF16))

    def columns(v):
        return v.reshape(DC, P).T

    arrays = {
        "x": a["x"], "ctx": a["ctx_1024"].transpose(0, 2, 1).reshape(B, DC, P, S).transpose(0, 2, 1, 3),
        "attn_w": np.stack([a["L0_attn_Wk"], a["L0_attn_Wv"], a["L0_attn_Wq"]]),
        "attn_b": np.stack([columns(a[k]) for k in ("L0_attn_bk", "L0_attn_bv", "L0_attn_bq")], axis=1),
        "wq": a["L0_xattn_Wq"][:, order], "wk": a["L0_xattn_Wk"][:, order], "wv": a["L0_xattn_Wv"][order, :],
        "wo": a["L0_xattn_Wo"],
        "rows": np.stack([a[k] for k in ("L0_xattn_bv", "L0_xattn_bo", "L0_xattn_g0", "L0_xattn_b0", "L0_xattn_g1",
                                         "L0_xattn_b1")]),
        "columns": np.stack([columns(v) for v in (a["L0_xattn_g0"], a["L0_xattn_b0"], a["L0_ffn_mu_r"],
                                                  a["L0_ffn_mu_k"], a["L0_xattn_bq"][order],
                                                  a["L0_xattn_bk"][order])], axis=1),
        "wr_t": a["L0_ffn_W_r"].T, "wk_t": a["L0_ffn_W_k"].T, "wv_t": a["L0_ffn_W_v"].T,
        "dft": dft, "idft": idft, "tri": tri, "ident": ident, "picks": picks,
        "ones_rows": np.ones((3, R * H * S), mybir.dt.np(BF16)),
    }
    arrays = {"in_" + k: np.ascontiguousarray(v) for k, v in arrays.items()}
    nc = bacc.Bacc("TRN2", target_bir_lowering=False, num_devices=1)
    aps = {k[3:]: nc.dram_tensor(k, v.shape, mybir.dt.from_np(v.dtype), kind="ExternalInput").ap()
           for k, v in arrays.items()}
    out = nc.dram_tensor("out_rows", (B, S, D), F32, kind="ExternalOutput").ap()
    decoder_kernel(nc, *(aps[k] for k in ("x", "ctx", "attn_w", "attn_b", "wq", "wk", "wv", "wo", "rows", "columns",
                                          "wr_t", "wk_t", "wv_t", "dft", "idft", "tri",
                                          "ident", "picks", "ones_rows")), out)
    return run_bass_kernel_spmd(nc, [arrays], core_ids=[0]).results[0]["out_rows"]
```
